# Optimizing a Trainium2 kernel written in Bass

```python
import numpy as np
import jax
import jax.numpy as jnp

def _softmax(x, axis=-1):
    return jax.nn.softmax(x, axis=axis)

def _gelu(x):
    return jax.nn.gelu(x, approximate=True)

def _silu(x):
    return jax.nn.silu(x)

def _sigmoid(x):
    return jax.nn.sigmoid(x)

def _layernorm(x, axis=-1, eps=1e-05):
    m = jnp.mean(x, axis=axis, keepdims=True)
    v = jnp.var(x, axis=axis, keepdims=True)
    return (x - m) / jnp.sqrt(v + eps)

def _scatter_add(tgt, idx, src, axis=0):
    return tgt.at[idx].add(src)

def _segment_sum(src, seg, n):
    return jax.ops.segment_sum(src, seg, n)
kernel_name = 'mk_gps_d2_gnn_r32_de6654'

def setup_inputs(seed: int=0):
    np.random.seed(seed)
    _w = jnp.asarray

    def _rec_inputs():
        import jax
        import jax.numpy as jnp
        _gk = jax.random.key(seed)
        x = -0.0002117 + 1 * jax.random.normal(jax.random.fold_in(_gk, 1), (3125, 256), jnp.float32)
        _s = jax.random.randint(jax.random.fold_in(_gk, 2), (25000,), 0, 3125, jnp.int32)
        _d = jax.random.randint(jax.random.fold_in(_gk, 3), (25000,), 0, 3125, jnp.int32)
        _loop = jnp.arange(3125, dtype=jnp.int32)
        src = jnp.concatenate([_s, _d, _loop])
        dst = jnp.concatenate([_d, _s, _loop])
        _o = jnp.argsort(dst, stable=True)
        src = src[_o]
        dst = dst[_o]
        edge_weight = jax.random.uniform(jax.random.fold_in(_gk, 13), (53125,), jnp.float32, 0.0, 1)
        return (x, src, dst, edge_weight)
    x, src, dst, edge_weight = _rec_inputs()

    def _L0_gnn_setup():
        import jax, jax.numpy as jnp
        import numpy as np
        NW, NS, E = (3125, 10000, 25000)
        D, H, DH, DF = (256, 4, 64, 512)
        NEG_SLOPE = 0.2
        key = jax.random.key(seed)
        ks = jax.random.split(key, 14)
        s = 1.0 / np.sqrt(D)
        sh = 1.0 / np.sqrt(DF)
        return {'word_repr': jax.random.normal(ks[0], (NW, D), jnp.float32), 'sent_repr': jax.random.normal(ks[1], (NS, D), jnp.float32), 'src': jax.random.randint(ks[2], (E,), 0, NS, jnp.int32), 'dst': jax.random.randint(ks[3], (E,), 0, NW, jnp.int32), 'W_src': jax.random.normal(ks[4], (D, H * DH), jnp.float32) * s, 'W_dst': jax.random.normal(ks[5], (D, H * DH), jnp.float32) * s, 'attn_l': jax.random.normal(ks[6], (H, DH), jnp.float32) * s, 'attn_r': jax.random.normal(ks[7], (H, DH), jnp.float32) * s, 'gat_bias': jnp.zeros((H * DH,), jnp.float32), 'w1': jax.random.normal(ks[8], (D, DF), jnp.float32) * s, 'b1': jnp.zeros((DF,), jnp.float32), 'w2': jax.random.normal(ks[9], (DF, D), jnp.float32) * sh, 'b2': jnp.zeros((D,), jnp.float32)}
    _L0_gnn_all = _L0_gnn_setup()
    _L0_gnn_in = {k: v for k, v in _L0_gnn_all.items() if k in ('sent_repr', 'W_src', 'W_dst', 'attn_l', 'attn_r', 'gat_bias', 'w1', 'b1', 'w2', 'b2')}
    del _L0_gnn_all

    def _L0_mix_setup():
        import jax, jax.numpy as jnp
        import numpy as np
        HEADS = 4
        DIM_HEAD = 32
        key = jax.random.key(seed)
        k1, k2, k3 = jax.random.split(key, 3)
        B, L, D = (16, 256, 256)
        hidden = HEADS * DIM_HEAD
        x = jax.random.normal(k1, (B, L, D), dtype=jnp.float32)
        W_qkv = jax.random.normal(k2, (D, 3 * hidden), dtype=jnp.float32) * D ** (-0.5)
        W_out = jax.random.normal(k3, (hidden, D), dtype=jnp.float32) * hidden ** (-0.5)
        b_out = jnp.zeros((D,), dtype=jnp.float32)
        return {'x': x, 'W_qkv': W_qkv, 'W_out': W_out, 'b_out': b_out}
    _L0_mix_all = _L0_mix_setup()
    _L0_mix_in = {k: v for k, v in _L0_mix_all.items() if k in ('W_qkv', 'W_out', 'b_out')}
    del _L0_mix_all

    def _L0_ffn_setup():
        import math
        import jax, jax.numpy as jnp
        import numpy as np
        CAPACITY_FACTOR = 1.25
        TOP_K = 2
        LN_EPS = 1e-05

        def _layer_norm(x, gamma, beta):
            mu = jnp.mean(x, axis=-1, keepdims=True)
            var = jnp.var(x, axis=-1, keepdims=True)
            return (x - mu) * jax.lax.rsqrt(var + LN_EPS) * gamma + beta
        key = jax.random.key(seed)
        ks = jax.random.split(key, 4)
        B, S, D, F, E = (8, 128, 256, 512, 8)
        x = jax.random.normal(ks[0], (B, S, D), dtype=jnp.float32)
        Wr = jax.random.normal(ks[1], (D, E), dtype=jnp.float32) / np.sqrt(D)
        br = jnp.zeros((E,), jnp.float32)
        W1 = jax.random.normal(ks[2], (E, D, F), dtype=jnp.float32) / np.sqrt(D)
        b1 = jnp.zeros((E, F), jnp.float32)
        W2 = jax.random.normal(ks[3], (E, F, D), dtype=jnp.float32) / np.sqrt(F)
        b2 = jnp.zeros((E, D), jnp.float32)
        gamma = jnp.ones((D,), jnp.float32)
        beta = jnp.zeros((D,), jnp.float32)
        return {'x': x, 'Wr': Wr, 'br': br, 'W1': W1, 'b1': b1, 'W2': W2, 'b2': b2, 'gamma': gamma, 'beta': beta}
    _L0_ffn_all = _L0_ffn_setup()
    _L0_ffn_in = {k: v for k, v in _L0_ffn_all.items() if k in ('Wr', 'br', 'W1', 'b1', 'W2', 'b2', 'gamma', 'beta')}
    del _L0_ffn_all

    def _L1_gnn_setup():
        import jax, jax.numpy as jnp
        import numpy as np
        N_NODES = 3125
        key = jax.random.key(seed)
        k1, k2, k3, k4 = jax.random.split(key, 4)
        inp = jax.random.normal(k1, (3125, 256), dtype=jnp.float32)
        edge_index = jax.random.randint(k2, (2, 100000), 0, N_NODES, dtype=jnp.int64)
        edge_weight = jax.random.uniform(k3, (100000,), dtype=jnp.float32)
        fan_in, fan_out = (256, 256)
        limit = float(np.sqrt(6.0 / (fan_in + fan_out)))
        weight = jax.random.uniform(k4, (256, 256), dtype=jnp.float32, minval=-limit, maxval=limit)
        return {'input': inp, 'edge_index': edge_index, 'edge_weight': edge_weight, 'weight': weight}
    _L1_gnn_all = _L1_gnn_setup()
    _L1_gnn_in = {k: v for k, v in _L1_gnn_all.items() if k in ('weight',)}
    del _L1_gnn_all

    def _L1_mix_setup():
        import jax, jax.numpy as jnp
        import numpy as np
        B, N, C = (8, 256, 256)
        H, D, S = (8, 32, 32)
        HID = 4 * C

        def layernorm(x, w, b, eps=1e-05):
            mu = jnp.mean(x, axis=-1, keepdims=True)
            var = jnp.mean(jnp.square(x - mu), axis=-1, keepdims=True)
            return (x - mu) * jax.lax.rsqrt(var + eps) * w + b

        def linear_no_attn(x, Wx, bx, Wq, Wk, Wv, Wo, bo):
            x_mid = x @ Wx.T + bx
            x_mid = x_mid.reshape(x.shape[0], x.shape[1], H, D).transpose(0, 2, 1, 3)
            q = jax.nn.softmax(x_mid @ Wq.T, axis=-1)
            k = jax.nn.softmax(x_mid @ Wk.T, axis=-2)
            v = x_mid @ Wv.T
            kv = jnp.einsum('bhns,bhnd->bhsd', k, v)
            qkv = jnp.einsum('bhns,bhsd->bhnd', q, kv)
            qkv = qkv.transpose(0, 2, 1, 3).reshape(x.shape[0], x.shape[1], H * D)
            return qkv @ Wo.T + bo
        key = jax.random.key(seed)
        ks = jax.random.split(key, 16)
        s = lambda fan: 1.0 / np.sqrt(fan)
        return {'fx': jax.random.normal(ks[0], (B, N, C), jnp.float32), 'ln1_w': jnp.ones((C,), jnp.float32), 'ln1_b': jnp.zeros((C,), jnp.float32), 'Wx': jax.random.uniform(ks[1], (C, C), jnp.float32, -s(C), s(C)), 'bx': jax.random.uniform(ks[2], (C,), jnp.float32, -s(C), s(C)), 'Wq': jax.random.uniform(ks[3], (S, D), jnp.float32, -s(D), s(D)), 'Wk': jax.random.uniform(ks[4], (S, D), jnp.float32, -s(D), s(D)), 'Wv': jax.random.uniform(ks[5], (D, D), jnp.float32, -s(D), s(D)), 'Wo': jax.random.uniform(ks[6], (C, C), jnp.float32, -s(C), s(C)), 'bo': jax.random.uniform(ks[7], (C,), jnp.float32, -s(C), s(C)), 'ln2_w': jnp.ones((C,), jnp.float32), 'ln2_b': jnp.zeros((C,), jnp.float32), 'W1': jax.random.uniform(ks[8], (HID, C), jnp.float32, -s(C), s(C)), 'b1': jax.random.uniform(ks[9], (HID,), jnp.float32, -s(C), s(C)), 'W2': jax.random.uniform(ks[10], (C, HID), jnp.float32, -s(HID), s(HID)), 'b2': jax.random.uniform(ks[11], (C,), jnp.float32, -s(HID), s(HID))}
    _L1_mix_all = _L1_mix_setup()
    _L1_mix_in = {k: v for k, v in _L1_mix_all.items() if k in ('ln1_w', 'ln1_b', 'Wx', 'bx', 'Wq', 'Wk', 'Wv', 'Wo', 'bo', 'ln2_w', 'ln2_b', 'W1', 'b1', 'W2', 'b2')}
    del _L1_mix_all

    def _L1_ffn_setup():
        import jax, jax.numpy as jnp
        import numpy as np
        NUM_EXPERTS = 8
        TOP_K = 2
        B, S, D = (8, 256, 256)

        def _moe(tokens, router_w, w1, b1, w2, b2):
            N = tokens.shape[0]
            E = router_w.shape[0]
            logits = tokens.astype(jnp.float32) @ router_w.astype(jnp.float32).T
            probs = jax.nn.softmax(logits, axis=-1)
            rw, re = jax.lax.top_k(probs, TOP_K)
            if TOP_K > 1:
                rw = rw / jnp.maximum(rw.sum(-1, keepdims=True), 1e-12)
            rw = rw.astype(tokens.dtype)
            combine = jnp.zeros((N, E), tokens.dtype).at[jnp.arange(N)[:, None], re].set(rw)
            out = tokens
            for e in range(E):
                h = jax.nn.gelu(tokens @ w1[e] + b1[e], approximate=False)
                y = h @ w2[e] + b2[e]
                out = out + combine[:, e:e + 1] * y
            return out
        key = jax.random.key(seed)
        ks = jax.random.split(key, 4)
        scale = 1.0 / np.sqrt(D).astype(np.float32)
        return {'input_embeddings': jax.random.normal(ks[0], (B, S, D), jnp.float32), 'router_w': jax.random.normal(ks[1], (NUM_EXPERTS, D), jnp.float32) * scale, 'w1': jax.random.normal(ks[2], (NUM_EXPERTS, D, D), jnp.float32) * scale, 'b1': jnp.zeros((NUM_EXPERTS, D), jnp.float32), 'w2': jax.random.normal(ks[3], (NUM_EXPERTS, D, D), jnp.float32) * scale, 'b2': jnp.zeros((NUM_EXPERTS, D), jnp.float32)}
    _L1_ffn_all = _L1_ffn_setup()
    _L1_ffn_in = {k: v for k, v in _L1_ffn_all.items() if k in ('router_w', 'w1', 'b1', 'w2', 'b2')}
    del _L1_ffn_all
    return {'x': x, 'src': src, 'dst': dst, 'edge_weight': edge_weight, 'L0_gnn_sent_repr': _L0_gnn_in['sent_repr'], 'L0_gnn_W_src': _L0_gnn_in['W_src'], 'L0_gnn_W_dst': _L0_gnn_in['W_dst'], 'L0_gnn_attn_l': _L0_gnn_in['attn_l'], 'L0_gnn_attn_r': _L0_gnn_in['attn_r'], 'L0_gnn_gat_bias': _L0_gnn_in['gat_bias'], 'L0_gnn_w1': _L0_gnn_in['w1'], 'L0_gnn_b1': _L0_gnn_in['b1'], 'L0_gnn_w2': _L0_gnn_in['w2'], 'L0_gnn_b2': _L0_gnn_in['b2'], 'L0_mix_W_qkv': _L0_mix_in['W_qkv'], 'L0_mix_W_out': _L0_mix_in['W_out'], 'L0_mix_b_out': _L0_mix_in['b_out'], 'L0_ffn_Wr': _L0_ffn_in['Wr'], 'L0_ffn_br': _L0_ffn_in['br'], 'L0_ffn_W1': _L0_ffn_in['W1'], 'L0_ffn_b1': _L0_ffn_in['b1'], 'L0_ffn_W2': _L0_ffn_in['W2'], 'L0_ffn_b2': _L0_ffn_in['b2'], 'L0_ffn_gamma': _L0_ffn_in['gamma'], 'L0_ffn_beta': _L0_ffn_in['beta'], 'L1_gnn_weight': _L1_gnn_in['weight'], 'L1_mix_ln1_w': _L1_mix_in['ln1_w'], 'L1_mix_ln1_b': _L1_mix_in['ln1_b'], 'L1_mix_Wx': _L1_mix_in['Wx'], 'L1_mix_bx': _L1_mix_in['bx'], 'L1_mix_Wq': _L1_mix_in['Wq'], 'L1_mix_Wk': _L1_mix_in['Wk'], 'L1_mix_Wv': _L1_mix_in['Wv'], 'L1_mix_Wo': _L1_mix_in['Wo'], 'L1_mix_bo': _L1_mix_in['bo'], 'L1_mix_ln2_w': _L1_mix_in['ln2_w'], 'L1_mix_ln2_b': _L1_mix_in['ln2_b'], 'L1_mix_W1': _L1_mix_in['W1'], 'L1_mix_b1': _L1_mix_in['b1'], 'L1_mix_W2': _L1_mix_in['W2'], 'L1_mix_b2': _L1_mix_in['b2'], 'L1_ffn_router_w': _L1_ffn_in['router_w'], 'L1_ffn_w1': _L1_ffn_in['w1'], 'L1_ffn_b1': _L1_ffn_in['b1'], 'L1_ffn_w2': _L1_ffn_in['w2'], 'L1_ffn_b2': _L1_ffn_in['b2']}

def reference(x, src, dst, edge_weight, L0_gnn_sent_repr, L0_gnn_W_src, L0_gnn_W_dst, L0_gnn_attn_l, L0_gnn_attn_r, L0_gnn_gat_bias, L0_gnn_w1, L0_gnn_b1, L0_gnn_w2, L0_gnn_b2, L0_mix_W_qkv, L0_mix_W_out, L0_mix_b_out, L0_ffn_Wr, L0_ffn_br, L0_ffn_W1, L0_ffn_b1, L0_ffn_W2, L0_ffn_b2, L0_ffn_gamma, L0_ffn_beta, L1_gnn_weight, L1_mix_ln1_w, L1_mix_ln1_b, L1_mix_Wx, L1_mix_bx, L1_mix_Wq, L1_mix_Wk, L1_mix_Wv, L1_mix_Wo, L1_mix_bo, L1_mix_ln2_w, L1_mix_ln2_b, L1_mix_W1, L1_mix_b1, L1_mix_W2, L1_mix_b2, L1_ffn_router_w, L1_ffn_w1, L1_ffn_b1, L1_ffn_w2, L1_ffn_b2):
    import jax
    import jax.numpy as jnp

    def _L0_gnn_ref(word_repr, sent_repr, src, dst, W_src, W_dst, attn_l, attn_r, gat_bias, w1, b1, w2, b2):
        import jax, jax.numpy as jnp
        import numpy as np
        NW, NS, E = (3125, 10000, 25000)
        D, H, DH, DF = (256, 4, 64, 512)
        NEG_SLOPE = 0.2
        feat_src = (sent_repr @ W_src).reshape(NS, H, DH)
        feat_dst = (word_repr @ W_dst).reshape(NW, H, DH)
        el = jnp.sum(feat_src * attn_l, axis=-1)
        er = jnp.sum(feat_dst * attn_r, axis=-1)
        e = jax.nn.leaky_relu(el[src] + er[dst], NEG_SLOPE)
        emax = jax.ops.segment_max(e, dst, num_segments=NW)
        ex = jnp.exp(e - emax[dst])
        den = jax.ops.segment_sum(ex, dst, num_segments=NW)
        alpha = ex / den[dst]
        msg = feat_src[src] * alpha[:, :, None]
        rst = jax.ops.segment_sum(msg, dst, num_segments=NW)
        rst = rst + gat_bias.reshape(1, H, DH)
        update = jax.nn.elu(rst.reshape(NW, H * DH))
        h = word_repr + update
        out = jax.nn.relu(h @ w1 + b1) @ w2 + b2
        return out

    def _L0_mix_ref(x, W_qkv, W_out, b_out):
        import jax, jax.numpy as jnp
        import numpy as np
        HEADS = 4
        DIM_HEAD = 32
        B, L, D = x.shape
        scale = DIM_HEAD ** (-0.5)
        qkv = jnp.einsum('bld,df->blf', x, W_qkv)
        qkv = qkv.reshape(B, L, 3, HEADS, DIM_HEAD)
        q = jnp.transpose(qkv[:, :, 0], (0, 2, 1, 3)) * scale
        k = jax.nn.softmax(jnp.transpose(qkv[:, :, 1], (0, 2, 1, 3)), axis=2)
        v = jnp.transpose(qkv[:, :, 2], (0, 2, 1, 3))
        context = jnp.einsum('bhld,bhle->bhde', k, v)
        out = jnp.einsum('bhde,bhld->bhle', context, q)
        out = jnp.transpose(out, (0, 2, 1, 3)).reshape(B, L, HEADS * DIM_HEAD)
        return jnp.einsum('blf,fd->bld', out, W_out) + b_out

    def _L0_ffn_ref(x, Wr, br, W1, b1, W2, b2, gamma, beta):
        import math
        import jax, jax.numpy as jnp
        import numpy as np
        CAPACITY_FACTOR = 1.25
        TOP_K = 2
        LN_EPS = 1e-05

        def _layer_norm(x, gamma, beta):
            mu = jnp.mean(x, axis=-1, keepdims=True)
            var = jnp.var(x, axis=-1, keepdims=True)
            return (x - mu) * jax.lax.rsqrt(var + LN_EPS) * gamma + beta
        B, S, D = x.shape
        E = Wr.shape[1]
        N = B * S
        K = TOP_K
        logits = jnp.mean(x, axis=1) @ Wr + br
        routing_weights = jax.nn.softmax(logits, axis=-1)
        capacity = float(math.ceil(N * CAPACITY_FACTOR / E))
        expected_loads = routing_weights.sum(axis=0) * (N / B)
        scale = jnp.where(expected_loads > capacity, capacity / expected_loads, 1.0)
        routing_weights = jax.nn.softmax(routing_weights * scale, axis=-1)
        rw_tok = jnp.broadcast_to(routing_weights[:, None, :], (B, S, E)).reshape(N, E)
        top_w, top_i = jax.lax.top_k(rw_tok, K)
        top_w = jax.nn.softmax(top_w, axis=-1)
        xf = x.reshape(N, D)
        h = jax.nn.gelu(jnp.einsum('nd,edf->enf', xf, W1) + b1[:, None, :], approximate=False)
        y = jnp.einsum('enf,efd->end', h, W2) + b2[:, None, :]
        w_dense = jnp.zeros((N, E), x.dtype).at[jnp.arange(N)[:, None], top_i].add(top_w)
        out = jnp.einsum('ne,end->nd', w_dense, y).reshape(B, S, D)
        out = _layer_norm(out + x, gamma, beta)
        return out

    def _L1_gnn_ref(input, edge_index, edge_weight, weight):
        import jax, jax.numpy as jnp
        import numpy as np
        N_NODES = 3125
        support = input @ weight
        src, dst = (edge_index[0], edge_index[1])
        msgs = support[src] * edge_weight[:, None]
        agg = jax.ops.segment_sum(msgs, dst, num_segments=N_NODES)
        return jax.nn.relu(agg)

    def _L1_mix_ref(fx, ln1_w, ln1_b, Wx, bx, Wq, Wk, Wv, Wo, bo, ln2_w, ln2_b, W1, b1, W2, b2):
        import jax, jax.numpy as jnp
        import numpy as np
        B, N, C = (8, 256, 256)
        H, D, S = (8, 32, 32)
        HID = 4 * C

        def layernorm(x, w, b, eps=1e-05):
            mu = jnp.mean(x, axis=-1, keepdims=True)
            var = jnp.mean(jnp.square(x - mu), axis=-1, keepdims=True)
            return (x - mu) * jax.lax.rsqrt(var + eps) * w + b

        def linear_no_attn(x, Wx, bx, Wq, Wk, Wv, Wo, bo):
            x_mid = x @ Wx.T + bx
            x_mid = x_mid.reshape(x.shape[0], x.shape[1], H, D).transpose(0, 2, 1, 3)
            q = jax.nn.softmax(x_mid @ Wq.T, axis=-1)
            k = jax.nn.softmax(x_mid @ Wk.T, axis=-2)
            v = x_mid @ Wv.T
            kv = jnp.einsum('bhns,bhnd->bhsd', k, v)
            qkv = jnp.einsum('bhns,bhsd->bhnd', q, kv)
            qkv = qkv.transpose(0, 2, 1, 3).reshape(x.shape[0], x.shape[1], H * D)
            return qkv @ Wo.T + bo
        h = linear_no_attn(layernorm(fx, ln1_w, ln1_b), Wx, bx, Wq, Wk, Wv, Wo, bo) + fx
        y = layernorm(h, ln2_w, ln2_b)
        y = jax.nn.gelu(y @ W1.T + b1, approximate=False)
        y = y @ W2.T + b2
        return y + h

    def _L1_ffn_ref(input_embeddings, router_w, w1, b1, w2, b2):
        import jax, jax.numpy as jnp
        import numpy as np
        NUM_EXPERTS = 8
        TOP_K = 2
        B, S, D = (8, 256, 256)

        def _moe(tokens, router_w, w1, b1, w2, b2):
            N = tokens.shape[0]
            E = router_w.shape[0]
            logits = tokens.astype(jnp.float32) @ router_w.astype(jnp.float32).T
            probs = jax.nn.softmax(logits, axis=-1)
            rw, re = jax.lax.top_k(probs, TOP_K)
            if TOP_K > 1:
                rw = rw / jnp.maximum(rw.sum(-1, keepdims=True), 1e-12)
            rw = rw.astype(tokens.dtype)
            combine = jnp.zeros((N, E), tokens.dtype).at[jnp.arange(N)[:, None], re].set(rw)
            out = tokens
            for e in range(E):
                h = jax.nn.gelu(tokens @ w1[e] + b1[e], approximate=False)
                y = h @ w2[e] + b2[e]
                out = out + combine[:, e:e + 1] * y
            return out
        b, s, d = input_embeddings.shape
        tokens = input_embeddings.reshape(b * s, d)
        return _moe(tokens, router_w, w1, b1, w2, b2).reshape(b, s, d)
    edge_index = jnp.stack([src, dst])
    xn = _layernorm(x, axis=-1)
    x = x + _L0_gnn_ref(xn, L0_gnn_sent_repr, src, dst, L0_gnn_W_src, L0_gnn_W_dst, L0_gnn_attn_l, L0_gnn_attn_r, L0_gnn_gat_bias, L0_gnn_w1, L0_gnn_b1, L0_gnn_w2, L0_gnn_b2) + _L0_mix_ref(xn[None], L0_mix_W_qkv, L0_mix_W_out, L0_mix_b_out)[0]
    x = x + _L0_ffn_ref(_layernorm(x, axis=-1)[None], L0_ffn_Wr, L0_ffn_br, L0_ffn_W1, L0_ffn_b1, L0_ffn_W2, L0_ffn_b2, L0_ffn_gamma, L0_ffn_beta)[0]
    xn = _layernorm(x, axis=-1)
    x = x + _L1_gnn_ref(xn, edge_index, edge_weight, L1_gnn_weight) + _L1_mix_ref(xn[None], L1_mix_ln1_w, L1_mix_ln1_b, L1_mix_Wx, L1_mix_bx, L1_mix_Wq, L1_mix_Wk, L1_mix_Wv, L1_mix_Wo, L1_mix_bo, L1_mix_ln2_w, L1_mix_ln2_b, L1_mix_W1, L1_mix_b1, L1_mix_W2, L1_mix_b2)[0]
    x = x + _L1_ffn_ref(_layernorm(x, axis=-1)[None], L1_ffn_router_w, L1_ffn_w1, L1_ffn_b1, L1_ffn_w2, L1_ffn_b2)[0]
    return x

_drawn_inputs = setup_inputs


def setup_inputs(seed=0):
    import zlib

    import numpy as np

    out = dict(_drawn_inputs(seed))
    spreads = {'L0_gnn_gat_bias': (0.0, 0.1),
     'L0_gnn_b1': (0.0, 0.1),
     'L0_gnn_b2': (0.0, 0.1),
     'L0_mix_b_out': (0.0, 0.1),
     'L0_ffn_br': (0.0, 0.1),
     'L0_ffn_b1': (0.0, 0.1),
     'L0_ffn_b2': (0.0, 0.1),
     'L0_ffn_gamma': (1.0, 0.2),
     'L0_ffn_beta': (0.0, 0.1),
     'L1_mix_ln1_w': (1.0, 0.6),
     'L1_mix_ln1_b': (0.0, 0.8),
     'L1_mix_ln2_w': (1.0, 0.6),
     'L1_mix_ln2_b': (0.0, 0.8),
     'L1_ffn_b1': (0.0, 0.8),
     'L1_ffn_b2': (0.0, 0.573)}
    factors = {'L0_gnn_W_dst': 3.126,
     'L0_gnn_attn_r': 3.08,
     'L1_mix_Wx': 2.968,
     'L1_mix_bx': 8.0,
     'L1_mix_Wq': 8.0,
     'L1_mix_Wk': 8.0,
     'L1_mix_bo': 5.647,
     'L1_mix_b1': 8.0,
     'L1_mix_b2': 8.0}
    for name, (base, spread) in spreads.items():
        noise = np.random.default_rng([zlib.crc32(name.encode()), seed]).standard_normal(out[name].shape)
        drawn = base * np.exp(spread * noise) if base else spread * noise
        out[name] = jnp.asarray(drawn.astype(out[name].dtype))
    for name, factor in factors.items():
        out[name] = (out[name] * factor).astype(out[name].dtype)
    return out
```

```python
from contextlib import ExitStack

import numpy as np
import concourse.bass as bass
from concourse import mybir

ALU = mybir.AluOpType
ACT = mybir.ActivationFunctionType
AX = mybir.AxisListType.X
F32 = mybir.dt.float32
BF16 = mybir.dt.bfloat16
I32 = mybir.dt.int32
U32 = mybir.dt.uint32

P = 128
N_NODES = 3125
D = 256
KT = D // P
T = -(-N_NODES // P)
NP = T * P
R = 5
NI = T // R
N_EDGES = 53125
NC = -(-N_EDGES // P)
NS = NC + T - 1
RB = 110
SB = NS // RB
G = 8
H = 4
DH = D // H
DF = 512
HID = 1024
E = 8
PAD_DST = 4095
BIG = 1.0e30
EPS = 1.0e-5
assert T % R == 0 and NS == RB * SB and NS % G == 0

C_ID, C_BD, C_IOTA = 0, 128, 256
C_P, C_STEP, C_TILE, C_CHUNK, C_ONE, C_EXP = 384, 385, 389, 414, 414 + NC, 414 + NC + P
C_ZERO = C_EXP + 8
C_POW = C_ZERO + P
C_N = C_POW + 1


class Stage(ExitStack):

    def __init__(self, nc):
        super().__init__()
        self.nc, self.semaphores = nc, []

    def semaphore(self, name):
        self.semaphores.append(self.nc.alloc_semaphore(name))
        return self.semaphores[-1]

    def __exit__(self, *failure):
        super().__exit__(*failure)
        self.nc.clear_and_free_semaphores(self.semaphores)
        self.nc.all_engine_barrier()


class Steps:

    def __init__(self, eng, sem, i=None, per=0, base=0):
        self.eng, self.sem, self.i, self.per, self.base, self.k = eng, sem, i, per, base, 0

    def at(self):
        k = self.base + self.k
        return k if self.i is None else self.i * self.per + k

    def __call__(self, ins):
        self.k += 1
        ins.then_inc(self.sem, 1)
        self.eng.wait_ge(self.sem, self.at())

    def end(self):
        assert self.i is None or self.per == self.k, self.k


def pipeline(eng, stages, turns=NI, width=R):
    longest = max(lag for lag, _ in stages)
    assert longest <= width
    first = 2 if longest else 1
    for n in range(first * width):
        for lag, stage in stages:
            if n >= lag:
                stage((n - lag) // width, (n - lag) % width)
    with eng.Fori(first, turns) as i:
        for j in range(width):
            for lag, stage in stages:
                if j >= lag:
                    stage(i, j - lag)
                else:
                    stage(i - 1, j - lag + width)
    for j in range(longest):
        for lag, stage in stages:
            if j < lag:
                stage(turns - 1, j - lag + width)


def once(eng, sem, n, hold=None):
    if isinstance(n, int) and n <= 0:
        return
    if hold is None:
        eng.wait_ge(sem, n)
    else:
        hold(eng, sem, n)


def bank_gap(j, n=2):
    return n if j >= n else R - (R - 1 - j) // n * n


class Norm:

    def __init__(self, nc, ctx, name, hold, power):
        self.power = power
        self.stats = ctx.enter_context(nc.sbuf_tensor(f"{name}_stats", [P, 6], F32))
        self.mv = ctx.enter_context(nc.sbuf_tensor(f"{name}_mv", [P, 2], F32))
        self.rstd = ctx.enter_context(nc.sbuf_tensor(f"{name}_rstd", [P, 1], F32))
        self.found = ctx.semaphore(f"{name}_found")
        self.rooted = ctx.semaphore(f"{name}_rooted")
        self.step = ctx.semaphore(f"{name}_step")
        self.hold = hold

    def find(self, dve, x, n):
        dve.bn_stats(self.stats[:, :], x).then_inc(self.step, 1)
        self.hold(dve, self.step, n * 2 + 1)
        dve.bn_aggr(self.mv[:, :], self.stats[:, :]).then_inc(self.step, 1)
        dve.wait_ge(self.step, n * 2 + 2)
        dve.tensor_scalar(self.mv[:, 1:2], self.mv[:, 1:2], EPS, None, ALU.add).then_inc(self.found, 1)
        dve.wait_ge(self.rooted, n + 1)

    def root(self, pool, n):
        self.hold(pool, self.found, n + 1)
        pool.tensor_tensor(self.rstd[:, :], self.mv[:, 1:2], self.power, ALU.pow).then_inc(self.rooted, 1)

    def apply(self, dve, out, x):
        return dve.tensor_scalar(out, x, self.mv[:, 0:1], self.rstd[:, 0:1], ALU.subtract, ALU.mult)


def program(nc, A, out):
    with ExitStack() as top:
        def sb(name, shape, dt=F32, ctx=top):
            return ctx.enter_context(nc.sbuf_tensor(name, shape, dt))

        def dram(name, shape, dt=F32):
            return nc.dram_tensor(name, shape, dt, kind="Internal").ap()

        passed = top.enter_context(nc.semaphore("passed"))

        def hold(eng, sem, value):
            eng.wait_ge(sem, value)
            eng.sem_inc(passed, 1)

        bank = [top.enter_context(nc.psum_tensor(f"bank{i}", [P, 512], F32)) for i in range(8)]

        const = sb("const", [P, C_N])
        ident = const[:, C_ID:C_ID + P]
        blocks32 = const[:, C_BD:C_BD + P]
        iota = const[:, C_IOTA:C_IOTA + P]
        pidx = const[:, C_P:C_P + 1]

        step_tile = sb("step_tile", [1, NS], I32)
        src_lane = sb("src_lane", [P, NS], I32)
        dst_lane = sb("dst_lane", [P, NS])
        ew_lane = sb("ew_lane", [P, NS])
        hi_lane = sb("hi_lane", [P, NS])
        acc = sb("acc", [P, T, D + H])
        big_k = sb("big_k", [P, KT * NP])
        big_v = sb("big_v", [P, T, D])
        combine = sb("combine", [P, T, 8])

        src_lo_d = dram("src_lo_d", [NS, P], BF16)
        dst_lo_d = dram("dst_lo_d", [NS, P], BF16)
        feat_d = dram("feat_d", [NP, D])
        xn_d = dram("xn_d", [NP, D])
        xnT_d = dram("xnT_d", [T, P, D])
        x1_d = dram("x1_d", [NP, D])
        xn1_d = dram("xn1_d", [NP, D])
        x2_d = dram("x2_d", [NP, D])
        xn2_d = dram("xn2_d", [NP, D])
        qT_d = dram("qT_d", [T, P, D])
        mixed_d = dram("mixed_d", [NP, D])

        dst_rows = sb("dst_rows", [RB, SB, P])
        edge_schedule(nc, A, dst_rows, bank, const, step_tile, src_lane, dst_lane, ew_lane, hi_lane,
                      src_lo_d, dst_lo_d)
        scores = sb("scores", [P, 2, T, H])
        first_projections(nc, A, hold, bank, const, big_k, big_v, scores, feat_d, xn_d, xnT_d)
        fold = sb("fold", [P, KT, D])
        first_mixer(nc, A, hold, bank, const, big_k, big_v, fold)
        with ExitStack() as held:
            weight = sb("edge_exp", [P, NS, H], ctx=held)
            with ExitStack() as brief:
                el_er = sb("el_er", [P, 2, NS, H], ctx=brief)
                er = sb("er", [P, NS, H], ctx=brief)
                edge_lookup(nc, A, hold, bank, const, scores, el_er, er, hi_lane, step_tile, src_lo_d, dst_lo_d)
                segment_maximum(nc, bank, const, dst_rows, el_er)
                edge_exp(nc, el_er, er, weight)
            aggregate(nc, A, hold, "a0", bank, const, acc, step_tile, src_lane, dst_lane, feat_d, weight, None)
        with ExitStack() as held:
            xnT = sb("xn1T", [P, KT, NP], ctx=held)
            first_graph_mlp(nc, A, hold, bank, const, acc, fold, xnT, A["x"], xn_d, xnT_d, x1_d, xn1_d)
            w1 = sb("top_w1", [P, 2, KT, DF], ctx=held)
            w2 = sb("top_w2", [P, 2, DF // P, D], ctx=held)
            b1 = sb("top_b1", [P, 2, DF // P], ctx=held)
            bias = sb("top_bias", [P, D], ctx=held)
            first_router(nc, A, hold, bank, const, xnT, w1, w2, b1, bias)
            first_experts(nc, A, hold, bank, const, xnT, w1, w2, b1, bias, big_k, big_v,
                          x1_d, xn1_d, x2_d, xn2_d, qT_d)
        folded = sb("folded", [P, KT, D])
        second_mixer(nc, A, hold, bank, const, big_k, big_v, folded)
        mixer_mlp(nc, A, hold, bank, const, folded, x2_d, xn2_d, qT_d, mixed_d)
        aggregate(nc, A, hold, "a1", bank, const, acc, step_tile, src_lane, dst_lane, xn2_d, None, ew_lane)
        with ExitStack() as held:
            xnT = sb("xn3T", [P, KT, NP], ctx=held)
            second_graph(nc, A, hold, bank, const, acc, xnT, combine, mixed_d)
            second_experts(nc, A, hold, bank, const, acc, xnT, combine, big_k, big_v, out)


def edge_schedule(nc, A, rows, bank, const, step_tile, src_lane, dst_lane, ew_lane, hi_lane, src_lo_d, dst_lo_d):
    with Stage(nc) as ctx:
        def sb(name, shape, dt=F32):
            return ctx.enter_context(nc.sbuf_tensor(name, shape, dt))

        def sem(name):
            return ctx.semaphore(name)

        first = sb("es_first", [1, NC], I32)
        first_t = sb("es_first_t", [1, NC], I32)
        key = sb("es_key", [1, NC])
        below = sb("es_below", [RB, NC])
        count = sb("es_count", [RB, SB])
        chunk = sb("es_chunk", [RB, SB], I32)
        tile_f = sb("es_tile_f", [RB, SB])
        base = sb("es_base", [RB, SB])
        src_i = sb("es_src_i", [RB, SB, P], I32)
        dst_i = sb("es_dst_i", [RB, SB, P], I32)
        ew_r = sb("es_ew_r", [RB, SB, P])
        hi_i = sb("es_hi_i", [RB, SB, P], I32)
        lo_i = sb("es_lo_i", [RB, SB, P], I32)
        src_f = sb("es_src_f", [RB, SB, P])
        hi_f = sb("es_hi_f", [RB, SB, P])
        local = sb("es_local", [RB, SB, P])
        lo_b = sb("es_lo_b", [RB, SB, P], BF16)
        loc_b = sb("es_loc_b", [RB, SB, P], BF16)

        const_in, first_in = sem("es_const_in"), sem("es_first_in")
        dve_step, key_ready, key_spread = sem("es_dve_step"), sem("es_key_ready"), sem("es_key_spread")
        chunk_ready, tile_ready, tile_row = sem("es_chunk_ready"), sem("es_tile_ready"), sem("es_tile_row")
        rows_in = [sem(f"es_rows_in{k}") for k in range(3)]
        rows_ready, lanes_ready, stored, lo_ready = (sem("es_rows_ready"), sem("es_lanes_ready"),
                                                     sem("es_stored"), sem("es_lo_ready"))
        block = ctx.enter_context(nc.Block())

        @block.sync
        def _(sp):
            sp.dma_start(const[:, :], A["const"]).then_inc(const_in, 16)
            sp.dma_start(first[:, :], A["dst_first"]).then_inc(first_in, 16)
            sp.wait_ge(lo_ready, 1)
            sp.dma_start(src_lo_d.rearrange("(b p) l -> p b l", b=SB), lo_b[:, :, :]).then_inc(stored, 16)
            sp.dma_start(dst_lo_d.rearrange("(b p) l -> p b l", b=SB), loc_b[:, :, :]).then_inc(stored, 16)
            sp.wait_ge(stored, 32)

        @block.gpsimd
        def _(pool):
            pool.wait_ge(chunk_ready, 1)
            for b in range(SB):
                at = bass.IndirectOffsetOnAxis(ap=chunk[:, b:b + 1], axis=0)
                for k, (dst, src) in enumerate(((dst_i, A["dst"]), (src_i, A["src"]), (ew_r, A["ew"]))):
                    pool.indirect_dma_start(dst[:, b, :], None, src, at).then_inc(rows_in[k], 16)

        @block.vector
        def _(dve):
            link = Steps(dve, dve_step)
            dve.wait_ge(const_in, 16)
            dve.wait_ge(first_in, 16)
            link(dve.tensor_single_scalar(first_t[:, :], first[:, :], 7, ALU.arith_shift_right))
            link(dve.tensor_copy(key[:, :], first_t[:, :]))
            dve.tensor_tensor(key[:, :], key[:, :], const[0:1, C_CHUNK:C_CHUNK + NC], ALU.add).then_inc(key_ready, 1)
            dve.wait_ge(key_spread, 1)
            for b in range(SB):
                link(dve.tensor_scalar(below[:, 1:NC], bank[0][0:RB, 1:NC], const[0:RB, C_STEP + b:C_STEP + b + 1],
                                       None, ALU.is_le))
                link(dve.tensor_reduce(count[:, b:b + 1], below[:, 1:NC], AX, ALU.add))
            dve.tensor_copy(chunk[:, :], count[:, :]).then_inc(chunk_ready, 1)
            dve.tensor_tensor(tile_f[:, :], const[0:RB, C_STEP:C_STEP + SB], count[:, :], ALU.subtract)\
               .then_inc(tile_ready, 1)
            dve.wait_ge(tile_ready, 1)
            link(dve.tensor_scalar(base[:, :], tile_f[:, :], float(P), None, ALU.mult))
            dve.wait_ge(tile_row, 1)
            link(dve.tensor_copy(step_tile[:, :], bank[1][0:1, 0:NS]))
            dve.wait_ge(rows_in[0], 16 * SB)
            link(dve.tensor_copy(rows[:, :, :], dst_i[:, :, :]))
            link(dve.tensor_tensor(local[:, :, :], rows[:, :, :],
                                   base[:, :].unsqueeze(2).broadcast_to([RB, SB, P]), ALU.subtract))
            link(dve.tensor_copy(loc_b[:, :, :], local[:, :, :]))
            dve.wait_ge(rows_in[1], 16 * SB)
            link(dve.tensor_copy(src_f[:, :, :], src_i[:, :, :]))
            link(dve.tensor_single_scalar(hi_i[:, :, :], src_i[:, :, :], 7, ALU.arith_shift_right))
            link(dve.tensor_single_scalar(lo_i[:, :, :], src_i[:, :, :], P - 1, ALU.bitwise_and))
            dve.tensor_copy(lo_b[:, :, :], lo_i[:, :, :]).then_inc(lo_ready, 1)
            dve.tensor_copy(hi_f[:, :, :], hi_i[:, :, :]).then_inc(rows_ready, 1)
            dve.wait_ge(lanes_ready, 4)
            for b, dst in ((2, src_lane), (3, dst_lane), (4, ew_lane), (5, hi_lane)):
                link(dve.tensor_copy(dst[:, :], bank[b][:, 0:NS]))

        @block.tensor
        def _(pe):
            pe.wait_ge(const_in, 16)
            pe.wait_ge(key_ready, 1)
            pe.matmul(bank[0][:, 0:NC], const[0:1, C_ONE:C_ONE + P], key[:, :], start=True, stop=True)\
              .then_inc(key_spread, 1)
            pe.wait_ge(tile_ready, 1)
            for b in range(SB):
                last = pe.matmul(bank[1][0:1, b * RB:(b + 1) * RB], tile_f[:, b:b + 1], const[0:RB, C_ID:C_ID + RB],
                                 start=True, stop=True)
            last.then_inc(tile_row, 1)
            pe.wait_ge(rows_in[2], 16 * SB)
            pe.wait_ge(rows_ready, 1)
            for n, src in ((2, src_f), (3, local), (4, ew_r), (5, hi_f)):
                for b in range(SB):
                    last = pe.transpose(bank[n][:, b * RB:(b + 1) * RB], src[:, b, :], const[0:RB, C_ID:C_ID + RB])
                last.then_inc(lanes_ready, 1)


def first_projections(nc, A, hold, bank, const, big_k, big_v, scores, feat_d, xn_d, xnT_d):
    ident = const[:, C_ID:C_ID + P]
    HD = 128
    with Stage(nc) as ctx:
        def sb(name, shape, dt=F32):
            return ctx.enter_context(nc.sbuf_tensor(name, shape, dt))

        def sem(name):
            return ctx.semaphore(name)

        w_feat = sb("p1_w_feat", [P, KT, D + H])
        w_v = sb("p1_w_v", [P, KT, HD + H])
        w_k = sb("p1_w_k", [P, KT, HD])
        w_dst = sb("p1_w_dst", [P, KT, D])
        attn = sb("p1_attn", [P, 2, D])
        prod = sb("p1_prod", [P, KT, D])
        x_in = sb("p1_x_in", [P, R, D])
        sent_in = sb("p1_sent_in", [P, R, KT, P])
        xn = sb("p1_xn", [P, R, D])
        xnT = sb("p1_xnT", [P, R, D])
        feat = sb("p1_feat", [P, R, D])
        norm = Norm(nc, ctx, "p1_norm", hold, const[:, C_POW:C_POW + 1])
        turned_ps, feat_ps, v_ps, k_ps = ([bank[2 * n], bank[2 * n + 1]] for n in range(4))

        w_in, wd, w_ready = sem("p1_w_in"), sem("p1_wd"), sem("p1_w_ready")
        x_loaded = [sem(f"p1_x_loaded{j}") for j in range(R)]
        sent_loaded = [sem(f"p1_sent_loaded{j}") for j in range(R)]
        xn_stored = [sem(f"p1_xn_stored{j}") for j in range(R)]
        xnT_stored = [sem(f"p1_xnT_stored{j}") for j in range(R)]
        feat_stored = [sem(f"p1_feat_stored{j}") for j in range(R)]
        xn_ready = sem("p1_xn_ready")
        turned, turned_sb = sem("p1_turned"), sem("p1_turned_sb")
        feat_done, feat_sb = sem("p1_feat_done"), sem("p1_feat_sb")
        el_sb = sem("p1_el_sb")
        v_done, k_done = sem("p1_v_done"), sem("p1_k_done")
        v_sb, k_sb = sem("p1_v_sb"), sem("p1_k_sb")
        block = ctx.enter_context(nc.Block())

        def before(j):
            return 1 if j == 0 else 2

        @block.sync
        def _(sp):
            sp.dma_start(w_feat[:, :, 0:D], A["L0_gnn_W_src"].rearrange("(k p) n -> p k n", p=P)).then_inc(w_in, 16)
            sp.dma_start(w_dst[:, :, :], A["L0_gnn_W_dst"].rearrange("(k p) n -> p k n", p=P)).then_inc(w_in, 16)
            sp.dma_start(w_k[:, :, :], A["L0_mix_W_k"].rearrange("(k p) n -> p k n", p=P)).then_inc(w_in, 16)
            sp.dma_start(w_v[:, :, 0:HD], A["L0_mix_W_v"].rearrange("(k p) n -> p k n", p=P)).then_inc(w_in, 16)
            sp.dma_start(attn[:, 0, :], A["L0_gnn_attn_l"].broadcast_to([P, D])).then_inc(w_in, 16)
            sp.dma_start(attn[:, 1, :], A["L0_gnn_attn_r"].broadcast_to([P, D])).then_inc(w_in, 16)
            with sp.Fori(0, NI) as i:
                for j in range(R):
                    g = i * R + j
                    hold(sp, xn_ready, g + 1)
                    sp.dma_start(x_in[:, j, :], A["x"][bass.ds(g * P, P), :]).then_inc(x_loaded[j], 16)
                    hold(sp, feat_done, g + 1)
                    sp.dma_start(sent_in[:, j, :, :],
                                 A["sentT"][:, bass.ds(g * P, P)].rearrange("(k p) n -> p k n", p=P))\
                      .then_inc(sent_loaded[j], 16)
            for j in range(R):
                sp.wait_ge(xn_stored[j], 16 * NI)
                sp.wait_ge(xnT_stored[j], 16 * NI)
                sp.wait_ge(feat_stored[j], 16 * NI)

        @block.gpsimd
        def _(pool):
            with pool.Fori(0, NI) as i:
                for j in range(R):
                    g = i * R + j
                    norm.root(pool, g)
                    hold(pool, xn_ready, R + g + 1)
                    pool.dma_start(xn_d[bass.ds(g * P, P), :], xn[:, j, :]).then_inc(xn_stored[j], 16)

        @block.scalar
        def _(act):
            act.sem_inc(turned_sb, 2)
            act.sem_inc(feat_sb, 2)
            act.sem_inc(k_sb, 2)
            with act.Fori(0, NI) as i:
                for j in range(R):
                    g = i * R + j
                    act.wait_ge(turned, g + 1)
                    act.wait_ge(k_done, g + 1)
                    act.wait_ge(xnT_stored[j], i * 16)
                    act.activation(xnT[:, j, :], turned_ps[j % 2][:, 0:D], ACT.Copy).then_inc(turned_sb, 1)
                    act.wait_ge(feat_done, R + g + 1)
                    act.wait_ge(feat_stored[j], i * 16)
                    act.activation(feat[:, j, :], feat_ps[j % 2][:, 0:D], ACT.Copy).then_inc(el_sb, 1)
                    act.activation(scores[:, 0, bass.ds(g, 1), :].rearrange("p a h -> p (a h)"),
                                   feat_ps[j % 2][:, D:D + H], ACT.Copy).then_inc(feat_sb, 1)
                    act.wait_ge(turned_sb, 2 + g + 1)
                    act.dma_start(xnT_d[bass.ds(g, 1), :, :].rearrange("a p n -> p (a n)"), xnT[:, j, :])\
                       .then_inc(xnT_stored[j], 16)
                    act.wait_ge(el_sb, g + 1)
                    act.dma_start(feat_d[bass.ds(g * P, P), :], feat[:, j, :]).then_inc(feat_stored[j], 16)
                    act.wait_ge(k_done, R + g + 1)
                    act.activation(big_k[:, bass.ds(g * P, P)], k_ps[j % 2][:, 0:P], ACT.Copy).then_inc(k_sb, 1)

        @block.vector
        def _(dve):
            dve.sem_inc(xn_ready, R)
            dve.sem_inc(v_sb, 2)
            link = Steps(dve, wd)
            dve.wait_ge(w_in, 96)
            for w, side in ((w_feat[:, :, 0:D], 0), (w_dst[:, :, :], 1)):
                link(dve.tensor_tensor(prod[:, :, :], w, attn[:, side:side + 1, :].broadcast_to([P, KT, D]), ALU.mult))
                to = (w_feat[:, :, D:D + H], w_v[:, :, HD:HD + H])[side]
                link(dve.tensor_reduce(to, prod[:, :, :].rearrange("p k (h d) -> p k h d", h=H), AX, ALU.add))
            dve.engine_nop().then_inc(w_ready, 1)
            with dve.Fori(0, NI) as i:
                for j in range(R):
                    g = i * R + j
                    dve.wait_ge(x_loaded[j], i * 16 + 16)
                    dve.wait_ge(k_done, g + 1)
                    dve.wait_ge(xn_stored[j], i * 16)
                    norm.find(dve, x_in[:, j, :], g)
                    norm.apply(dve, xn[:, j, :], x_in[:, j, :]).then_inc(xn_ready, 1)
                    dve.wait_ge(v_done, g + 1)
                    dve.tensor_copy(big_v[:, bass.ds(g, 1), 0:HD + H].rearrange("p a n -> p (a n)"),
                                    v_ps[j % 2][:, 0:HD + H]).then_inc(v_sb, 1)
            dve.wait_ge(v_sb, 2 + T)
            dve.tensor_copy(scores[:, 1, :, :], big_v[:, :, HD:HD + H]).then_inc(wd, 1)
            dve.wait_ge(wd, 5)

        @block.tensor
        def _(pe):
            pe.sem_inc(feat_done, R)
            pe.sem_inc(k_done, R)
            pe.wait_ge(w_ready, 1)
            with pe.Fori(0, NI) as i:
                for j in range(R):
                    g = i * R + j
                    pe.wait_ge(xn_ready, R + g + 1)
                    pe.wait_ge(turned_sb, 2 + g + 1 - before(j))
                    for k in range(KT):
                        last = pe.transpose(turned_ps[j % 2][:, k * P:(k + 1) * P], xn[:, j, k * P:(k + 1) * P], ident)
                    last.then_inc(turned, 1)
                    pe.wait_ge(sent_loaded[j], i * 16 + 16)
                    pe.wait_ge(feat_sb, 2 + g + 1 - before(j))
                    for k in range(KT):
                        last = pe.matmul(feat_ps[j % 2][:, 0:D + H], sent_in[:, j, k, :], w_feat[:, k, :],
                                         start=(k == 0), stop=(k == KT - 1))
                    last.then_inc(feat_done, 1)
                    pe.wait_ge(turned_sb, 2 + g + 1)
                    pe.wait_ge(v_sb, 2 + g + 1 - before(j))
                    for k in range(KT):
                        last = pe.matmul(v_ps[j % 2][:, 0:HD + H], xnT[:, j, k * P:(k + 1) * P], w_v[:, k, :],
                                         start=(k == 0), stop=(k == KT - 1))
                    last.then_inc(v_done, 1)
                    pe.wait_ge(k_sb, 2 + g + 1 - before(j))
                    for k in range(KT):
                        last = pe.matmul(k_ps[j % 2][:, 0:P], w_k[:, k, :], xnT[:, j, k * P:(k + 1) * P],
                                         start=(k == 0), stop=(k == KT - 1))
                    last.then_inc(k_done, 1)


def first_mixer(nc, A, hold, bank, const, big_k, big_v, fold):
    ident = const[:, C_ID:C_ID + P]
    with Stage(nc) as ctx:
        def sb(name, shape, dt=F32):
            return ctx.enter_context(nc.sbuf_tensor(name, shape, dt))

        def sem(name):
            return ctx.semaphore(name)

        w_qT = sb("m1_w_qT", [P, D])
        w_out = sb("m1_w_out", [P, D])
        peak = sb("m1_peak", [P, 1])
        total = sb("m1_total", [P, 1])
        ekT = sb("m1_ekT", [P, R, P])
        ek = sb("m1_ek", [P, R, P])
        ctx_sb = sb("m1_ctx", [P, P])
        ctxT = sb("m1_ctxT", [P, P])
        through = sb("m1_through", [P, D])
        w_in, dve_step, peak_ready, exp_ready = (sem("m1_w_in"), sem("m1_dve_step"), sem("m1_peak_ready"),
                                                 sem("m1_exp_ready"))
        turned, turned_sb = sem("m1_turned"), sem("m1_turned_sb")
        cut = sem("m1_cut")
        summed = sem("m1_summed")
        pe_step, done = sem("m1_pe_step"), sem("m1_done")
        block = ctx.enter_context(nc.Block())

        @block.sync
        def _(sp):
            sp.dma_start(w_qT[:, :], A["L0_mix_W_qT"]).then_inc(w_in, 16)
            sp.dma_start(w_out[:, :], A["L0_mix_W_out"]).then_inc(w_in, 16)

        @block.vector
        def _(dve):
            link = Steps(dve, dve_step)
            link(dve.tensor_reduce(peak[:, :], big_k[:, 0:N_NODES], AX, ALU.max))
            dve.tensor_scalar(peak[:, :], peak[:, :], -1.0, None, ALU.mult).then_inc(peak_ready, 1)
            dve.wait_ge(exp_ready, 1)
            link(dve.reciprocal(total[:, :], total[:, :]))
            link(dve.tensor_scalar(total[:, :], total[:, :], 32.0 ** -0.5, None, ALU.mult))
            with dve.Fori(0, NI) as i:
                for j in range(R):
                    g = i * R + j
                    dve.wait_ge(summed, g + 1)
                    dve.tensor_copy(ekT[:, j, :], big_k[:, bass.ds(g * P, P)]).then_inc(cut, 1)
            dve.wait_ge(pe_step, 1)
            dve.tensor_tensor(ctx_sb[:, :], bank[7][:, 0:P], const[:, C_BD:C_BD + P], ALU.mult).then_inc(done, 1)
            dve.wait_ge(pe_step, 2)
            dve.tensor_copy(ctxT[:, :], bank[2][:, 0:P]).then_inc(done, 1)
            dve.wait_ge(pe_step, 3)
            dve.tensor_scalar(through[:, :], bank[3][:, 0:D], total[:, 0:1], None, ALU.mult).then_inc(done, 1)
            dve.wait_ge(pe_step, 4)
            dve.tensor_copy(fold[:, :, :].rearrange("p k n -> p (k n)"), bank[4][:, :]).then_inc(done, 1)
            dve.wait_ge(done, 4)

        @block.scalar
        def _(act):
            act.sem_inc(turned_sb, 2)
            act.wait_ge(peak_ready, 1)
            act.activation(big_k[:, 0:N_NODES], big_k[:, 0:N_NODES], ACT.Exp, bias=peak[:, :],
                           accum_out=total[:, :]).then_inc(exp_ready, 1)
            with act.Fori(0, NI) as i:
                for j in range(R):
                    g = i * R + j
                    act.wait_ge(turned, g + 1)
                    act.wait_ge(summed, g + 1)
                    act.activation(ek[:, j, :], bank[j % 2][:, 0:P], ACT.Copy).then_inc(turned_sb, 1)

        @block.tensor
        def _(pe):
            pe.sem_inc(summed, R)
            pe.wait_ge(exp_ready, 1)
            pe.matmul(bank[7][:, 0:P], const[:, C_ZERO:C_ZERO + P], ident, start=True, stop=False)
            with pe.Fori(0, NI) as i:
                for j in range(R):
                    g = i * R + j
                    pe.wait_ge(turned_sb, 2 + g + 1 - (1 if j == 0 else 2))
                    pe.wait_ge(cut, g + 1)
                    pe.transpose(bank[j % 2][:, 0:P], ekT[:, j, :], ident).then_inc(turned, 1)
                    pe.wait_ge(turned_sb, 2 + g + 1)
                    pe.matmul(bank[7][:, 0:P], ek[:, j, :],
                              big_v[:, bass.ds(g, 1), 0:P].rearrange("p a n -> p (a n)"),
                              start=False, stop=False).then_inc(summed, 1)
            pe.matmul(bank[7][:, 0:P], const[:, C_ZERO:C_ZERO + P], ident, start=False, stop=True).then_inc(pe_step, 1)
            pe.wait_ge(done, 1)
            pe.transpose(bank[2][:, 0:P], ctx_sb[:, :], ident).then_inc(pe_step, 1)
            pe.wait_ge(w_in, 32)
            pe.wait_ge(done, 2)
            pe.matmul(bank[3][:, 0:D], ctxT[:, :], w_out[:, :], start=True, stop=True).then_inc(pe_step, 1)
            pe.wait_ge(done, 3)
            for k in range(KT):
                last = pe.matmul(bank[4][:, k * D:(k + 1) * D], w_qT[:, k * P:(k + 1) * P], through[:, :],
                                 start=True, stop=True)
            last.then_inc(pe_step, 1)


def edge_lookup(nc, A, hold, bank, const, scores, el_er, er, hi_lane, step_tile, src_lo_d, dst_lo_d):
    ident = const[:, C_ID:C_ID + P]
    U = G // 2
    NT = NS // G
    with Stage(nc) as ctx:
        def sb(name, shape, dt=F32):
            return ctx.enter_context(nc.sbuf_tensor(name, shape, dt))

        def sem(name):
            return ctx.semaphore(name)

        part_el = sb("ew_part_el", [P, 3, H, T], BF16)
        part_er = sb("ew_part_er", [P, 3, T, H], BF16)
        rest = sb("ew_rest", [P, T, H])
        src_bc = sb("ew_src_bc", [P, 2, U * P], BF16)
        dst_bc = sb("ew_dst_bc", [P, 2, U * P], BF16)
        src_hot = sb("ew_src_hot", [P, 2, U * P], BF16)
        dst_hot = sb("ew_dst_hot", [P, 2, U * P], BF16)
        hi_hot = sb("ew_hi_hot", [P, 2, U, T])
        picked = sb("ew_picked", [P, 2, U, H, T])
        el_ps, er_ps = [bank[0], bank[1]], [bank[2], bank[3]]

        split, parts_ready = sem("ew_split"), sem("ew_parts_ready")
        src_loaded = [sem(f"ew_src_loaded{u}") for u in range(2)]
        dst_loaded = [sem(f"ew_dst_loaded{u}") for u in range(2)]
        src_hot_ready, dst_hot_ready = sem("ew_src_hot_ready"), sem("ew_dst_hot_ready")
        looked_up = sem("ew_looked_up")
        hi_hot_ready, was_picked, el_taken, er_taken = (sem("ew_hi_hot_ready"), sem("ew_was_picked"),
                                                        sem("ew_el_taken"), sem("ew_er_taken"))
        block = ctx.enter_context(nc.Block())

        @block.sync
        def _(sp):
            with sp.Fori(0, NT) as i:
                for u in range(2):
                    q = 2 * i + u
                    for bc, lo, loaded, ready in ((src_bc, src_lo_d, src_loaded, src_hot_ready),
                                                  (dst_bc, dst_lo_d, dst_loaded, dst_hot_ready)):
                        hold(sp, ready, q + 1)
                        row = lo[bass.ds(q * U, U), :].rearrange("s l -> (s l)").partition_broadcast(P)
                        sp.dma_start(bc[:, u, :], row).then_inc(loaded[u], 16)

        @block.vector
        def _(dve):
            link = Steps(dve, split)
            dve.sem_inc(src_hot_ready, 2)
            dve.sem_inc(dst_hot_ready, 2)
            dve.sem_inc(er_taken, 2)
            for side, part in ((0, part_el[:, :, :, :].rearrange("p n h t -> p n t h")), (1, part_er[:, :, :, :])):
                link(dve.tensor_copy(rest[:, :, :], scores[:, side, :, :]))
                for n in range(3):
                    link(dve.tensor_copy(part[:, n], rest[:, :, :]))
                    if n < 2:
                        link(dve.tensor_tensor(rest[:, :, :], rest[:, :, :], part[:, n], ALU.subtract))
            dve.engine_nop().then_inc(parts_ready, 1)
            with dve.Fori(0, NT) as i:
                for u in range(2):
                    q = 2 * i + u
                    dve.wait_ge(src_loaded[u], 16 * i + 16)
                    dve.wait_ge(looked_up, q + 1)
                    dve.tensor_scalar(src_hot[:, u, :], src_bc[:, u, :], const[:, C_P:C_P + 1], None,
                                      ALU.is_equal).then_inc(src_hot_ready, 1)
                    dve.wait_ge(dst_loaded[u], 16 * i + 16)
                    dve.tensor_scalar(dst_hot[:, u, :], dst_bc[:, u, :], const[:, C_P:C_P + 1], None,
                                      ALU.is_equal).then_inc(dst_hot_ready, 1)
                    dve.wait_ge(el_taken, q)
                    dve.tensor_tensor(hi_hot[:, u, :, :],
                                      const[:, C_TILE:C_TILE + T].unsqueeze(1).broadcast_to([P, U, T]),
                                      hi_lane[:, bass.ds(q * U, U)].unsqueeze(2).broadcast_to([P, U, T]),
                                      ALU.is_equal).then_inc(hi_hot_ready, 1)
                    dve.wait_ge(hi_hot_ready, q + 1)
                    dve.wait_ge(looked_up, 2 + q + 1)
                    dve.tensor_tensor(picked[:, u, :, :, :],
                                      el_ps[u][:, 0:U * H * T].rearrange("p (s h t) -> p s h t", s=U, h=H),
                                      hi_hot[:, u, :, :].unsqueeze(2).broadcast_to([P, U, H, T]),
                                      ALU.mult).then_inc(was_picked, 1)
                    dve.wait_ge(was_picked, q + 1)
                    dve.tensor_reduce(el_er[:, 0, bass.ds(q * U, U), :], picked[:, u, :, :, :], AX, ALU.add)\
                       .then_inc(el_taken, 1)
                    dve.tensor_copy(er[:, bass.ds(q * U, U), :],
                                    er_ps[u][:, 0:U * H].rearrange("p (s h) -> p s h", s=U)).then_inc(er_taken, 1)

        @block.tensor
        def _(pe):
            pe.sem_inc(looked_up, 2)
            pe.wait_ge(parts_ready, 1)
            with pe.Fori(0, NT) as i:
                for u in range(2):
                    q = 2 * i + u
                    pe.wait_ge(src_hot_ready, 2 + q + 1)
                    pe.wait_ge(dst_hot_ready, 2 + q + 1)
                    pe.wait_ge(er_taken, q + 1)
                    for s in range(U):
                        for n in range(3):
                            pe.matmul(el_ps[u][:, s * H * T:(s + 1) * H * T], src_hot[:, u, s * P:(s + 1) * P],
                                      part_el[:, n, :, :].rearrange("p h t -> p (h t)"),
                                      start=(n == 0), stop=(n == 2))
                    for s in range(U):
                        tile = pe.value_load(step_tile[0:1, bass.ds(q * U + s, 1)], min_val=0, max_val=T - 1)
                        for n in range(3):
                            last = pe.matmul(er_ps[u][:, s * H:(s + 1) * H], dst_hot[:, u, s * P:(s + 1) * P],
                                             part_er[:, n, bass.ds(tile, 1), :].rearrange("p a h -> p (a h)"),
                                             start=(n == 0), stop=(n == 2))
                    last.then_inc(looked_up, 1)


def edge_exp(nc, el_er, er, weight):
    with Stage(nc) as last_ctx:
        def sem2(name):
            return last_ctx.semaphore(name)

        step, diff_ready, exp_ready = sem2("ee_step"), sem2("ee_diff_ready"), sem2("ee_exp_ready")
        leaky = last_ctx.enter_context(nc.sbuf_tensor("ee_leaky", [P, 2, NS, H], F32))
        block = last_ctx.enter_context(nc.Block())

        @block.vector
        def _(dve):
            link = Steps(dve, step)
            link(dve.tensor_tensor(el_er[:, :, :, :], el_er[:, :, :, :],
                                   er[:, :, :].unsqueeze(1).broadcast_to([P, 2, NS, H]), ALU.add))
            link(dve.scalar_tensor_tensor(out=leaky[:, :, :, :], in0=el_er[:, :, :, :], scalar=0.2,
                                          in1=el_er[:, :, :, :], op0=ALU.mult, op1=ALU.max))
            dve.tensor_tensor(weight[:, :, :], leaky[:, 0], leaky[:, 1], ALU.subtract).then_inc(diff_ready, 1)

        @block.scalar
        def _(act):
            act.wait_ge(diff_ready, 1)
            flat = weight[:, :, :].rearrange("p s h -> p (s h)")
            act.activation(flat, flat, ACT.Exp).then_inc(exp_ready, 1)
            act.wait_ge(exp_ready, 1)


def segment_maximum(nc, bank, const, dst_rows, el_er):
    with Stage(nc) as inner:
        def sb(name, shape, dt=F32):
            return inner.enter_context(nc.sbuf_tensor(name, shape, dt))

        def sem(name):
            return inner.semaphore(name)

        value = sb("sm_value", [RB, SB, H, P])
        change = sb("sm_change", [RB, SB, H, P])
        best = sb("sm_best", [RB, SB, H, P])
        ends = sb("sm_ends", [RB, 2, SB, H])
        peaks = sb("sm_peaks", [RB, 2, SB, H])
        end_row = sb("sm_end_row", [H, 2, NS])
        peak_row = sb("sm_peak_row", [H, 2, NS])
        linked = sb("sm_linked", [H, NS + 1])
        whole = sb("sm_whole", [H, NS])
        decay = sb("sm_decay", [H, NS])
        carried = sb("sm_carried", [H, 2, NS + 1])
        carry_row = sb("sm_carry_row", [H, 2, NS])
        carry = sb("sm_carry", [RB, 2, SB, H])
        same = sb("sm_same", [RB, SB, P])
        offer = sb("sm_offer", [RB, SB, H, P])
        step, pe_step, taken = sem("sm_step"), sem("sm_pe_step"), sem("sm_taken")
        block = inner.enter_context(nc.Block())
        ID = const[0:RB, C_ID:C_ID + RB]

        @block.tensor
        def _(pe):
            for b in range(SB):
                for h in range(H):
                    last = pe.transpose(bank[b][0:RB, h * P:(h + 1) * P],
                                        el_er[:, 0, b * RB:(b + 1) * RB, h], const[:, C_ID:C_ID + P])
                last.then_inc(pe_step, 1)
            pe.wait_ge(taken, 1)
            for n, src in enumerate((ends, peaks)):
                for side in range(2):
                    for b in range(SB):
                        last = pe.transpose(bank[4 + 2 * n + side][0:H, b * RB:(b + 1) * RB], src[:, side, b, :], ID)
            last.then_inc(pe_step, 1)
            pe.wait_ge(taken, 2)
            for side in range(2):
                for b in range(SB):
                    last = pe.transpose(bank[side][0:RB, b * H:(b + 1) * H],
                                        carry_row[:, side, b * RB:(b + 1) * RB], const[0:H, C_ID:C_ID + H])
            last.then_inc(pe_step, 1)
            pe.wait_ge(taken, 3)
            for h in range(H):
                for b in range(SB):
                    last = pe.transpose(bank[4 + h][:, b * RB:(b + 1) * RB], best[:, b, h, :], ID)
            last.then_inc(pe_step, 1)

        @block.vector
        def _(dve):
            link = Steps(dve, step)
            link(dve.memset(change[:, :, :, 0:1], -BIG))
            differ = dve.tensor_tensor(same[:, :, 1:P], dst_rows[:, :, 1:P], dst_rows[:, :, 0:P - 1], ALU.not_equal)
            link(differ)
            link(dve.tensor_scalar(change[:, :, :, 1:P], same[:, :, 1:P].unsqueeze(2).broadcast_to([RB, SB, H, P - 1]),
                                   -BIG, None, ALU.mult))
            for b in range(SB):
                dve.wait_ge(pe_step, b + 1)
                link(dve.tensor_copy(value[:, b, :, :].rearrange("p h l -> p (h l)"), bank[b][0:RB, :]))
            flat = "p b h l -> p (b h l)"
            n = SB * H * P
            v, c, m = (x[:, :, :, :].rearrange(flat) for x in (value, change, best))
            link(dve.tensor_tensor_scan(m, c, v, -BIG, ALU.add, ALU.max))
            link(dve.tensor_copy(v[:, n - 1:n], m[:, n - 1:n]))
            link(dve.tensor_tensor_scan(v[:, 0:n - 1][:, ::-1], c[:, 1:n][:, ::-1], m[:, 0:n - 1][:, ::-1],
                                        v[:, n - 1:n], ALU.add, ALU.max))
            for side, at in ((0, 0), (1, P - 1)):
                link(dve.tensor_copy(ends[:, side, :, :], dst_rows[:, :, at:at + 1].broadcast_to([RB, SB, H])))
                last = dve.tensor_copy(peaks[:, side, :, :], value[:, :, :, at])
                link(last) if side == 0 else last.then_inc(taken, 1)
            dve.wait_ge(pe_step, SB + 1)
            for side in range(2):
                link(dve.tensor_copy(end_row[:, side, :], bank[4 + side][0:H, 0:NS]))
                link(dve.tensor_copy(peak_row[:, side, :], bank[6 + side][0:H, 0:NS]))
            link(dve.memset(linked[:, :], -BIG))
            link(dve.tensor_tensor(linked[:, 1:NS], end_row[:, 0, 1:NS], end_row[:, 1, 0:NS - 1], ALU.not_equal))
            link(dve.tensor_scalar(linked[:, 1:NS], linked[:, 1:NS], -BIG, None, ALU.mult))
            link(dve.tensor_tensor(whole[:, :], end_row[:, 0, :], end_row[:, 1, :], ALU.not_equal))
            link(dve.tensor_scalar(whole[:, :], whole[:, :], -BIG, None, ALU.mult))
            link(dve.tensor_tensor(decay[:, :], whole[:, :], linked[:, 0:NS], ALU.min))
            link(dve.memset(carried[:, 0, 0:1], -BIG))
            link(dve.tensor_tensor_scan(carried[:, 0, 1:NS + 1], decay[:, :], peak_row[:, 1, :], -BIG,
                                        ALU.add, ALU.max))
            link(dve.tensor_tensor(carry_row[:, 0, :], carried[:, 0, 0:NS], linked[:, 0:NS], ALU.add))
            link(dve.tensor_tensor(decay[:, :], whole[:, :], linked[:, 1:NS + 1], ALU.min))
            link(dve.memset(carried[:, 1, NS:NS + 1], -BIG))
            link(dve.tensor_tensor_scan(carried[:, 1, 0:NS][:, ::-1], decay[:, ::-1], peak_row[:, 0, ::-1], -BIG,
                                        ALU.add, ALU.max))
            dve.tensor_tensor(carry_row[:, 1, :], carried[:, 1, 1:NS + 1], linked[:, 1:NS + 1], ALU.add)\
               .then_inc(taken, 1)
            dve.wait_ge(pe_step, SB + 2)
            for side in range(2):
                link(dve.tensor_copy(carry[:, side, :, :].rearrange("p b h -> p (b h)"), bank[side][0:RB, 0:SB * H]))
            for side in range(2):
                link(dve.tensor_tensor(same[:, :, :], dst_rows[:, :, :],
                                       ends[:, side, :, 0:1].broadcast_to([RB, SB, P]), ALU.not_equal))
                link(dve.tensor_scalar(offer[:, :, :, :], same[:, :, :].unsqueeze(2).broadcast_to([RB, SB, H, P]),
                                       -BIG, None, ALU.mult))
                link(dve.tensor_tensor(offer[:, :, :, :], offer[:, :, :, :],
                                       carry[:, side, :, :].unsqueeze(3).broadcast_to([RB, SB, H, P]), ALU.add))
                last = dve.tensor_tensor((value, best)[side][:, :, :, :], value[:, :, :, :], offer[:, :, :, :], ALU.max)
                link(last) if side == 0 else last.then_inc(taken, 1)
            dve.wait_ge(pe_step, SB + 3)
            for h in range(H):
                link(dve.tensor_copy(el_er[:, 1, :, h], bank[4 + h][:, 0:NS]))


def aggregate(nc, A, hold, name, bank, const, acc, step_tile, src_lane, dst_lane, table, weight, edge_weight):
    NT = NS // G
    W = D + H if edge_weight is None else D
    with Stage(nc) as ctx:
        def sb(nm, shape, dt=F32):
            return ctx.enter_context(nc.sbuf_tensor(f"{name}_{nm}", shape, dt))

        def sem(nm):
            return ctx.semaphore(f"{name}_{nm}")

        index = sb("index", [P, G], I32)
        rows = sb("rows", [P, G, D])
        hot = sb("hot", [P, G, P])
        msg = sb("msg", [P, G, W])
        zeroed, index_ready = sem("zeroed"), sem("index_ready")
        gathered = [sem(f"gathered{s}") for s in range(G)]
        hot_ready, msg_ready = sem("hot_ready"), sem("msg_ready")
        summed, added = sem("summed"), sem("added")
        block = ctx.enter_context(nc.Block())

        @block.gpsimd
        def _(pool):
            with pool.Fori(0, NT) as i:
                hold(pool, index_ready, i + 1)
                for s in range(G):
                    hold(pool, summed, i * G + s + 1)
                    pool.indirect_dma_start(rows[:, s, :], None, table,
                                            bass.IndirectOffsetOnAxis(ap=index[:, s:s + 1], axis=0))\
                        .then_inc(gathered[s], 16)

        @block.vector
        def _(dve):
            def add(i, s):
                n = i * G + s
                tile = dve.value_load(step_tile[0:1, bass.ds(n, 1)], min_val=0, max_val=T - 1)
                dve.wait_ge(summed, G + n + 1)
                dve.wait_ge(added, 2 + n)
                to = acc[:, bass.ds(tile, 1), 0:W].rearrange("p a n -> p (a n)")
                dve.tensor_tensor(to, bank[s % 2][:, 0:W], to, ALU.add).then_inc(added, 1)

            dve.memset(acc[:, :, :], 0.0).then_inc(zeroed, 1)
            dve.wait_ge(zeroed, 1)
            dve.sem_inc(added, 2)
            with dve.Fori(0, NT) as i:
                dve.wait_ge(gathered[G - 1], i * 16)
                dve.tensor_copy(index[:, :], src_lane[:, bass.ds(i * G, G)]).then_inc(index_ready, 1)
                for s in range(G):
                    n = i * G + s
                    dve.wait_ge(summed, n + 1)
                    dve.tensor_scalar(hot[:, s, :], const[:, C_IOTA:C_IOTA + P], dst_lane[:, bass.ds(n, 1)], None,
                                      ALU.is_equal).then_inc(hot_ready, 1)
                for s in range(G):
                    n = i * G + s
                    dve.wait_ge(gathered[s], i * 16 + 16)
                    if edge_weight is None:
                        w = weight[:, bass.ds(n, 1), :]
                        dve.tensor_tensor(msg[:, s, 0:D].rearrange("p (h d) -> p h d", h=H),
                                          rows[:, s, :].rearrange("p (h d) -> p h d", h=H),
                                          w.rearrange("p a h -> p (a h)").unsqueeze(2).broadcast_to([P, H, DH]),
                                          ALU.mult)
                        dve.tensor_copy(msg[:, s, D:D + H], w.rearrange("p a h -> p (a h)")).then_inc(msg_ready, 1)
                    else:
                        dve.tensor_scalar(msg[:, s, :], rows[:, s, :], edge_weight[:, bass.ds(n, 1)], None,
                                          ALU.mult).then_inc(msg_ready, 1)
                    if s >= 1:
                        add(i, s - 1)
                add(i, G - 1)

        @block.tensor
        def _(pe):
            pe.sem_inc(summed, G)
            with pe.Fori(0, NT) as i:
                for s in range(G):
                    n = i * G + s
                    pe.wait_ge(hot_ready, n + 1)
                    pe.wait_ge(msg_ready, n + 1)
                    pe.wait_ge(added, n + 1)
                    pe.matmul(bank[s % 2][:, 0:W], hot[:, s, :], msg[:, s, :], start=True, stop=True)\
                      .then_inc(summed, 1)


class Scope:

    def __init__(self, nc, ctx, name):
        self.nc, self.ctx, self.name = nc, ctx, name

    def sb(self, name, shape, dt=F32):
        return self.ctx.enter_context(self.nc.sbuf_tensor(f"{self.name}_{name}", shape, dt))

    def sem(self, name):
        return self.ctx.semaphore(f"{self.name}_{name}")

    def sems(self, name, n=R):
        return [self.sem(f"{name}{j}") for j in range(n)]

    def block(self):
        return self.ctx.enter_context(self.nc.Block())


def rows_of(x, g):
    return x[bass.ds(g * P, P), :]


def tile_of(x, g):
    return x[:, bass.ds(g, 1), :].rearrange("p a n -> p (a n)")


def weights(x):
    return x.rearrange("(k p) n -> p k n", p=P)


def first_graph_mlp(nc, A, hold, bank, const, acc, fold, xn1T, x_d, xn_d, xnT_d, x1_d, xn1_d):
    ident = const[:, C_ID:C_ID + P]
    FT = DF // P
    with Stage(nc) as ctx:
        S = Scope(nc, ctx, "g1")
        w1, w2, b1 = S.sb("w1", [P, KT, DF]), S.sb("w2", [P, FT, D]), S.sb("b1", [P, FT])
        bias = S.sb("bias", [P, 3, D])
        x_in, xn_in, xT_in = S.sb("x_in", [P, R, D]), S.sb("xn_in", [P, R, D]), S.sb("xT_in", [P, R, D])
        share, rst, low, high = (S.sb("share", [P, H]), S.sb("rst", [P, R, D]), S.sb("low", [P, R, D]),
                                 S.sb("high", [P, D]))
        h, hT, mid, x1, xn1 = (S.sb("h", [P, R, D]), S.sb("hT", [P, R, D]), S.sb("mid", [P, R, DF]),
                               S.sb("x1", [P, R, D]), S.sb("xn1", [P, R, D]))
        hT_ps, mid_ps, y_ps, xT_ps = ([bank[2 * n], bank[2 * n + 1]] for n in range(4))
        w_in, bias_ready = S.sem("w_in"), S.sem("bias_ready")
        loaded, x1_stored, xn1_stored = S.sems("loaded"), S.sems("x1_stored"), S.sems("xn1_stored")
        a_step, b_step, c_step = S.sem("a_step"), S.sem("b_step"), S.sem("c_step")
        low_ready, low_exp, h_ready, h_turned, hT_ready, mid_done, mid_ready, y_done, x1_ready, xn1_ready, \
            xn1_turned, xn1T_ready = (S.sem(n) for n in (
                "low_ready", "low_exp", "h_ready", "h_turned", "hT_ready", "mid_done", "mid_ready", "y_done",
                "x1_ready", "xn1_ready", "xn1_turned", "xn1T_ready"))
        norm = Norm(nc, ctx, "g1_norm", hold, const[:, C_POW:C_POW + 1])
        block = S.block()

        @block.sync
        def _(sp):
            for dst, src in ((w1, weights(A["L0_gnn_w1"])), (w2, weights(A["L0_gnn_w2"])), (b1, A["L0_gnn_b1"])):
                sp.dma_start(dst[...], src).then_inc(w_in, 16)
            for n, name in enumerate(("L0_gnn_gat_bias", "L0_gnn_b2", "L0_mix_b_out")):
                sp.dma_start(bias[:, n, :], A[name].broadcast_to([P, D])).then_inc(w_in, 16)

            def load(i, j):
                g = i * R + j
                once(sp, y_done, g - R + 1)
                once(sp, x1_ready, g - R + 1, hold)
                sp.dma_start(x_in[:, j, :], rows_of(x_d, g)).then_inc(loaded[j], 16)
                sp.dma_start(xn_in[:, j, :], rows_of(xn_d, g)).then_inc(loaded[j], 16)
                sp.dma_start(xT_in[:, j, :], xnT_d[bass.ds(g, 1), :, :].rearrange("a p n -> p (a n)"))\
                  .then_inc(loaded[j], 16)

            pipeline(sp, [(0, load)])
            for j in range(R):
                sp.wait_ge(x1_stored[j], 16 * NI)
                sp.wait_ge(xn1_stored[j], 16 * NI)

        @block.gpsimd
        def _(pool):
            def store(i, j):
                g = i * R + j
                hold(pool, x1_ready, g + 1)
                pool.dma_start(rows_of(x1_d, g), x1[:, j, :]).then_inc(x1_stored[j], 16)
                norm.root(pool, g)
                hold(pool, xn1_ready, g + 1)
                pool.dma_start(rows_of(xn1_d, g), xn1[:, j, :]).then_inc(xn1_stored[j], 16)

            pipeline(pool, [(0, store)])

        @block.vector
        def _(dve):
            dve.wait_ge(w_in, 96)
            dve.tensor_tensor(bias[:, 1, :], bias[:, 1, :], bias[:, 2, :], ALU.add).then_inc(bias_ready, 1)
            dve.wait_ge(bias_ready, 1)

            def mean(i, j):
                g = i * R + j
                link = Steps(dve, a_step, g, 4)
                link(dve.tensor_scalar(share[:, :], tile_of(acc, g)[:, D:D + H], 1e-30, None, ALU.max))
                link(dve.reciprocal(share[:, :], share[:, :]))
                link(dve.tensor_tensor(rst[:, j, :].rearrange("p (h d) -> p h d", h=H),
                                       tile_of(acc, g)[:, 0:D].rearrange("p (h d) -> p h d", h=H),
                                       share[:, :].unsqueeze(2).broadcast_to([P, H, DH]), ALU.mult))
                link(dve.tensor_tensor(rst[:, j, :], rst[:, j, :], bias[:, 0, :], ALU.add))
                link.end()
                dve.tensor_scalar(low[:, j, :], rst[:, j, :], 0.0, None, ALU.min).then_inc(low_ready, 1)

            def elu(i, j):
                g = i * R + j
                link = Steps(dve, b_step, g, 1)
                dve.wait_ge(low_exp, g + 1)
                dve.wait_ge(loaded[j], 48 * i + 48)
                link(dve.scalar_tensor_tensor(out=high[:, :], in0=rst[:, j, :], scalar=0.0, in1=low[:, j, :],
                                              op0=ALU.max, op1=ALU.add))
                link.end()
                dve.scalar_tensor_tensor(out=h[:, j, :], in0=high[:, :], scalar=-1.0, in1=xn_in[:, j, :],
                                         op0=ALU.add, op1=ALU.add).then_inc(h_ready, 1)

            def residual(i, j):
                g = i * R + j
                link = Steps(dve, c_step, g, 1)
                once(dve, x1_stored[j], i * 16)
                link(dve.tensor_tensor(x1[:, j, :], x_in[:, j, :], bias[:, 1, :], ALU.add))
                link.end()
                dve.wait_ge(y_done, g + 1)
                dve.tensor_tensor(x1[:, j, :], y_ps[j % 2][:, 0:D], x1[:, j, :], ALU.add).then_inc(x1_ready, 1)
                dve.wait_ge(x1_ready, g + 1)
                norm.find(dve, x1[:, j, :], g)
                once(dve, xn1_stored[j], i * 16)
                once(dve, xn1_turned, g - R + 1)
                norm.apply(dve, xn1[:, j, :], x1[:, j, :]).then_inc(xn1_ready, 1)

            pipeline(dve, [(0, mean), (1, elu), (3, residual)])

        @block.scalar
        def _(act):
            act.wait_ge(w_in, 96)

            def exp_low(i, j):
                g = i * R + j
                act.wait_ge(low_ready, g + 1)
                act.activation(low[:, j, :], low[:, j, :], ACT.Exp).then_inc(low_exp, 1)

            def copy_h(i, j):
                g = i * R + j
                act.wait_ge(h_turned, g + 1)
                act.activation(hT[:, j, :], hT_ps[j % 2][:, 0:D], ACT.Copy).then_inc(hT_ready, 1)

            def relu(i, j):
                g = i * R + j
                act.wait_ge(mid_done, g + 1)
                for f in range(FT):
                    last = act.activation(mid[:, j, f * P:(f + 1) * P], mid_ps[j % 2][:, f * P:(f + 1) * P], ACT.Relu,
                                          bias=b1[:, f:f + 1])
                last.then_inc(mid_ready, 1)

            def copy_x(i, j):
                g = i * R + j
                act.wait_ge(xn1_turned, g + 1)
                act.activation(xn1T[:, :, bass.ds(g * P, P)], xT_ps[j % 2][:, 0:D].rearrange("p (k n) -> p k n", k=KT),
                               ACT.Copy).then_inc(xn1T_ready, 1)

            pipeline(act, [(0, exp_low), (1, copy_h), (2, relu), (4, copy_x)])

        @block.tensor
        def _(pe):
            pe.wait_ge(w_in, 96)

            def turn_h(i, j):
                g = i * R + j
                pe.wait_ge(h_ready, g + 1)
                once(pe, hT_ready, g - bank_gap(j) + 1)
                for k in range(KT):
                    last = pe.transpose(hT_ps[j % 2][:, k * P:(k + 1) * P], h[:, j, k * P:(k + 1) * P], ident)
                last.then_inc(h_turned, 1)

            def mlp_in(i, j):
                g = i * R + j
                pe.wait_ge(hT_ready, g + 1)
                once(pe, mid_ready, g - bank_gap(j) + 1)
                for f in range(FT):
                    for k in range(KT):
                        last = pe.matmul(mid_ps[j % 2][:, f * P:(f + 1) * P], w1[:, k, f * P:(f + 1) * P],
                                         hT[:, j, k * P:(k + 1) * P], start=(k == 0), stop=(k == KT - 1))
                last.then_inc(mid_done, 1)

            def mlp_out(i, j):
                g = i * R + j
                pe.wait_ge(mid_ready, g + 1)
                once(pe, x1_ready, g - bank_gap(j) + 1)
                pe.wait_ge(loaded[j], 48 * i + 48)
                for f in range(FT):
                    pe.matmul(y_ps[j % 2][:, 0:D], mid[:, j, f * P:(f + 1) * P], w2[:, f, :], start=(f == 0), stop=False)
                for k in range(KT):
                    last = pe.matmul(y_ps[j % 2][:, 0:D], xT_in[:, j, k * P:(k + 1) * P], fold[:, k, :],
                                     start=False, stop=(k == KT - 1))
                last.then_inc(y_done, 1)

            def turn_x(i, j):
                g = i * R + j
                pe.wait_ge(xn1_ready, g + 1)
                once(pe, xn1T_ready, g - bank_gap(j) + 1)
                for k in range(KT):
                    last = pe.transpose(xT_ps[j % 2][:, k * P:(k + 1) * P], xn1[:, j, k * P:(k + 1) * P], ident)
                last.then_inc(xn1_turned, 1)

            pipeline(pe, [(0, turn_h), (1, mlp_in), (2, mlp_out), (4, turn_x)])


def first_router(nc, A, hold, bank, const, xn1T, w1, w2, b1, bias):
    FT = DF // P
    capacity = float(-(-N_NODES * 5 // (4 * E)))
    with Stage(nc) as ctx:
        S = Scope(nc, ctx, "r1")
        mean, w_r, line, small = S.sb("mean", [P, KT]), S.sb("w_r", [P, KT, E]), S.sb("line", [1, 6, E]), S.sb("small", [1, 4])
        top, index, pair = S.sb("top", [1, E]), S.sb("index", [1, E], U32), S.sb("pair", [1, 2])
        share, b2 = S.sb("share", [P, 2]), S.sb("b2", [P, 2, D])
        w_in, step, mean_ready, logits, peak, exp_done, picked, spread, experts_in, shared = (S.sem(n) for n in (
            "w_in", "step", "mean_ready", "logits", "peak", "exp_done", "picked", "spread", "experts_in", "shared"))
        block = S.block()
        x, e, rw, load, cut, br = (line[:, n, :] for n in range(6))

        @block.sync
        def _(sp):
            sp.dma_start(w_r[:, :, :], weights(A["L0_ffn_Wr"])).then_inc(w_in, 16)
            sp.dma_start(br, A["L0_ffn_br"]).then_inc(w_in, 16)
            sp.wait_ge(picked, 1)
            for n in range(2):
                at = sp.value_load(index[0:1, n:n + 1], min_val=0, max_val=E - 1)
                sp.dma_start(w1[:, n, :, :], A["L0_ffn_W1"][bass.ds(at, 1), :, :]
                             .rearrange("a (k p) n -> p (a k) n", p=P)).then_inc(experts_in, 16)
                sp.dma_start(w2[:, n, :, :], A["L0_ffn_W2"][bass.ds(at, 1), :, :]
                             .rearrange("a (k p) n -> p (a k) n", p=P)).then_inc(experts_in, 16)
                sp.dma_start(b1[:, n, :], A["L0_ffn_b1"][bass.ds(at, 1), :, :].rearrange("a p f -> p (a f)"))\
                  .then_inc(experts_in, 16)
                sp.dma_start(b2[:, n, :], A["L0_ffn_b2"][bass.ds(at, 1), :].broadcast_to([P, D])).then_inc(experts_in, 16)

        @block.tensor
        def _(pe):
            pe.wait_ge(w_in, 32)
            pe.wait_ge(mean_ready, 1)
            for k in range(KT):
                last = pe.matmul(bank[0][0:1, 0:E], mean[:, k:k + 1], w_r[:, k, :], start=(k == 0), stop=(k == KT - 1))
            last.then_inc(logits, 1)
            pe.wait_ge(shared, 1)
            pe.matmul(bank[1][:, 0:2], const[0:1, C_ONE:C_ONE + P], pair[:, :], start=True, stop=True).then_inc(spread, 1)

        @block.scalar
        def _(act):
            for n, (dst, width) in enumerate(((e, E), (e, E), (pair[:, :], 2))):
                act.wait_ge(peak, n + 1)
                src = dst if n == 2 else x
                act.activation(dst, src, ACT.Exp).then_inc(exp_done, 1)

        @block.vector
        def _(dve):
            link = Steps(dve, step)

            def softmax(src, dst, at, n, tmp):
                link(dve.tensor_reduce(small[:, at:at + 1], src, AX, ALU.max))
                dve.tensor_scalar(tmp, src, small[:, at:at + 1], None, ALU.subtract).then_inc(peak, 1)
                dve.wait_ge(exp_done, n + 1)
                out = pair[:, :] if n == 2 else e
                link(dve.tensor_reduce(small[:, at:at + 1], out, AX, ALU.add))
                link(dve.reciprocal(small[:, at:at + 1], small[:, at:at + 1]))
                return dve.tensor_scalar(dst, out, small[:, at:at + 1], None, ALU.mult)

            link(dve.tensor_reduce(mean[:, :], xn1T[:, :, 0:N_NODES], AX, ALU.add))
            dve.tensor_scalar(mean[:, :], mean[:, :], 1.0 / N_NODES, None, ALU.mult).then_inc(mean_ready, 1)
            dve.wait_ge(logits, 1)
            link(dve.tensor_tensor(cut, bank[0][0:1, 0:E], br, ALU.add))
            link(softmax(cut, rw, 0, 0, x))
            link(dve.tensor_scalar(load, rw, float(N_NODES), None, ALU.mult))
            link(dve.reciprocal(cut, load))
            link(dve.tensor_scalar(cut, cut, capacity, None, ALU.mult))
            link(dve.tensor_scalar(load, load, capacity, None, ALU.is_gt))
            link(dve.tensor_tensor(cut, cut, load, ALU.mult))
            link(dve.tensor_scalar(load, load, -1.0, 1.0, ALU.mult, ALU.add))
            link(dve.tensor_tensor(cut, cut, load, ALU.add))
            link(dve.tensor_tensor(rw, rw, cut, ALU.mult))
            link(softmax(rw, cut, 1, 1, x))
            link(dve.max(top[:, :], cut))
            dve.max_index(index[:, :], top[:, :], cut).then_inc(picked, 1)
            link(softmax(top[:, 0:2], pair[:, :], 2, 2, pair[:, :]))
            dve.engine_nop().then_inc(shared, 1)
            dve.wait_ge(spread, 1)
            link(dve.tensor_copy(share[:, :], bank[1][:, 0:2]))
            dve.wait_ge(experts_in, 16 * 8)
            for n in range(2):
                link(dve.tensor_scalar(w2[:, n, :, :], w2[:, n, :, :], share[:, n:n + 1], None, ALU.mult))
            link(dve.tensor_scalar(bias[:, :], b2[:, 0, :], share[:, 0:1], None, ALU.mult))
            link(dve.scalar_tensor_tensor(out=bias[:, :], in0=b2[:, 1, :], scalar=share[:, 1:2], in1=bias[:, :],
                                          op0=ALU.mult, op1=ALU.add))


def first_experts(nc, A, hold, bank, const, xn1T, w1, w2, b1, bias, big_k, big_v, x1_d, xn1_d, x2_d, xn2_d, qT_d):
    ident = const[:, C_ID:C_ID + P]
    FT = 2 * DF // P
    HM, SM = 8, 32
    with Stage(nc) as ctx:
        S = Scope(nc, ctx, "e1")
        vec = S.sb("vec", [P, 2, D])
        col = S.sb("col", [P, 3, KT])
        w_x, w_q, w_k, w_v = S.sb("w_x", [P, KT, D]), S.sb("w_q", [P, P]), S.sb("w_k", [P, P]), S.sb("w_v", [P, P])
        N2 = 2
        x1_in, xn1_in = S.sb("x1_in", [P, R, D]), S.sb("xn1_in", [P, R, D])
        mid = S.sb("mid", [P, N2, FT * P])
        y, out0 = S.sb("y", [P, D]), S.sb("out0", [P, D])
        x2, xn2, ln = S.sb("x2", [P, R, D]), S.sb("xn2", [P, R, D]), S.sb("ln", [P, R, D])
        lnT, xm = S.sb("lnT", [P, D]), S.sb("xm", [P, D])
        q, small, qT = S.sb("q", [P, R, D]), S.sb("small", [P, HM]), S.sb("qT", [P, R, D])
        w_in = S.sem("w_in")
        loaded, x2_stored, xn2_stored, qT_stored = (S.sems(n) for n in ("loaded", "x2_stored", "xn2_stored", "qT_stored"))
        c_step, a_step, b_step, l_step, m_step = (S.sem(n) for n in ("c_step", "a_step", "b_step", "l_step", "m_step"))
        mid_done0, mid_done1, mid_ready0, mid_ready1, y_done, y_ready, x2_ready, xn2_ready, ln_ready, ln_turned, lnT_ready, \
            xm_done, xm_ready, qv_done, k_done, k_ready, q_cut, v_ready, q_exp, q_ready, q_turned, qT_ready = (
                S.sem(n) for n in ("mid_done0", "mid_done1", "mid_ready0", "mid_ready1", "y_done", "y_ready",
                                   "x2_ready", "xn2_ready", "ln_ready", "ln_turned", "lnT_ready", "xm_done", "xm_ready",
                                   "qv_done", "k_done", "k_ready", "q_cut", "v_ready", "q_exp", "q_ready", "q_turned",
                                   "qT_ready"))
        norms = [Norm(nc, ctx, f"e1_norm{n}", hold, const[:, C_POW:C_POW + 1]) for n in range(3)]
        mid_ps, y_ps, ln_ps, xm_ps, qv_ps, k_ps, q_ps = [bank[0], bank[1]], *bank[2:8]
        mid_done, mid_ready = [mid_done0, mid_done1], [mid_ready0, mid_ready1]
        block = S.block()

        @block.sync
        def _(sp):
            for n, name in enumerate(("L0_ffn_gamma", "L0_ffn_beta")):
                sp.dma_start(vec[:, n, :], A[name].broadcast_to([P, D])).then_inc(w_in, 16)
            for n, name in enumerate(("L1_mix_ln1_w", "L1_mix_ln1_b", "L1_mix_bx")):
                sp.dma_start(col[:, n, :], A[name]).then_inc(w_in, 16)
            sp.dma_start(w_x[:, :, :], weights(A["L1_mix_WxT"])).then_inc(w_in, 16)
            for w, name in ((w_q, "L1_mix_WqT4"), (w_k, "L1_mix_WkT4"), (w_v, "L1_mix_WvT4")):
                sp.dma_start(w[:, :], A[name]).then_inc(w_in, 16)

            def load(i, j):
                g = i * R + j
                once(sp, x2_ready, g - R + 1, hold)
                sp.dma_start(x1_in[:, j, :], rows_of(x1_d, g)).then_inc(loaded[j], 16)
                sp.dma_start(xn1_in[:, j, :], rows_of(xn1_d, g)).then_inc(loaded[j], 16)

            pipeline(sp, [(0, load)])
            for j in range(R):
                for s in (x2_stored, xn2_stored, qT_stored):
                    sp.wait_ge(s[j], 16 * NI)

        @block.gpsimd
        def _(pool):
            def tail(i, j):
                g = i * R + j
                norms[0].root(pool, g)
                hold(pool, x2_ready, g + 1)
                pool.dma_start(rows_of(x2_d, g), x2[:, j, :]).then_inc(x2_stored[j], 16)
                norms[1].root(pool, g)
                hold(pool, xn2_ready, g + 1)
                pool.dma_start(rows_of(xn2_d, g), xn2[:, j, :]).then_inc(xn2_stored[j], 16)
                norms[2].root(pool, g)

            pipeline(pool, [(0, tail)])

        @block.vector
        def _(dve):
            dve.wait_ge(w_in, 16 * 9)

            def chain(i, j):
                g = i * R + j
                dve.wait_ge(loaded[j], 32 * i + 32)
                link = Steps(dve, c_step, g, 5)
                link(dve.tensor_tensor(y[:, :], xn1_in[:, j, :], bias[:, :], ALU.add))
                dve.wait_ge(y_done, g + 1)
                dve.tensor_tensor(y[:, :], y_ps[:, 0:D], y[:, :], ALU.add).then_inc(y_ready, 1)
                dve.wait_ge(y_ready, g + 1)
                norms[0].find(dve, y[:, :], g)
                link(norms[0].apply(dve, out0[:, :], y[:, :]))
                link(dve.tensor_tensor(out0[:, :], out0[:, :], vec[:, 0, :], ALU.mult))
                link(dve.tensor_tensor(out0[:, :], out0[:, :], vec[:, 1, :], ALU.add))
                once(dve, x2_stored[j], 16 * i)
                dve.tensor_tensor(x2[:, j, :], out0[:, :], x1_in[:, j, :], ALU.add).then_inc(x2_ready, 1)
                dve.wait_ge(x2_ready, g + 1)
                norms[1].find(dve, x2[:, j, :], g)
                once(dve, xn2_stored[j], 16 * i)
                norms[1].apply(dve, xn2[:, j, :], x2[:, j, :]).then_inc(xn2_ready, 1)
                dve.wait_ge(xn2_ready, g + 1)
                norms[2].find(dve, xn2[:, j, :], g)
                once(dve, ln_turned, g - R + 1)
                norms[2].apply(dve, ln[:, j, :], xn2[:, j, :]).then_inc(ln_ready, 1)
                link(dve.tensor_copy(small[:, 0:1], norms[2].mv[:, 0:1]))
                link.end()

            def cut(i, j):
                g = i * R + j
                dve.wait_ge(qv_done, g + 1)
                link = Steps(dve, a_step, g, 1)
                q_in = qv_ps[:, 0:D].rearrange("p (h s) -> p h s", h=HM)
                link(dve.tensor_reduce(small[:, :], q_in, AX, ALU.max))
                link.end()
                once(dve, q_turned, g - R + 1)
                dve.tensor_tensor(q[:, j, :].rearrange("p (h s) -> p h s", h=HM), q_in,
                                  small[:, :].unsqueeze(2).broadcast_to([P, HM, SM]), ALU.subtract).then_inc(q_cut, 1)
                dve.tensor_copy(tile_of(big_v, g), qv_ps[:, D:2 * D]).then_inc(v_ready, 1)

            def divide(i, j):
                g = i * R + j
                dve.wait_ge(q_exp, g + 1)
                link = Steps(dve, b_step, g, 2)
                view = q[:, j, :].rearrange("p (h s) -> p h s", h=HM)
                link(dve.tensor_reduce(small[:, :], view, AX, ALU.add))
                link(dve.reciprocal(small[:, :], small[:, :]))
                link.end()
                dve.tensor_tensor(view, view, small[:, :].unsqueeze(2).broadcast_to([P, HM, SM]), ALU.mult)\
                   .then_inc(q_ready, 1)

            pipeline(dve, [(4, divide), (1, chain), (3, cut)])

        @block.scalar
        def _(act):
            act.wait_ge(w_in, 16 * 9)

            def copy_ln(i, j):
                g = i * R + j
                act.wait_ge(ln_turned, g + 1)
                once(act, xm_done, g)
                for k in range(KT):
                    last = act.activation(lnT[:, k * P:(k + 1) * P], ln_ps[:, k * P:(k + 1) * P], ACT.Identity,
                                          bias=col[:, 1, k:k + 1], scale=col[:, 0, k:k + 1])
                last.then_inc(lnT_ready, 1)

            def copy_q(i, j):
                g = i * R + j
                act.wait_ge(q_turned, g + 1)
                once(act, qT_stored[j], 16 * i)
                act.activation(qT[:, j, :], q_ps[:, 0:D], ACT.Copy).then_inc(qT_ready, 1)
                act.wait_ge(qT_ready, g + 1)
                act.dma_start(qT_d[bass.ds(g, 1), :, :].rearrange("a p n -> p (a n)"), qT[:, j, :])\
                   .then_inc(qT_stored[j], 16)

            def gelu(i, j):
                g = i * R + j
                once(act, y_done, g)
                for half in range(2):
                    act.wait_ge(mid_done[half], g + 1)
                    for f in range(4):
                        n = half * 4 + f
                        last = act.activation(mid[:, 0, n * P:(n + 1) * P], mid_ps[half][:, f * P:(f + 1) * P],
                                              ACT.Gelu, bias=b1[:, half, f:f + 1])
                    last.then_inc(mid_ready[half], 1)

            def add_bx(i, j):
                g = i * R + j
                act.wait_ge(xm_done, g + 1)
                once(act, k_done, g)
                for k in range(KT):
                    last = act.activation(xm[:, k * P:(k + 1) * P], xm_ps[:, k * P:(k + 1) * P], ACT.Identity,
                                          bias=col[:, 2, k:k + 1])
                last.then_inc(xm_ready, 1)

            def copy_k(i, j):
                g = i * R + j
                act.wait_ge(k_done, g + 1)
                act.activation(big_k[:, :].rearrange("p (k n) -> p k n", k=KT)[:, :, bass.ds(g * P, P)],
                               k_ps[:, 0:D].rearrange("p (k n) -> p k n", k=KT), ACT.Copy).then_inc(k_ready, 1)
                act.wait_ge(q_cut, g + 1)
                act.activation(q[:, j, :], q[:, j, :], ACT.Exp).then_inc(q_exp, 1)

            pipeline(act, [(3, copy_ln), (4, copy_q), (0, gelu), (3, add_bx), (3, copy_k)])

        @block.tensor
        def _(pe):
            pe.wait_ge(w_in, 16 * 9)

            def turn_ln(i, j):
                g = i * R + j
                pe.wait_ge(ln_ready, g + 1)
                once(pe, lnT_ready, g)
                for k in range(KT):
                    last = pe.transpose(ln_ps[:, k * P:(k + 1) * P], ln[:, j, k * P:(k + 1) * P], ident)
                last.then_inc(ln_turned, 1)

            def turn_q(i, j):
                g = i * R + j
                pe.wait_ge(q_ready, g + 1)
                once(pe, qT_ready, g)
                for k in range(KT):
                    last = pe.transpose(q_ps[:, k * P:(k + 1) * P], q[:, j, k * P:(k + 1) * P], ident)
                last.then_inc(q_turned, 1)

            def expert_in(i, j):
                g = i * R + j
                for half in range(2):
                    once(pe, mid_ready[half], g)
                    for f in range(4):
                        for k in range(KT):
                            last = pe.matmul(mid_ps[half][:, f * P:(f + 1) * P], w1[:, half, k, f * P:(f + 1) * P],
                                             xn1T[:, k, bass.ds(g * P, P)], start=(k == 0), stop=(k == KT - 1))
                    last.then_inc(mid_done[half], 1)

            def expert_out(i, j):
                g = i * R + j
                once(pe, y_ready, g)
                for half in range(2):
                    pe.wait_ge(mid_ready[half], g + 1)
                    for f in range(4):
                        n = half * 4 + f
                        last = pe.matmul(y_ps[:, 0:D], mid[:, 0, n * P:(n + 1) * P], w2[:, half, f, :],
                                         start=(n == 0), stop=(n == FT - 1))
                last.then_inc(y_done, 1)

            def project_x(i, j):
                g = i * R + j
                pe.wait_ge(lnT_ready, g + 1)
                once(pe, xm_ready, g)
                for m in range(KT):
                    for k in range(KT):
                        last = pe.matmul(xm_ps[:, m * P:(m + 1) * P], w_x[:, k, m * P:(m + 1) * P],
                                         lnT[:, k * P:(k + 1) * P], start=(k == 0), stop=(k == KT - 1))
                last.then_inc(xm_done, 1)

            def project_qkv(i, j):
                g = i * R + j
                pe.wait_ge(xm_ready, g + 1)
                once(pe, v_ready, g)
                for n, w in enumerate((w_q, w_v)):
                    for m in range(KT):
                        last = pe.matmul(qv_ps[:, n * D + m * P:n * D + (m + 1) * P], xm[:, m * P:(m + 1) * P], w[:, :],
                                         start=True, stop=True)
                last.then_inc(qv_done, 1)
                once(pe, k_ready, g)
                for m in range(KT):
                    last = pe.matmul(k_ps[:, m * P:(m + 1) * P], w_k[:, :], xm[:, m * P:(m + 1) * P],
                                     start=True, stop=True)
                last.then_inc(k_done, 1)

            pipeline(pe, [(3, turn_ln), (4, turn_q), (0, expert_in), (3, project_x), (1, expert_out), (3, project_qkv)])


def second_mixer(nc, A, hold, bank, const, big_k, big_v, folded):
    ident = const[:, C_ID:C_ID + P]
    zero = const[:, C_ZERO:C_ZERO + P]
    with Stage(nc) as ctx:
        S = Scope(nc, ctx, "m2")
        w_o, peak, total = S.sb("w_o", [P, KT, D]), S.sb("peak", [P, KT]), S.sb("total", [P, KT])
        ekT, ek = S.sb("ekT", [P, R, D]), S.sb("ek", [P, R, D])
        kv, kvT = S.sb("kv", [P, KT, P]), S.sb("kvT", [P, KT, P])
        w_in, step, peak_ready, exp_ready, cut, turned, ek_ready, summed, pe_step, done = (S.sem(n) for n in (
            "w_in", "step", "peak_ready", "exp_ready", "cut", "turned", "ek_ready", "summed", "pe_step", "done"))
        block = S.block()
        k_view = big_k[:, :].rearrange("p (k n) -> p k n", k=KT)

        @block.sync
        def _(sp):
            sp.dma_start(w_o[:, :, :], weights(A["L1_mix_WoT"])).then_inc(w_in, 16)

        @block.vector
        def _(dve):
            link = Steps(dve, step)
            link(dve.memset(k_view[:, :, N_NODES:NP], 0.0))
            link(dve.tensor_reduce(peak[:, :], k_view[:, :, 0:N_NODES], AX, ALU.max))
            dve.tensor_scalar(peak[:, :], peak[:, :], -1.0, None, ALU.mult).then_inc(peak_ready, 1)
            dve.wait_ge(exp_ready, KT)
            link(dve.reciprocal(total[:, :], total[:, :]))

            def cut_tile(i, j):
                g = i * R + j
                once(dve, turned, g - R + 1)
                dve.tensor_copy(ekT[:, j, :].rearrange("p (k n) -> p k n", k=KT), k_view[:, :, bass.ds(g * P, P)])\
                   .then_inc(cut, 1)

            pipeline(dve, [(0, cut_tile)])
            dve.wait_ge(pe_step, 1)
            for m in range(KT):
                last = dve.tensor_tensor(kv[:, m, :], bank[4 + m][:, 0:P], const[:, C_BD:C_BD + P], ALU.mult)
            last.then_inc(done, 1)
            dve.wait_ge(pe_step, 2)
            dve.tensor_copy(kvT[:, :, :].rearrange("p k n -> p (k n)"), bank[2][:, 0:D]).then_inc(done, 1)
            dve.wait_ge(pe_step, 3)
            for m in range(KT):
                last = dve.tensor_scalar(folded[:, m, :], bank[3][:, m * D:(m + 1) * D], total[:, m:m + 1], None, ALU.mult)
            last.then_inc(done, 1)
            dve.wait_ge(done, 3)

        @block.scalar
        def _(act):
            act.wait_ge(peak_ready, 1)
            for k in range(KT):
                act.activation(k_view[:, k, 0:N_NODES], k_view[:, k, 0:N_NODES], ACT.Exp, bias=peak[:, k:k + 1],
                               accum_out=total[:, k:k + 1]).then_inc(exp_ready, 1)

            def copy_ek(i, j):
                g = i * R + j
                act.wait_ge(turned, g + 1)
                once(act, summed, g - R + 1)
                act.activation(ek[:, j, :], bank[j % 2][:, 0:D], ACT.Copy).then_inc(ek_ready, 1)

            pipeline(act, [(0, copy_ek)])

        @block.tensor
        def _(pe):
            pe.wait_ge(w_in, 16)
            for m in range(KT):
                pe.matmul(bank[4 + m][:, 0:P], zero, ident, start=True, stop=False)

            def turn(i, j):
                g = i * R + j
                pe.wait_ge(cut, g + 1)
                once(pe, ek_ready, g - bank_gap(j) + 1)
                for k in range(KT):
                    last = pe.transpose(bank[j % 2][:, k * P:(k + 1) * P], ekT[:, j, k * P:(k + 1) * P], ident)
                last.then_inc(turned, 1)

            def add(i, j):
                g = i * R + j
                pe.wait_ge(ek_ready, g + 1)
                for m in range(KT):
                    last = pe.matmul(bank[4 + m][:, 0:P], ek[:, j, m * P:(m + 1) * P],
                                     tile_of(big_v, g)[:, m * P:(m + 1) * P], start=False, stop=False)
                last.then_inc(summed, 1)

            pipeline(pe, [(0, turn), (1, add)])
            for m in range(KT):
                last = pe.matmul(bank[4 + m][:, 0:P], zero, ident, start=False, stop=True)
            last.then_inc(pe_step, 1)
            pe.wait_ge(done, 1)
            for m in range(KT):
                last = pe.transpose(bank[2][:, m * P:(m + 1) * P], kv[:, m, :], ident)
            last.then_inc(pe_step, 1)
            pe.wait_ge(done, 2)
            for m in range(KT):
                last = pe.matmul(bank[3][:, m * D:(m + 1) * D], kvT[:, m, :], w_o[:, m, :], start=True, stop=True)
            last.then_inc(pe_step, 1)


def mixer_mlp(nc, A, hold, bank, const, folded, x2_d, xn2_d, qT_d, mixed_d):
    ident = const[:, C_ID:C_ID + P]
    FT = HID // P
    with Stage(nc) as ctx:
        S = Scope(nc, ctx, "x2")
        w1, w2, b1 = S.sb("w1", [P, KT, HID]), S.sb("w2", [P, FT, D]), S.sb("b1", [P, FT])
        vec, col = S.sb("vec", [P, 2, D]), S.sb("col", [P, 2, KT])
        x_in, xn_in, qT_in = S.sb("x_in", [P, R, D]), S.sb("xn_in", [P, R, D]), S.sb("qT_in", [P, R, D])
        h, ln, lnT, mid, mixed = (S.sb("h", [P, R, D]), S.sb("ln", [P, R, D]), S.sb("lnT", [P, R, D]),
                                  S.sb("mid", [P, FT * P]), S.sb("mixed", [P, R, D]))
        w_in = S.sem("w_in")
        loaded, stored = S.sems("loaded"), S.sems("stored")
        a_step, c_step = S.sem("a_step"), S.sem("c_step")
        h_done, h_ready, ln_ready, ln_turned, lnT_ready, y_done, mixed_ready, mid_done0, mid_done1, mid_ready0, \
            mid_ready1 = (S.sem(n) for n in ("h_done", "h_ready", "ln_ready", "ln_turned", "lnT_ready", "y_done",
                                             "mixed_ready", "mid_done0", "mid_done1", "mid_ready0", "mid_ready1"))
        mid_done, mid_ready = [mid_done0, mid_done1], [mid_ready0, mid_ready1]
        norm = Norm(nc, ctx, "x2_norm", hold, const[:, C_POW:C_POW + 1])
        block = S.block()
        mid_ps, h_ps, ln_ps, y_ps = bank[0:2], bank[2], bank[3], bank[4]

        @block.sync
        def _(sp):
            for dst, src in ((w1, weights(A["L1_mix_W1T"])), (w2, weights(A["L1_mix_W2T"])), (b1, A["L1_mix_b1"])):
                sp.dma_start(dst[...], src).then_inc(w_in, 16)
            for n, name in enumerate(("L1_mix_bo", "L1_mix_b2")):
                sp.dma_start(vec[:, n, :], A[name].broadcast_to([P, D])).then_inc(w_in, 16)
            for n, name in enumerate(("L1_mix_ln2_w", "L1_mix_ln2_b")):
                sp.dma_start(col[:, n, :], A[name]).then_inc(w_in, 16)

            def load(i, j):
                g = i * R + j
                once(sp, mixed_ready, g - R + 1, hold)
                sp.dma_start(x_in[:, j, :], rows_of(x2_d, g)).then_inc(loaded[j], 16)
                sp.dma_start(xn_in[:, j, :], rows_of(xn2_d, g)).then_inc(loaded[j], 16)
                sp.dma_start(qT_in[:, j, :], qT_d[bass.ds(g, 1), :, :].rearrange("a p n -> p (a n)"))\
                  .then_inc(loaded[j], 16)

            pipeline(sp, [(0, load)])
            for j in range(R):
                sp.wait_ge(stored[j], 16 * NI)

        @block.gpsimd
        def _(pool):
            def root(i, j):
                norm.root(pool, i * R + j)

            def store(i, j):
                g = i * R + j
                hold(pool, mixed_ready, g + 1)
                pool.dma_start(rows_of(mixed_d, g), mixed[:, j, :]).then_inc(stored[j], 16)

            pipeline(pool, [(0, root), (4, store)])

        @block.vector
        def _(dve):
            dve.wait_ge(w_in, 16 * 7)

            def attend(i, j):
                g = i * R + j
                link = Steps(dve, a_step, g, 2)
                dve.wait_ge(loaded[j], 48 * i + 48)
                link(dve.tensor_tensor(h[:, j, :], xn_in[:, j, :], vec[:, 0, :], ALU.add))
                dve.wait_ge(h_done, g + 1)
                dve.tensor_tensor(h[:, j, :], h_ps[:, 0:D], h[:, j, :], ALU.add).then_inc(h_ready, 1)
                dve.wait_ge(h_ready, g + 1)
                norm.find(dve, h[:, j, :], g)
                norm.apply(dve, ln[:, j, :], h[:, j, :]).then_inc(ln_ready, 1)
                link(dve.tensor_tensor(x_in[:, j, :], x_in[:, j, :], h[:, j, :], ALU.add))
                link.end()

            def residual(i, j):
                g = i * R + j
                link = Steps(dve, c_step, g, 1)
                once(dve, stored[j], 16 * i)
                link(dve.tensor_tensor(mixed[:, j, :], x_in[:, j, :], vec[:, 1, :], ALU.add))
                link.end()
                dve.wait_ge(y_done, g + 1)
                dve.tensor_tensor(mixed[:, j, :], y_ps[:, 0:D], mixed[:, j, :], ALU.add).then_inc(mixed_ready, 1)

            pipeline(dve, [(0, attend), (3, residual)])

        @block.scalar
        def _(act):
            act.wait_ge(w_in, 16 * 7)

            def copy_ln(i, j):
                g = i * R + j
                act.wait_ge(ln_turned, g + 1)
                for k in range(KT):
                    last = act.activation(lnT[:, j, k * P:(k + 1) * P], ln_ps[:, k * P:(k + 1) * P], ACT.Identity,
                                          bias=col[:, 1, k:k + 1], scale=col[:, 0, k:k + 1])
                last.then_inc(lnT_ready, 1)

            def gelu(i, j):
                g = i * R + j
                once(act, y_done, g)
                for half in range(2):
                    act.wait_ge(mid_done[half], g + 1)
                    for f in range(4):
                        n = half * 4 + f
                        last = act.activation(mid[:, n * P:(n + 1) * P], mid_ps[half][:, f * P:(f + 1) * P],
                                              ACT.Gelu, bias=b1[:, n:n + 1])
                    last.then_inc(mid_ready[half], 1)

            pipeline(act, [(1, copy_ln), (2, gelu)])

        @block.tensor
        def _(pe):
            pe.wait_ge(w_in, 16 * 7)

            def attend(i, j):
                g = i * R + j
                pe.wait_ge(loaded[j], 48 * i + 48)
                once(pe, h_ready, g)
                for k in range(KT):
                    last = pe.matmul(h_ps[:, 0:D], qT_in[:, j, k * P:(k + 1) * P], folded[:, k, :],
                                     start=(k == 0), stop=(k == KT - 1))
                last.then_inc(h_done, 1)

            def turn(i, j):
                g = i * R + j
                pe.wait_ge(ln_ready, g + 1)
                once(pe, lnT_ready, g)
                for k in range(KT):
                    last = pe.transpose(ln_ps[:, k * P:(k + 1) * P], ln[:, j, k * P:(k + 1) * P], ident)
                last.then_inc(ln_turned, 1)

            def mlp_in(i, j):
                g = i * R + j
                pe.wait_ge(lnT_ready, g + 1)
                for half in range(2):
                    once(pe, mid_ready[half], g)
                    for f in range(4):
                        n = half * 4 + f
                        for k in range(KT):
                            last = pe.matmul(mid_ps[half][:, f * P:(f + 1) * P], w1[:, k, n * P:(n + 1) * P],
                                             lnT[:, j, k * P:(k + 1) * P], start=(k == 0), stop=(k == KT - 1))
                    last.then_inc(mid_done[half], 1)

            def mlp_out(i, j):
                g = i * R + j
                once(pe, mixed_ready, g)
                for half in range(2):
                    pe.wait_ge(mid_ready[half], g + 1)
                    for f in range(4):
                        n = half * 4 + f
                        last = pe.matmul(y_ps[:, 0:D], mid[:, n * P:(n + 1) * P], w2[:, n, :],
                                         start=(n == 0), stop=(n == FT - 1))
                last.then_inc(y_done, 1)

            pipeline(pe, [(0, attend), (1, turn), (2, mlp_in), (3, mlp_out)])


def second_graph(nc, A, hold, bank, const, acc, xn3T, combine, mixed_d):
    ident = const[:, C_ID:C_ID + P]
    with Stage(nc) as ctx:
        S = Scope(nc, ctx, "g2")
        w, w_r, b2 = S.sb("w", [P, KT, D]), S.sb("w_r", [P, KT, E]), S.sb("b2", [E, D])
        mixed, sums, sumsT, x3, xn3, nT = (S.sb(n, [P, R, D]) for n in ("mixed", "sums", "sumsT", "x3", "xn3", "nT"))
        pr, top, index, pick, fi = (S.sb("pr", [P, E]), S.sb("top", [P, E]), S.sb("index", [P, E], U32),
                                    S.sb("pick", [P, 2, E]), S.sb("fi", [P, E]))
        small, comb, combT = S.sb("small", [P, 4]), S.sb("comb", [P, R, E]), S.sb("combT", [E, R, P])
        w_in, loaded = S.sem("w_in"), S.sems("loaded")
        r_step, c_step, d_step = S.sem("r_step"), S.sem("c_step"), S.sem("d_step")
        sums_ready, sums_turned, sumsT_ready, g_done, x3_ready, xn3_ready, xn3_turned, nT_ready, xn3T_ready, logits, \
            pr_cut, pr_exp, comb_ready, comb_turned, combT_ready, b2_done, rest_ready = (S.sem(n) for n in (
                "sums_ready", "sums_turned", "sumsT_ready", "g_done", "x3_ready", "xn3_ready", "xn3_turned", "nT_ready",
                "xn3T_ready", "logits", "pr_cut", "pr_exp", "comb_ready", "comb_turned", "combT_ready", "b2_done",
                "rest_ready"))
        norm = Norm(nc, ctx, "g2_norm", hold, const[:, C_POW:C_POW + 1])
        block = S.block()
        s_ps, g_ps, n_ps, l_ps, c_ps, b_ps = bank[0], bank[1], bank[2], bank[3], bank[4], bank[5]

        @block.sync
        def _(sp):
            sp.dma_start(w[:, :, :], weights(A["L1_gnn_weight"])).then_inc(w_in, 16)
            sp.dma_start(w_r[:, :, :], weights(A["L1_ffn_router_wT"])).then_inc(w_in, 16)
            sp.dma_start(b2[:, :], A["L1_ffn_b2"]).then_inc(w_in, 16)

            def load(i, j):
                g = i * R + j
                once(sp, x3_ready, g - R + 1, hold)
                sp.dma_start(mixed[:, j, :], rows_of(mixed_d, g)).then_inc(loaded[j], 16)

            pipeline(sp, [(0, load)])

        @block.gpsimd
        def _(pool):
            pipeline(pool, [(0, lambda i, j: norm.root(pool, i * R + j))])

        @block.vector
        def _(dve):
            def cut(i, j):
                g = i * R + j
                once(dve, sums_turned, g - R + 1)
                dve.tensor_copy(sums[:, j, :], tile_of(acc, g)[:, 0:D]).then_inc(sums_ready, 1)

            def residual(i, j):
                g = i * R + j
                dve.wait_ge(loaded[j], 16 * i + 16)
                dve.wait_ge(g_done, g + 1)
                once(dve, rest_ready, g - R + 1)
                dve.scalar_tensor_tensor(out=x3[:, j, :], in0=g_ps[:, 0:D], scalar=0.0, in1=mixed[:, j, :],
                                         op0=ALU.max, op1=ALU.add).then_inc(x3_ready, 1)
                dve.wait_ge(x3_ready, g + 1)
                norm.find(dve, x3[:, j, :], g)
                once(dve, xn3_turned, g - R + 1)
                norm.apply(dve, xn3[:, j, :], x3[:, j, :]).then_inc(xn3_ready, 1)
                dve.wait_ge(xn3_ready, g + 1)
                dve.tensor_tensor(x3[:, j, :], x3[:, j, :], xn3[:, j, :], ALU.add).then_inc(c_step, 1)

            def shift(i, j):
                g = i * R + j
                dve.wait_ge(logits, g + 1)
                dve.tensor_reduce(small[:, 0:1], l_ps[:, 0:E], AX, ALU.max).then_inc(d_step, 1)
                dve.wait_ge(d_step, g + 1)
                dve.tensor_scalar(pr[:, :], l_ps[:, 0:E], small[:, 0:1], None, ALU.subtract).then_inc(pr_cut, 1)

            def route(i, j):
                g = i * R + j
                dve.wait_ge(pr_exp, g + 1)
                dve.wait_ge(pr_cut, g + 1)
                link = Steps(dve, r_step, g, 13)
                link(dve.tensor_reduce(small[:, 0:1], pr[:, :], AX, ALU.add))
                link(dve.reciprocal(small[:, 0:1], small[:, 0:1]))
                for ins in (lambda: dve.tensor_scalar(pr[:, :], pr[:, :], small[:, 0:1], None, ALU.mult),
                            lambda: dve.max(top[:, :], pr[:, :])):
                    ins().then_inc(link.sem, 1)
                    link.k += 1
                    hold(dve, link.sem, link.at())
                link(dve.max_index(index[:, :], top[:, :], pr[:, :]))
                link(dve.tensor_copy(fi[:, :], index[:, :]))
                link(dve.tensor_tensor(small[:, 1:2], top[:, 0:1], top[:, 1:2], ALU.add))
                link(dve.tensor_scalar(small[:, 1:2], small[:, 1:2], 1e-12, None, ALU.max))
                link(dve.reciprocal(small[:, 1:2], small[:, 1:2]))
                link(dve.tensor_scalar(small[:, 2:4], top[:, 0:2], small[:, 1:2], None, ALU.mult))
                for n in range(2):
                    link(dve.tensor_scalar(pick[:, n, :], const[:, C_EXP:C_EXP + E], fi[:, n:n + 1], small[:, 2 + n:3 + n],
                                           ALU.is_equal, ALU.mult))
                once(dve, comb_turned, g - R + 1)
                link(dve.tensor_tensor(comb[:, j, :], pick[:, 0, :], pick[:, 1, :], ALU.add))
                link.end()
                dve.tensor_copy(tile_of(combine, g), comb[:, j, :]).then_inc(comb_ready, 1)

            def rest(i, j):
                g = i * R + j
                dve.wait_ge(b2_done, g + 1)
                dve.wait_ge(c_step, g + 1)
                dve.tensor_tensor(tile_of(acc, g)[:, 0:D], b_ps[:, 0:D], x3[:, j, :], ALU.add).then_inc(rest_ready, 1)

            pipeline(dve, [(0, cut), (1, residual), (3, route), (2, shift), (4, rest)])

        @block.scalar
        def _(act):
            def copy_sums(i, j):
                g = i * R + j
                act.wait_ge(sums_turned, g + 1)
                once(act, g_done, g - R + 1)
                act.activation(sumsT[:, j, :], s_ps[:, 0:D], ACT.Copy).then_inc(sumsT_ready, 1)

            def copy_n(i, j):
                g = i * R + j
                act.wait_ge(xn3_turned, g + 1)
                once(act, logits, g - R + 1)
                act.activation(nT[:, j, :], n_ps[:, 0:D], ACT.Copy).then_inc(nT_ready, 1)
                act.activation(xn3T[:, :, bass.ds(g * P, P)], n_ps[:, 0:D].rearrange("p (k n) -> p k n", k=KT), ACT.Copy)\
                   .then_inc(xn3T_ready, 1)

            def exp(i, j):
                g = i * R + j
                act.wait_ge(pr_cut, g + 1)
                act.activation(pr[:, :], pr[:, :], ACT.Exp).then_inc(pr_exp, 1)

            def copy_comb(i, j):
                g = i * R + j
                act.wait_ge(comb_turned, g + 1)
                once(act, b2_done, g - R + 1)
                act.activation(combT[:, j, :], c_ps[0:E, 0:P], ACT.Copy).then_inc(combT_ready, 1)

            pipeline(act, [(0, copy_sums), (1, copy_n), (2, exp), (3, copy_comb)])

        @block.tensor
        def _(pe):
            pe.wait_ge(w_in, 48)

            def turn_sums(i, j):
                g = i * R + j
                pe.wait_ge(sums_ready, g + 1)
                once(pe, sumsT_ready, g)
                for k in range(KT):
                    last = pe.transpose(s_ps[:, k * P:(k + 1) * P], sums[:, j, k * P:(k + 1) * P], ident)
                last.then_inc(sums_turned, 1)

            def project(i, j):
                g = i * R + j
                pe.wait_ge(sumsT_ready, g + 1)
                once(pe, x3_ready, g)
                for k in range(KT):
                    last = pe.matmul(g_ps[:, 0:D], sumsT[:, j, k * P:(k + 1) * P], w[:, k, :],
                                     start=(k == 0), stop=(k == KT - 1))
                last.then_inc(g_done, 1)

            def turn_n(i, j):
                g = i * R + j
                pe.wait_ge(xn3_ready, g + 1)
                once(pe, xn3T_ready, g)
                for k in range(KT):
                    last = pe.transpose(n_ps[:, k * P:(k + 1) * P], xn3[:, j, k * P:(k + 1) * P], ident)
                last.then_inc(xn3_turned, 1)

            def score(i, j):
                g = i * R + j
                pe.wait_ge(nT_ready, g + 1)
                once(pe, pr_cut, g)
                for k in range(KT):
                    last = pe.matmul(l_ps[:, 0:E], nT[:, j, k * P:(k + 1) * P], w_r[:, k, :],
                                     start=(k == 0), stop=(k == KT - 1))
                last.then_inc(logits, 1)

            def turn_comb(i, j):
                g = i * R + j
                pe.wait_ge(comb_ready, g + 1)
                once(pe, combT_ready, g)
                pe.transpose(c_ps[0:E, 0:P], comb[:, j, :], ident).then_inc(comb_turned, 1)

            def add_b2(i, j):
                g = i * R + j
                pe.wait_ge(combT_ready, g + 1)
                once(pe, rest_ready, g)
                pe.matmul(b_ps[:, 0:D], combT[:, j, :], b2[:, :], start=True, stop=True).then_inc(b2_done, 1)

            pipeline(pe, [(0, turn_sums), (0, project), (1, turn_n), (2, score), (3, turn_comb), (4, add_b2)])


def second_experts(nc, A, hold, bank, const, acc, xn3T, combine, big_k, big_v, out):
    FT = D // P
    with Stage(nc) as ctx:
        S = Scope(nc, ctx, "e2")
        w1 = big_k[:, 0:E * KT * D].rearrange("p (e k n) -> p e k n", e=E, k=KT)
        w2 = big_v[:, :, :].rearrange("p t n -> p (t n)")[:, 0:E * FT * D].rearrange("p (e k n) -> p e k n", e=E, k=FT)
        b1 = S.sb("b1", [P, E, FT])
        mid, sent = S.sb("mid", [P, E, D]), S.sb("sent", [P, 2, D])
        w_in = S.sem("w_in")
        stored = S.sem("stored")
        mid_done, mid_ready, y_done, added, last_ready = (S.sem(n) for n in (
            "mid_done", "mid_ready", "y_done", "added", "last_ready"))
        block = S.block()

        @block.sync
        def _(sp):
            for e in range(E):
                sp.dma_start(w1[:, e, :, :], weights(A["L1_ffn_w1"][e, :, :])).then_inc(w_in, 16)
                sp.dma_start(w2[:, e, :, :], weights(A["L1_ffn_w2"][e, :, :])).then_inc(w_in, 16)
            sp.dma_start(b1[:, :, :], A["L1_ffn_b1"]).then_inc(w_in, 16)
            with sp.Fori(0, T) as g:
                hold(sp, added, (g + 1) * E)
                sp.dma_start(rows_of(out, g), tile_of(acc, g)[:, 0:D]).then_inc(stored, 16)
            sp.wait_ge(stored, 16 * T)

        def gap(e):
            return 2

        @block.tensor
        def _(pe):
            pe.wait_ge(w_in, 16 * (2 * E + 1))

            def expert_in(g, e):
                n = g * E + e
                once(pe, mid_ready, n - 1)
                for f in range(FT):
                    for k in range(KT):
                        last = pe.matmul(bank[e % 2][:, f * P:(f + 1) * P], w1[:, e, k, f * P:(f + 1) * P],
                                         xn3T[:, k, bass.ds(g * P, P)], start=(k == 0), stop=(k == KT - 1))
                last.then_inc(mid_done, 1)

            def expert_out(g, e):
                n = g * E + e
                pe.wait_ge(mid_ready, n + 1)
                once(pe, added, n - 1)
                for f in range(FT):
                    last = pe.matmul(bank[2 + e % 2][:, 0:D], mid[:, e, f * P:(f + 1) * P], w2[:, e, f, :],
                                     start=(f == 0), stop=(f == FT - 1))
                last.then_inc(y_done, 1)

            pipeline(pe, [(0, expert_in), (1, expert_out)], T, E)

        @block.scalar
        def _(act):
            act.wait_ge(w_in, 16 * (2 * E + 1))

            def gelu(g, e):
                n = g * E + e
                act.wait_ge(mid_done, n + 1)
                once(act, y_done, n - E + 1)
                for f in range(FT):
                    last = act.activation(mid[:, e, f * P:(f + 1) * P], bank[e % 2][:, f * P:(f + 1) * P], ACT.Gelu,
                                          bias=b1[:, e, f:f + 1])
                last.then_inc(mid_ready, 1)

            pipeline(act, [(0, gelu)], T, E)

        @block.vector
        def _(dve):
            def add(g, e):
                n = g * E + e
                dve.wait_ge(y_done, n + 1)
                once(dve, added, n)
                to = tile_of(acc, g)[:, 0:D]
                dve.scalar_tensor_tensor(out=to, in0=bank[2 + e % 2][:, 0:D], scalar=tile_of(combine, g)[:, e:e + 1],
                                         in1=to, op0=ALU.mult, op1=ALU.add).then_inc(added, 1)

            pipeline(dve, [(0, add)], T, E)


def laid_out(inputs):

    a = {k: np.asarray(v) for k, v in inputs.items()}

    def rows(x):
        y = np.zeros((NP, x.shape[1]), x.dtype)
        y[:N_NODES] = x[:N_NODES]
        return y

    def edges(x, fill):
        y = np.full((NC * P,), fill, x.dtype)
        y[:N_EDGES] = x
        return y.reshape(NC, P)

    def column(x):
        return np.ascontiguousarray(x.reshape(-1, P).T)

    def four(w):
        y = np.zeros((P, P), w.dtype)
        for n in range(4):
            y[32 * n:32 * n + 32, 32 * n:32 * n + 32] = w
        return y

    const = np.zeros((P, C_N), np.float32)
    const[:, C_ID:C_ID + P] = np.eye(P)
    const[:, C_BD:C_BD + P] = np.kron(np.eye(4), np.ones((32, 32)))
    const[:, C_IOTA:C_IOTA + P] = np.arange(P)
    const[:, C_P] = np.arange(P)
    const[:, C_STEP:C_STEP + SB] = np.arange(P)[:, None] + RB * np.arange(SB)
    const[:, C_TILE:C_TILE + T] = np.arange(T)
    const[:, C_CHUNK:C_CHUNK + NC] = np.arange(NC)
    const[:, C_ONE:C_ONE + P] = 1
    const[:, C_POW] = -0.5
    const[:, C_EXP:C_EXP + 8] = np.arange(8)
    return {
        "const": const,
        "x": rows(a["x"]),
        "sentT": np.ascontiguousarray(rows(a["L0_gnn_sent_repr"]).T),
        "L0_gnn_W_src": a["L0_gnn_W_src"], "L0_gnn_W_dst": a["L0_gnn_W_dst"],
        "L0_gnn_attn_l": a["L0_gnn_attn_l"].reshape(1, D), "L0_gnn_attn_r": a["L0_gnn_attn_r"].reshape(1, D),
        "L0_mix_W_qT": np.ascontiguousarray(a["L0_mix_W_qkv"][:, 0:128].T),
        "L0_mix_W_k": np.ascontiguousarray(a["L0_mix_W_qkv"][:, 128:256]),
        "L0_mix_W_v": np.ascontiguousarray(a["L0_mix_W_qkv"][:, 256:384]),
        "L0_mix_W_out": a["L0_mix_W_out"],
        "L0_gnn_w1": a["L0_gnn_w1"], "L0_gnn_w2": a["L0_gnn_w2"], "L0_gnn_b1": column(a["L0_gnn_b1"]),
        "L0_ffn_Wr": a["L0_ffn_Wr"], "L0_ffn_W1": a["L0_ffn_W1"], "L0_ffn_W2": a["L0_ffn_W2"],
        "L0_ffn_b1": np.ascontiguousarray(a["L0_ffn_b1"].reshape(E, -1, P).transpose(0, 2, 1)),
        "L0_ffn_b2": a["L0_ffn_b2"],
        **{k: a[k].reshape(1, -1) for k in ("L0_gnn_gat_bias", "L0_gnn_b2", "L0_mix_b_out", "L0_ffn_br",
                                            "L0_ffn_gamma", "L0_ffn_beta", "L1_mix_bo", "L1_mix_b2")},
        **{k: column(a[k]) for k in ("L1_mix_ln1_w", "L1_mix_ln1_b", "L1_mix_bx", "L1_mix_b1", "L1_mix_ln2_w",
                                     "L1_mix_ln2_b")},
        **{k + "T": np.ascontiguousarray(a[k].T) for k in ("L1_mix_Wx", "L1_mix_Wo", "L1_mix_W1", "L1_mix_W2",
                                                           "L1_ffn_router_w")},
        **{k + "T4": four(a[k].T) for k in ("L1_mix_Wq", "L1_mix_Wk", "L1_mix_Wv")},
        "L1_gnn_weight": a["L1_gnn_weight"], "L1_ffn_w1": a["L1_ffn_w1"], "L1_ffn_w2": a["L1_ffn_w2"],
        "L1_ffn_b1": np.ascontiguousarray(a["L1_ffn_b1"].reshape(E, -1, P).transpose(2, 0, 1)),
        "L1_ffn_b2": a["L1_ffn_b2"],
        "src": edges(a["src"], 0),
        "dst": edges(a["dst"], PAD_DST),
        "dst_first": np.ascontiguousarray(edges(a["dst"], PAD_DST)[:, 0].reshape(1, NC)),
        "ew": edges(a["edge_weight"], 0),
    }


def kernel(**inputs):
    import concourse.bacc as bacc
    from concourse.bass_utils import run_bass_kernel_spmd

    arrays = laid_out(inputs)
    nc = bacc.Bacc("TRN2", target_bir_lowering=False, num_devices=1)
    A = {k: nc.dram_tensor(f"in_{k}", v.shape, mybir.dt.from_np(v.dtype), kind="ExternalInput").ap()
         for k, v in arrays.items()}
    out = nc.dram_tensor("out", [NP, D], F32, kind="ExternalOutput").ap()
    program(nc, A, out)
    r = run_bass_kernel_spmd(nc, [{f"in_{k}": v for k, v in arrays.items()}], core_ids=[0])
    return r.results[0]["out"][:N_NODES]
```

```python
from contextlib import ExitStack

import numpy as np
import concourse.bass as bass
from concourse import mybir

ALU = mybir.AluOpType
ACT = mybir.ActivationFunctionType
AX = mybir.AxisListType.X
F32 = mybir.dt.float32
BF16 = mybir.dt.bfloat16
I32 = mybir.dt.int32
U32 = mybir.dt.uint32

P = 128
N_NODES = 3125
D = 256
KT = D // P
T = -(-N_NODES // P)
NP = T * P
R = 5
NI = T // R
N_EDGES = 53125
NC = -(-N_EDGES // P)
NS = NC + T - 1
RB = 110
SB = NS // RB
W_AGG = 20
G = 8
H = 4
DH = D // H
DW = DH + 1
DF = 512
HID = 1024
E = 8
PAD_DST = 4095
BIG = 1.0e30
EPS = 1.0e-5
assert T % R == 0 and NS == RB * SB and NS % G == 0

C_ID, C_BD, C_IOTA = 0, 128, 256
C_P, C_STEP, C_TILE, C_CHUNK, C_ONE, C_ZERO = 384, 385, 389, 414, 414 + NC, 414 + NC + P
C_POW = C_ZERO + P
C_ORDER = C_POW + 1
C_N = C_ORDER + E


class Stage(ExitStack):

    def __init__(self, nc):
        super().__init__()
        self.nc, self.semaphores = nc, []

    def semaphore(self, name):
        self.semaphores.append(self.nc.alloc_semaphore(name))
        return self.semaphores[-1]

    def __exit__(self, *failure):
        super().__exit__(*failure)
        self.nc.clear_and_free_semaphores(self.semaphores)
        self.nc.all_engine_barrier()


class Steps:

    def __init__(self, eng, sem, i=None, per=0, base=0):
        self.eng, self.sem, self.i, self.per, self.base, self.k = eng, sem, i, per, base, 0

    def at(self):
        k = self.base + self.k
        return k if self.i is None else self.i * self.per + k

    def __call__(self, ins):
        self.k += 1
        ins.then_inc(self.sem, 1)
        self.eng.wait_ge(self.sem, self.at())

    def end(self):
        assert self.i is None or self.per == self.k, self.k


def pipeline(eng, stages, turns=NI, width=R):
    longest = max(lag for lag, _ in stages)
    first = 1 - (-longest // width)
    for n in range(first * width):
        for lag, stage in stages:
            if n >= lag:
                stage((n - lag) // width, (n - lag) % width)
    with eng.Fori(first, turns) as i:
        for j in range(width):
            for lag, stage in stages:
                stage(i + (j - lag) // width, (j - lag) % width)
    for n in range(turns * width, turns * width + longest):
        for lag, stage in stages:
            if n - lag < turns * width:
                stage((n - lag) // width, (n - lag) % width)


def once(eng, sem, n, hold=None):
    if isinstance(n, int) and n <= 0:
        return
    if hold is None:
        eng.wait_ge(sem, n)
    else:
        hold(eng, sem, n)


def tiles_of(nc, eng, step_tile, n, count):
    return nc.values_load_multi_w_load_instructions(
        step_tile[0:1, bass.ds(n, count)], engines=[eng.engine], min_val=0, max_val=T - 1,
        skip_runtime_bounds_check_because="edge_schedule keeps every tile within 0 and T - 1")[1]


def bank_gap(j, n=2):
    return n if j >= n else R - (R - 1 - j) // n * n


class Norm:

    def __init__(self, nc, ctx, name, hold, power):
        self.power = power
        self.stats = ctx.enter_context(nc.sbuf_tensor(f"{name}_stats", [P, 6], F32))
        self.mv = ctx.enter_context(nc.sbuf_tensor(f"{name}_mv", [P, 2], F32))
        self.rstd = ctx.enter_context(nc.sbuf_tensor(f"{name}_rstd", [P, 1], F32))
        self.found = ctx.semaphore(f"{name}_found")
        self.rooted = ctx.semaphore(f"{name}_rooted")
        self.step = ctx.semaphore(f"{name}_step")
        self.hold = hold

    def find(self, dve, x, n):
        dve.bn_stats(self.stats[:, :], x).then_inc(self.step, 1)
        self.hold(dve, self.step, n * 2 + 1)
        dve.bn_aggr(self.mv[:, :], self.stats[:, :]).then_inc(self.step, 1)
        dve.wait_ge(self.step, n * 2 + 2)
        dve.tensor_scalar(self.mv[:, 1:2], self.mv[:, 1:2], EPS, None, ALU.add).then_inc(self.found, 1)

    def root(self, pool, n):
        self.hold(pool, self.found, n + 1)
        pool.tensor_tensor(self.rstd[:, :], self.mv[:, 1:2], self.power, ALU.pow).then_inc(self.rooted, 1)

    def apply(self, dve, out, x, n):
        dve.wait_ge(self.rooted, n + 1)
        dve.wait_ge(self.found, n + 1)
        return dve.tensor_scalar(out, x, self.mv[:, 0:1], self.rstd[:, 0:1], ALU.subtract, ALU.mult)


def program(nc, A, out):
    with ExitStack() as top:
        def sb(name, shape, dt=F32, ctx=top):
            return ctx.enter_context(nc.sbuf_tensor(name, shape, dt))

        def dram(name, shape, dt=F32):
            return nc.dram_tensor(name, shape, dt, kind="Internal").ap()

        passed = top.enter_context(nc.semaphore("passed"))

        def hold(eng, sem, value):
            eng.wait_ge(sem, value)
            eng.sem_inc(passed, 1)

        bank = [top.enter_context(nc.psum_tensor(f"bank{i}", [P, 512], F32)) for i in range(8)]

        const = sb("const", [P, C_N])
        ident = const[:, C_ID:C_ID + P]
        blocks32 = const[:, C_BD:C_BD + P]
        iota = const[:, C_IOTA:C_IOTA + P]
        pidx = const[:, C_P:C_P + 1]

        step_tile = sb("step_tile", [1, NS], I32)
        src_lane = sb("src_lane", [P, NS + W_AGG], I32)
        dst_lane = sb("dst_lane", [P, NS])
        ew_lane = sb("ew_lane", [P, NS])
        hi_lane = sb("hi_lane", [P, NS])
        acc = sb("acc", [P, T, D + H])
        big_k = sb("big_k", [P, KT * NP])
        big_v = sb("big_v", [P, T, D])
        combine = sb("combine", [P, T, 8])

        src_lo_d = dram("src_lo_d", [NS, P], BF16)
        dst_lo_d = dram("dst_lo_d", [NS, P], BF16)
        feat_d = dram("feat_d", [NP, H * DW])
        xn_d = dram("xn_d", [NP, D])
        xnT_d = dram("xnT_d", [T, P, D])
        x1_d = dram("x1_d", [NP, D])
        xn1_d = dram("xn1_d", [NP, D])
        x2_d = dram("x2_d", [NP, D])
        xn2_d = dram("xn2_d", [NP, D])
        qT_d = dram("qT_d", [T, P, D])
        mixed_d = dram("mixed_d", [NP, D])

        dst_rows = sb("dst_rows", [RB, SB, P])
        edge_schedule(nc, A, dst_rows, bank, const, step_tile, src_lane, dst_lane, ew_lane, hi_lane,
                      src_lo_d, dst_lo_d)
        scores = sb("scores", [P, 2, T, H])
        first_projections(nc, A, hold, bank, const, big_k, big_v, scores, feat_d, xn_d, xnT_d)
        fold = sb("fold", [P, KT, D])
        first_mixer(nc, A, hold, bank, const, big_k, big_v, fold)
        with ExitStack() as held:
            weight = sb("edge_exp", [P, NS, H], ctx=held)
            with ExitStack() as brief:
                el_er = sb("el_er", [P, 2, NS, H], ctx=brief)
                er = sb("er", [P, NS, H], ctx=brief)
                edge_lookup(nc, A, hold, bank, const, scores, el_er, er, hi_lane, step_tile, src_lo_d, dst_lo_d)
                segment_maximum(nc, bank, const, dst_rows, el_er)
                edge_exp(nc, el_er, er, weight)
            aggregate(nc, A, hold, "a0", bank, const, acc, step_tile, src_lane, dst_lane, feat_d, weight, None)
        with ExitStack() as held:
            xnT = sb("xn1T", [P, KT, NP], ctx=held)
            first_graph_mlp(nc, A, hold, bank, const, acc, fold, xnT, A["x"], xn_d, xnT_d, x1_d, xn1_d)
            w1 = sb("top_w1", [P, 2, KT, DF], ctx=held)
            w2 = sb("top_w2", [P, 2, DF // P, D], ctx=held)
            b1 = sb("top_b1", [P, 2, DF // P], ctx=held)
            bias = sb("top_bias", [P, D], ctx=held)
            first_router(nc, A, hold, bank, const, xnT, w1, w2, b1, bias)
            first_experts(nc, A, hold, bank, const, xnT, w1, w2, b1, bias, big_k, big_v,
                          x1_d, xn1_d, x2_d, xn2_d, qT_d)
        folded = sb("folded", [P, KT, D])
        second_mixer(nc, A, hold, bank, const, big_k, big_v, folded)
        mixer_mlp(nc, A, hold, bank, const, folded, x2_d, xn2_d, qT_d, mixed_d)
        aggregate(nc, A, hold, "a1", bank, const, acc, step_tile, src_lane, dst_lane, xn2_d, None, ew_lane)
        with ExitStack() as held:
            xnT = sb("xn3T", [P, KT, NP], ctx=held)
            second_graph(nc, A, hold, bank, const, acc, xnT, combine, mixed_d, big_k, big_v)
            second_experts(nc, A, hold, bank, const, acc, xnT, combine, big_k, big_v, out)


def edge_schedule(nc, A, rows, bank, const, step_tile, src_lane, dst_lane, ew_lane, hi_lane, src_lo_d, dst_lo_d):
    with Stage(nc) as ctx:
        def sb(name, shape, dt=F32):
            return ctx.enter_context(nc.sbuf_tensor(name, shape, dt))

        def sem(name):
            return ctx.semaphore(name)

        first = sb("es_first", [1, NC], I32)
        first_t = sb("es_first_t", [1, NC], I32)
        key = sb("es_key", [1, NC])
        below = sb("es_below", [RB, NC])
        count = sb("es_count", [RB, SB])
        chunk = sb("es_chunk", [RB, SB], I32)
        tile_f = sb("es_tile_f", [RB, SB])
        base = sb("es_base", [RB, SB])
        src_i = sb("es_src_i", [RB, SB, P], I32)
        dst_i = sb("es_dst_i", [RB, SB, P], I32)
        ew_r = sb("es_ew_r", [RB, SB, P])
        hi_i = sb("es_hi_i", [RB, SB, P], I32)
        lo_i = sb("es_lo_i", [RB, SB, P], I32)
        src_f = sb("es_src_f", [RB, SB, P])
        hi_f = sb("es_hi_f", [RB, SB, P])
        local = sb("es_local", [RB, SB, P])
        lo_b = sb("es_lo_b", [RB, SB, P], BF16)
        loc_b = sb("es_loc_b", [RB, SB, P], BF16)

        const_in, first_in = sem("es_const_in"), sem("es_first_in")
        dve_step, key_ready, key_spread = sem("es_dve_step"), sem("es_key_ready"), sem("es_key_spread")
        chunk_ready, tile_ready, tile_row = sem("es_chunk_ready"), sem("es_tile_ready"), sem("es_tile_row")
        rows_in = [sem(f"es_rows_in{k}") for k in range(3)]
        rows_ready, lanes_ready, stored, lo_ready = (sem("es_rows_ready"), sem("es_lanes_ready"),
                                                     sem("es_stored"), sem("es_lo_ready"))
        block = ctx.enter_context(nc.Block())

        @block.sync
        def _(sp):
            sp.dma_start(const[:, :], A["const"]).then_inc(const_in, 16)
            sp.dma_start(first[:, :], A["dst_first"]).then_inc(first_in, 16)
            sp.wait_ge(lo_ready, 1)
            sp.dma_start(src_lo_d.rearrange("(b p) l -> p b l", b=SB), lo_b[:, :, :]).then_inc(stored, 16)
            sp.dma_start(dst_lo_d.rearrange("(b p) l -> p b l", b=SB), loc_b[:, :, :]).then_inc(stored, 16)
            sp.wait_ge(stored, 32)

        @block.gpsimd
        def _(pool):
            pool.wait_ge(chunk_ready, 1)
            for b in range(SB):
                at = bass.IndirectOffsetOnAxis(ap=chunk[:, b:b + 1], axis=0)
                for k, (dst, src) in enumerate(((dst_i, A["dst"]), (src_i, A["src"]), (ew_r, A["ew"]))):
                    pool.indirect_dma_start(dst[:, b, :], None, src, at).then_inc(rows_in[k], 16)

        @block.vector
        def _(dve):
            link = Steps(dve, dve_step)
            dve.wait_ge(const_in, 16)
            dve.wait_ge(first_in, 16)
            link(dve.tensor_single_scalar(first_t[:, :], first[:, :], 7, ALU.arith_shift_right))
            link(dve.tensor_copy(key[:, :], first_t[:, :]))
            dve.tensor_tensor(key[:, :], key[:, :], const[0:1, C_CHUNK:C_CHUNK + NC], ALU.add).then_inc(key_ready, 1)
            dve.wait_ge(key_spread, 1)
            for b in range(SB):
                link(dve.tensor_scalar(below[:, 1:NC], bank[0][0:RB, 1:NC], const[0:RB, C_STEP + b:C_STEP + b + 1],
                                       None, ALU.is_le))
                link(dve.tensor_reduce(count[:, b:b + 1], below[:, 1:NC], AX, ALU.add))
            dve.tensor_copy(chunk[:, :], count[:, :]).then_inc(chunk_ready, 1)
            dve.tensor_tensor(tile_f[:, :], const[0:RB, C_STEP:C_STEP + SB], count[:, :], ALU.subtract)\
               .then_inc(tile_ready, 1)
            dve.wait_ge(tile_ready, 1)
            link(dve.tensor_scalar(base[:, :], tile_f[:, :], float(P), None, ALU.mult))
            dve.wait_ge(tile_row, 1)
            link(dve.tensor_scalar(step_tile[:, :], bank[1][0:1, 0:NS], 0.0, float(T - 1), ALU.max, ALU.min))
            dve.wait_ge(rows_in[0], 16 * SB)
            link(dve.tensor_copy(rows[:, :, :], dst_i[:, :, :]))
            link(dve.tensor_tensor(local[:, :, :], rows[:, :, :],
                                   base[:, :].unsqueeze(2).broadcast_to([RB, SB, P]), ALU.subtract))
            link(dve.tensor_copy(loc_b[:, :, :], local[:, :, :]))
            dve.wait_ge(rows_in[1], 16 * SB)
            link(dve.tensor_copy(src_f[:, :, :], src_i[:, :, :]))
            link(dve.tensor_single_scalar(hi_i[:, :, :], src_i[:, :, :], 7, ALU.arith_shift_right))
            link(dve.tensor_single_scalar(lo_i[:, :, :], src_i[:, :, :], P - 1, ALU.bitwise_and))
            dve.tensor_copy(lo_b[:, :, :], lo_i[:, :, :]).then_inc(lo_ready, 1)
            dve.tensor_copy(hi_f[:, :, :], hi_i[:, :, :]).then_inc(rows_ready, 1)
            dve.wait_ge(lanes_ready, 4)
            for b, dst in ((2, src_lane), (3, dst_lane), (4, ew_lane), (5, hi_lane)):
                link(dve.tensor_copy(dst[:, 0:NS], bank[b][:, 0:NS]))
            link(dve.memset(src_lane[:, NS:NS + W_AGG], 0))

        @block.tensor
        def _(pe):
            pe.wait_ge(const_in, 16)
            pe.wait_ge(key_ready, 1)
            pe.matmul(bank[0][:, 0:NC], const[0:1, C_ONE:C_ONE + P], key[:, :], start=True, stop=True)\
              .then_inc(key_spread, 1)
            pe.wait_ge(tile_ready, 1)
            for b in range(SB):
                last = pe.matmul(bank[1][0:1, b * RB:(b + 1) * RB], tile_f[:, b:b + 1], const[0:RB, C_ID:C_ID + RB],
                                 start=True, stop=True)
            last.then_inc(tile_row, 1)
            pe.wait_ge(rows_in[2], 16 * SB)
            pe.wait_ge(rows_ready, 1)
            for n, src in ((2, src_f), (3, local), (4, ew_r), (5, hi_f)):
                for b in range(SB):
                    last = pe.transpose(bank[n][:, b * RB:(b + 1) * RB], src[:, b, :], const[0:RB, C_ID:C_ID + RB])
                last.then_inc(lanes_ready, 1)


def first_projections(nc, A, hold, bank, const, big_k, big_v, scores, feat_d, xn_d, xnT_d):
    ident = const[:, C_ID:C_ID + P]
    HD = 128
    with Stage(nc) as ctx:
        def sb(name, shape, dt=F32):
            return ctx.enter_context(nc.sbuf_tensor(name, shape, dt))

        def sem(name):
            return ctx.semaphore(name)

        w_feat = sb("p1_w_feat", [P, KT, D + H])
        w_v = sb("p1_w_v", [P, KT, HD + H])
        w_k = sb("p1_w_k", [P, KT, HD])
        w_dst = sb("p1_w_dst", [P, KT, D])
        attn = sb("p1_attn", [P, 2, D])
        prod = sb("p1_prod", [P, KT, D])
        x_in = sb("p1_x_in", [P, R, D])
        sent_in = sb("p1_sent_in", [P, R, KT, P])
        xn = sb("p1_xn", [P, R, D])
        xnT = sb("p1_xnT", [P, R, D])
        feat = sb("p1_feat", [P, R, H * DW])
        norm = Norm(nc, ctx, "p1_norm", hold, const[:, C_POW:C_POW + 1])
        turned_ps, feat_ps, v_ps, k_ps = ([bank[2 * n], bank[2 * n + 1]] for n in range(4))

        w_in, wd, w_ready = sem("p1_w_in"), sem("p1_wd"), sem("p1_w_ready")
        x_loaded = [sem(f"p1_x_loaded{j}") for j in range(R)]
        sent_loaded = [sem(f"p1_sent_loaded{j}") for j in range(R)]
        xn_stored = [sem(f"p1_xn_stored{j}") for j in range(R)]
        xnT_stored = [sem(f"p1_xnT_stored{j}") for j in range(R)]
        feat_stored = [sem(f"p1_feat_stored{j}") for j in range(R)]
        xn_ready = sem("p1_xn_ready")
        turned, turned_sb = sem("p1_turned"), sem("p1_turned_sb")
        feat_done, feat_sb = sem("p1_feat_done"), sem("p1_feat_sb")
        el_sb = sem("p1_el_sb")
        v_done, k_done = sem("p1_v_done"), sem("p1_k_done")
        v_sb, k_sb = sem("p1_v_sb"), sem("p1_k_sb")
        block = ctx.enter_context(nc.Block())

        def before(j):
            return 1 if j == 0 else 2

        @block.sync
        def _(sp):
            sp.dma_start(w_feat[:, :, 0:D], A["L0_gnn_W_src"].rearrange("(k p) n -> p k n", p=P)).then_inc(w_in, 16)
            sp.dma_start(w_dst[:, :, :], A["L0_gnn_W_dst"].rearrange("(k p) n -> p k n", p=P)).then_inc(w_in, 16)
            sp.dma_start(w_k[:, :, :], A["L0_mix_W_k"].rearrange("(k p) n -> p k n", p=P)).then_inc(w_in, 16)
            sp.dma_start(w_v[:, :, 0:HD], A["L0_mix_W_v"].rearrange("(k p) n -> p k n", p=P)).then_inc(w_in, 16)
            sp.dma_start(attn[:, 0, :], A["L0_gnn_attn_l"].broadcast_to([P, D])).then_inc(w_in, 16)
            sp.dma_start(attn[:, 1, :], A["L0_gnn_attn_r"].broadcast_to([P, D])).then_inc(w_in, 16)
            with sp.Fori(0, NI) as i:
                for j in range(R):
                    g = i * R + j
                    hold(sp, xn_ready, g + 1)
                    sp.dma_start(x_in[:, j, :], A["x"][bass.ds(g * P, P), :]).then_inc(x_loaded[j], 16)
                    hold(sp, feat_done, g + 1)
                    sp.dma_start(sent_in[:, j, :, :],
                                 A["sentT"][:, bass.ds(g * P, P)].rearrange("(k p) n -> p k n", p=P))\
                      .then_inc(sent_loaded[j], 16)
            for j in range(R):
                sp.wait_ge(xn_stored[j], 16 * NI)
                sp.wait_ge(xnT_stored[j], 16 * NI)
                sp.wait_ge(feat_stored[j], 16 * NI)

        @block.gpsimd
        def _(pool):
            with pool.Fori(0, NI) as i:
                for j in range(R):
                    g = i * R + j
                    norm.root(pool, g)
                    hold(pool, xn_ready, R + g + 1)
                    pool.dma_start(xn_d[bass.ds(g * P, P), :], xn[:, j, :]).then_inc(xn_stored[j], 16)

        @block.scalar
        def _(act):
            act.sem_inc(turned_sb, 2)
            act.sem_inc(feat_sb, 2)
            act.sem_inc(k_sb, 2)
            with act.Fori(0, NI) as i:
                for j in range(R):
                    g = i * R + j
                    act.wait_ge(turned, g + 1)
                    act.wait_ge(k_done, g + 1)
                    act.wait_ge(xnT_stored[j], i * 16)
                    act.activation(xnT[:, j, :], turned_ps[j % 2][:, 0:D], ACT.Copy).then_inc(turned_sb, 1)
                    act.wait_ge(feat_done, R + g + 1)
                    act.wait_ge(feat_stored[j], i * 16)
                    act.activation(feat[:, j, :].rearrange("p (h d) -> p h d", h=H)[:, :, 0:DH],
                                   feat_ps[j % 2][:, 0:D].rearrange("p (h d) -> p h d", h=H), ACT.Copy).then_inc(el_sb, 1)
                    act.activation(scores[:, 0, bass.ds(g, 1), :].rearrange("p a h -> p (a h)"),
                                   feat_ps[j % 2][:, D:D + H], ACT.Copy).then_inc(feat_sb, 1)
                    act.wait_ge(turned_sb, 2 + g + 1)
                    act.dma_start(xnT_d[bass.ds(g, 1), :, :].rearrange("a p n -> p (a n)"), xnT[:, j, :])\
                       .then_inc(xnT_stored[j], 16)
                    act.wait_ge(el_sb, g + 1)
                    act.dma_start(feat_d[bass.ds(g * P, P), :], feat[:, j, :]).then_inc(feat_stored[j], 16)
                    act.wait_ge(k_done, R + g + 1)
                    act.activation(big_k[:, bass.ds(g * P, P)], k_ps[j % 2][:, 0:P], ACT.Copy).then_inc(k_sb, 1)

        @block.vector
        def _(dve):
            dve.sem_inc(xn_ready, R)
            dve.sem_inc(v_sb, 2)
            link = Steps(dve, wd)
            dve.wait_ge(w_in, 96)
            for w, side in ((w_feat[:, :, 0:D], 0), (w_dst[:, :, :], 1)):
                link(dve.tensor_tensor(prod[:, :, :], w, attn[:, side:side + 1, :].broadcast_to([P, KT, D]), ALU.mult))
                to = (w_feat[:, :, D:D + H], w_v[:, :, HD:HD + H])[side]
                link(dve.tensor_reduce(to, prod[:, :, :].rearrange("p k (h d) -> p k h d", h=H), AX, ALU.add))
            link(dve.memset(feat[:, :, :], 1.0))
            dve.engine_nop().then_inc(w_ready, 1)
            with dve.Fori(0, NI) as i:
                for j in range(R):
                    g = i * R + j
                    dve.wait_ge(x_loaded[j], i * 16 + 16)
                    dve.wait_ge(k_done, g + 1)
                    dve.wait_ge(xn_stored[j], i * 16)
                    norm.find(dve, x_in[:, j, :], g)
                    norm.apply(dve, xn[:, j, :], x_in[:, j, :], g).then_inc(xn_ready, 1)
                    dve.wait_ge(v_done, g + 1)
                    dve.tensor_copy(big_v[:, bass.ds(g, 1), 0:HD + H].rearrange("p a n -> p (a n)"),
                                    v_ps[j % 2][:, 0:HD + H]).then_inc(v_sb, 1)
            dve.wait_ge(v_sb, 2 + T)
            dve.tensor_copy(scores[:, 1, :, :], big_v[:, :, HD:HD + H]).then_inc(wd, 1)
            dve.wait_ge(wd, 6)

        @block.tensor
        def _(pe):
            pe.sem_inc(feat_done, R)
            pe.sem_inc(k_done, R)
            pe.wait_ge(w_ready, 1)
            with pe.Fori(0, NI) as i:
                for j in range(R):
                    g = i * R + j
                    pe.wait_ge(xn_ready, R + g + 1)
                    pe.wait_ge(turned_sb, 2 + g + 1 - before(j))
                    for k in range(KT):
                        last = pe.transpose(turned_ps[j % 2][:, k * P:(k + 1) * P], xn[:, j, k * P:(k + 1) * P], ident)
                    last.then_inc(turned, 1)
                    pe.wait_ge(sent_loaded[j], i * 16 + 16)
                    pe.wait_ge(feat_sb, 2 + g + 1 - before(j))
                    for k in range(KT):
                        last = pe.matmul(feat_ps[j % 2][:, 0:D + H], sent_in[:, j, k, :], w_feat[:, k, :],
                                         start=(k == 0), stop=(k == KT - 1))
                    last.then_inc(feat_done, 1)
                    pe.wait_ge(turned_sb, 2 + g + 1)
                    pe.wait_ge(v_sb, 2 + g + 1 - before(j))
                    for k in range(KT):
                        last = pe.matmul(v_ps[j % 2][:, 0:HD + H], xnT[:, j, k * P:(k + 1) * P], w_v[:, k, :],
                                         start=(k == 0), stop=(k == KT - 1))
                    last.then_inc(v_done, 1)
                    pe.wait_ge(k_sb, 2 + g + 1 - before(j))
                    for k in range(KT):
                        last = pe.matmul(k_ps[j % 2][:, 0:P], w_k[:, k, :], xnT[:, j, k * P:(k + 1) * P],
                                         start=(k == 0), stop=(k == KT - 1))
                    last.then_inc(k_done, 1)


def first_mixer(nc, A, hold, bank, const, big_k, big_v, fold):
    ident = const[:, C_ID:C_ID + P]
    with Stage(nc) as ctx:
        def sb(name, shape, dt=F32):
            return ctx.enter_context(nc.sbuf_tensor(name, shape, dt))

        def sem(name):
            return ctx.semaphore(name)

        w_qT = sb("m1_w_qT", [P, D])
        w_out = sb("m1_w_out", [P, D])
        peak = sb("m1_peak", [P, 1])
        total = sb("m1_total", [P, 1])
        ekT = sb("m1_ekT", [P, R, P])
        ek = sb("m1_ek", [P, R, P])
        ctx_sb = sb("m1_ctx", [P, P])
        ctxT = sb("m1_ctxT", [P, P])
        through = sb("m1_through", [P, D])
        w_in, dve_step, peak_ready, exp_ready = (sem("m1_w_in"), sem("m1_dve_step"), sem("m1_peak_ready"),
                                                 sem("m1_exp_ready"))
        turned, turned_sb = sem("m1_turned"), sem("m1_turned_sb")
        cut = sem("m1_cut")
        summed = sem("m1_summed")
        pe_step, done = sem("m1_pe_step"), sem("m1_done")
        block = ctx.enter_context(nc.Block())

        @block.sync
        def _(sp):
            sp.dma_start(w_qT[:, :], A["L0_mix_W_qT"]).then_inc(w_in, 16)
            sp.dma_start(w_out[:, :], A["L0_mix_W_out"]).then_inc(w_in, 16)

        @block.vector
        def _(dve):
            link = Steps(dve, dve_step)
            link(dve.tensor_reduce(peak[:, :], big_k[:, 0:N_NODES], AX, ALU.max))
            dve.tensor_scalar(peak[:, :], peak[:, :], -1.0, None, ALU.mult).then_inc(peak_ready, 1)
            dve.wait_ge(exp_ready, 1)
            link(dve.reciprocal(total[:, :], total[:, :]))
            link(dve.tensor_scalar(total[:, :], total[:, :], 32.0 ** -0.5, None, ALU.mult))
            with dve.Fori(0, NI) as i:
                for j in range(R):
                    g = i * R + j
                    dve.wait_ge(summed, g + 1)
                    dve.tensor_copy(ekT[:, j, :], big_k[:, bass.ds(g * P, P)]).then_inc(cut, 1)
            dve.wait_ge(pe_step, 1)
            dve.tensor_tensor(ctx_sb[:, :], bank[7][:, 0:P], const[:, C_BD:C_BD + P], ALU.mult).then_inc(done, 1)
            dve.wait_ge(pe_step, 2)
            dve.tensor_copy(ctxT[:, :], bank[2][:, 0:P]).then_inc(done, 1)
            dve.wait_ge(pe_step, 3)
            dve.tensor_scalar(through[:, :], bank[3][:, 0:D], total[:, 0:1], None, ALU.mult).then_inc(done, 1)
            dve.wait_ge(pe_step, 4)
            dve.tensor_copy(fold[:, :, :].rearrange("p k n -> p (k n)"), bank[4][:, :]).then_inc(done, 1)
            dve.wait_ge(done, 4)

        @block.scalar
        def _(act):
            act.sem_inc(turned_sb, 2)
            act.wait_ge(peak_ready, 1)
            act.activation(big_k[:, 0:N_NODES], big_k[:, 0:N_NODES], ACT.Exp, bias=peak[:, :],
                           accum_out=total[:, :]).then_inc(exp_ready, 1)
            with act.Fori(0, NI) as i:
                for j in range(R):
                    g = i * R + j
                    act.wait_ge(turned, g + 1)
                    act.wait_ge(summed, g + 1)
                    act.activation(ek[:, j, :], bank[j % 2][:, 0:P], ACT.Copy).then_inc(turned_sb, 1)

        @block.tensor
        def _(pe):
            pe.sem_inc(summed, R)
            pe.wait_ge(exp_ready, 1)
            pe.matmul(bank[7][:, 0:P], const[:, C_ZERO:C_ZERO + P], ident, start=True, stop=False)
            with pe.Fori(0, NI) as i:
                for j in range(R):
                    g = i * R + j
                    pe.wait_ge(turned_sb, 2 + g + 1 - (1 if j == 0 else 2))
                    pe.wait_ge(cut, g + 1)
                    pe.transpose(bank[j % 2][:, 0:P], ekT[:, j, :], ident).then_inc(turned, 1)
                    pe.wait_ge(turned_sb, 2 + g + 1)
                    pe.matmul(bank[7][:, 0:P], ek[:, j, :],
                              big_v[:, bass.ds(g, 1), 0:P].rearrange("p a n -> p (a n)"),
                              start=False, stop=False).then_inc(summed, 1)
            pe.matmul(bank[7][:, 0:P], const[:, C_ZERO:C_ZERO + P], ident, start=False, stop=True).then_inc(pe_step, 1)
            pe.wait_ge(done, 1)
            pe.transpose(bank[2][:, 0:P], ctx_sb[:, :], ident).then_inc(pe_step, 1)
            pe.wait_ge(w_in, 32)
            pe.wait_ge(done, 2)
            pe.matmul(bank[3][:, 0:D], ctxT[:, :], w_out[:, :], start=True, stop=True).then_inc(pe_step, 1)
            pe.wait_ge(done, 3)
            for k in range(KT):
                last = pe.matmul(bank[4][:, k * D:(k + 1) * D], w_qT[:, k * P:(k + 1) * P], through[:, :],
                                 start=True, stop=True)
            last.then_inc(pe_step, 1)


def edge_lookup(nc, A, hold, bank, const, scores, el_er, er, hi_lane, step_tile, src_lo_d, dst_lo_d):
    U = 4
    TURNS = NS // U // R
    EL = U * H * T
    with Stage(nc) as ctx:
        S = Scope(nc, ctx, "ew")
        part_el, part_er, rest = (S.sb("part_el", [P, 3, H, T], BF16), S.sb("part_er", [P, 3, T, H], BF16),
                                  S.sb("rest", [P, T, H]))
        src_bc, dst_bc, src_hot, dst_hot = (S.sb(n, [P, R, U * P], BF16) for n in ("src_bc", "dst_bc", "src_hot", "dst_hot"))
        hi_hot, picked = S.sb("hi_hot", [P, R, U, T]), S.sb("picked", [P, R, U, H, T])
        split, parts_ready, loaded = S.sem("split"), S.sem("parts_ready"), S.sems("loaded")
        hot_ready, looked_up, was_picked, el_taken, er_taken = (S.sem(n) for n in (
            "hot_ready", "looked_up", "was_picked", "el_taken", "er_taken"))
        block = S.block()

        @block.sync
        def _(sp):
            def load(i, j):
                q = i * R + j
                once(sp, hot_ready, q - R + 1, hold)
                for bc, lo in ((src_bc, src_lo_d), (dst_bc, dst_lo_d)):
                    row = lo[bass.ds(q * U, U), :].rearrange("s l -> (s l)").partition_broadcast(P)
                    sp.dma_start(bc[:, j, :], row).then_inc(loaded[j], 16)

            pipeline(sp, [(0, load)], TURNS)

        @block.vector
        def _(dve):
            link = Steps(dve, split)
            for side, part in ((0, part_el[:, :, :, :].rearrange("p n h t -> p n t h")), (1, part_er[:, :, :, :])):
                link(dve.tensor_copy(rest[:, :, :], scores[:, side, :, :]))
                for n in range(3):
                    link(dve.tensor_copy(part[:, n], rest[:, :, :]))
                    if n < 2:
                        link(dve.tensor_tensor(rest[:, :, :], rest[:, :, :], part[:, n], ALU.subtract))
            dve.engine_nop().then_inc(parts_ready, 1)

            def compare(i, j):
                q = i * R + j
                dve.wait_ge(loaded[j], 32 * i + 32)
                once(dve, looked_up, q - R + 1)
                once(dve, was_picked, q - R + 1)
                dve.tensor_scalar(src_hot[:, j, :], src_bc[:, j, :], const[:, C_P:C_P + 1], None, ALU.is_equal)
                dve.tensor_scalar(dst_hot[:, j, :], dst_bc[:, j, :], const[:, C_P:C_P + 1], None, ALU.is_equal)
                dve.tensor_tensor(hi_hot[:, j, :, :], const[:, C_TILE:C_TILE + T].unsqueeze(1).broadcast_to([P, U, T]),
                                  hi_lane[:, bass.ds(q * U, U)].unsqueeze(2).broadcast_to([P, U, T]),
                                  ALU.is_equal).then_inc(hot_ready, 1)

            def pick(i, j):
                q = i * R + j
                dve.wait_ge(looked_up, q + 1)
                dve.wait_ge(hot_ready, q + 1)
                once(dve, el_taken, q - R + 1)
                dve.tensor_tensor(picked[:, j, :, :, :], bank[j][:, 0:EL].rearrange("p (s h t) -> p s h t", s=U, h=H),
                                  hi_hot[:, j, :, :].unsqueeze(2).broadcast_to([P, U, H, T]), ALU.mult).then_inc(was_picked, 1)

            def add(i, j):
                q = i * R + j
                dve.wait_ge(was_picked, q + 1)
                dve.tensor_reduce(el_er[:, 0, bass.ds(q * U, U), :], picked[:, j, :, :, :], AX, ALU.add).then_inc(el_taken, 1)

            pipeline(dve, [(0, compare), (3, add), (2, pick)], TURNS)

        @block.scalar
        def _(act):
            def take(i, j):
                q = i * R + j
                act.wait_ge(looked_up, q + 1)
                act.wait_ge(was_picked, q + 1)
                act.activation(er[:, bass.ds(q * U, U), :], bank[j][:, EL:EL + U * H].rearrange("p (s h) -> p s h", s=U),
                               ACT.Copy).then_inc(er_taken, 1)

            pipeline(act, [(0, take)], TURNS)

        @block.tensor
        def _(pe):
            pe.wait_ge(parts_ready, 1)

            tiles = []

            def look_up(i, j):
                q = i * R + j
                if j == 0:
                    tiles[:] = tiles_of(nc, pe, step_tile, q * U, R * U)
                pe.wait_ge(hot_ready, q + 1)
                once(pe, er_taken, q - R + 1)
                for s in range(U):
                    for n in range(3):
                        pe.matmul(bank[j][:, s * H * T:(s + 1) * H * T], src_hot[:, j, s * P:(s + 1) * P],
                                  part_el[:, n, :, :].rearrange("p h t -> p (h t)"), start=(n == 0), stop=(n == 2))
                for s in range(U):
                    for n in range(3):
                        last = pe.matmul(bank[j][:, EL + s * H:EL + (s + 1) * H], dst_hot[:, j, s * P:(s + 1) * P],
                                         part_er[:, n, bass.ds(tiles[j * U + s], 1), :].rearrange("p a h -> p (a h)"),
                                         start=(n == 0), stop=(n == 2))
                last.then_inc(looked_up, 1)

            pipeline(pe, [(0, look_up)], TURNS)


def edge_exp(nc, el_er, er, weight):
    with Stage(nc) as last_ctx:
        def sem2(name):
            return last_ctx.semaphore(name)

        step, diff_ready, exp_ready = sem2("ee_step"), sem2("ee_diff_ready"), sem2("ee_exp_ready")
        leaky = last_ctx.enter_context(nc.sbuf_tensor("ee_leaky", [P, 2, NS, H], F32))
        block = last_ctx.enter_context(nc.Block())

        @block.vector
        def _(dve):
            link = Steps(dve, step)
            link(dve.tensor_tensor(el_er[:, :, :, :], el_er[:, :, :, :],
                                   er[:, :, :].unsqueeze(1).broadcast_to([P, 2, NS, H]), ALU.add))
            link(dve.scalar_tensor_tensor(out=leaky[:, :, :, :], in0=el_er[:, :, :, :], scalar=0.2,
                                          in1=el_er[:, :, :, :], op0=ALU.mult, op1=ALU.max))
            dve.tensor_tensor(weight[:, :, :], leaky[:, 0], leaky[:, 1], ALU.subtract).then_inc(diff_ready, 1)

        @block.scalar
        def _(act):
            act.wait_ge(diff_ready, 1)
            flat = weight[:, :, :].rearrange("p s h -> p (s h)")
            act.activation(flat, flat, ACT.Exp).then_inc(exp_ready, 1)
            act.wait_ge(exp_ready, 1)


def segment_maximum(nc, bank, const, dst_rows, el_er):
    with Stage(nc) as inner:
        def sb(name, shape, dt=F32):
            return inner.enter_context(nc.sbuf_tensor(name, shape, dt))

        def sem(name):
            return inner.semaphore(name)

        value = sb("sm_value", [RB, SB, H, P])
        change = sb("sm_change", [RB, SB, H, P])
        best = sb("sm_best", [RB, SB, H, P])
        ends = sb("sm_ends", [RB, 2, SB, H])
        peaks = sb("sm_peaks", [RB, 2, SB, H])
        end_row = sb("sm_end_row", [H, 2, NS])
        peak_row = sb("sm_peak_row", [H, 2, NS])
        linked = sb("sm_linked", [H, NS + 1])
        whole = sb("sm_whole", [H, NS])
        decay = sb("sm_decay", [H, NS])
        carried = sb("sm_carried", [H, 2, NS + 1])
        carry_row = sb("sm_carry_row", [H, 2, NS])
        carry = sb("sm_carry", [RB, 2, SB, H])
        same = sb("sm_same", [RB, SB, P])
        offer = sb("sm_offer", [RB, SB, H, P])
        step, pe_step, taken = sem("sm_step"), sem("sm_pe_step"), sem("sm_taken")
        block = inner.enter_context(nc.Block())
        ID = const[0:RB, C_ID:C_ID + RB]

        @block.tensor
        def _(pe):
            for b in range(SB):
                for h in range(H):
                    last = pe.transpose(bank[b][0:RB, h * P:(h + 1) * P],
                                        el_er[:, 0, b * RB:(b + 1) * RB, h], const[:, C_ID:C_ID + P])
                last.then_inc(pe_step, 1)
            pe.wait_ge(taken, 1)
            for n, src in enumerate((ends, peaks)):
                for side in range(2):
                    for b in range(SB):
                        last = pe.transpose(bank[4 + 2 * n + side][0:H, b * RB:(b + 1) * RB], src[:, side, b, :], ID)
            last.then_inc(pe_step, 1)
            pe.wait_ge(taken, 2)
            for side in range(2):
                for b in range(SB):
                    last = pe.transpose(bank[side][0:RB, b * H:(b + 1) * H],
                                        carry_row[:, side, b * RB:(b + 1) * RB], const[0:H, C_ID:C_ID + H])
            last.then_inc(pe_step, 1)
            pe.wait_ge(taken, 3)
            for h in range(H):
                for b in range(SB):
                    last = pe.transpose(bank[4 + h][:, b * RB:(b + 1) * RB], best[:, b, h, :], ID)
            last.then_inc(pe_step, 1)

        @block.vector
        def _(dve):
            link = Steps(dve, step)
            link(dve.memset(change[:, :, :, 0:1], -BIG))
            differ = dve.tensor_tensor(same[:, :, 1:P], dst_rows[:, :, 1:P], dst_rows[:, :, 0:P - 1], ALU.not_equal)
            link(differ)
            link(dve.tensor_scalar(change[:, :, :, 1:P], same[:, :, 1:P].unsqueeze(2).broadcast_to([RB, SB, H, P - 1]),
                                   -BIG, None, ALU.mult))
            for b in range(SB):
                dve.wait_ge(pe_step, b + 1)
                link(dve.tensor_copy(value[:, b, :, :].rearrange("p h l -> p (h l)"), bank[b][0:RB, :]))
            flat = "p b h l -> p (b h l)"
            n = SB * H * P
            v, c, m = (x[:, :, :, :].rearrange(flat) for x in (value, change, best))
            link(dve.tensor_tensor_scan(m, c, v, -BIG, ALU.add, ALU.max))
            link(dve.tensor_copy(v[:, n - 1:n], m[:, n - 1:n]))
            link(dve.tensor_tensor_scan(v[:, 0:n - 1][:, ::-1], c[:, 1:n][:, ::-1], m[:, 0:n - 1][:, ::-1],
                                        v[:, n - 1:n], ALU.add, ALU.max))
            for side, at in ((0, 0), (1, P - 1)):
                link(dve.tensor_copy(ends[:, side, :, :], dst_rows[:, :, at:at + 1].broadcast_to([RB, SB, H])))
                last = dve.tensor_copy(peaks[:, side, :, :], value[:, :, :, at])
                link(last) if side == 0 else last.then_inc(taken, 1)
            dve.wait_ge(pe_step, SB + 1)
            for side in range(2):
                link(dve.tensor_copy(end_row[:, side, :], bank[4 + side][0:H, 0:NS]))
                link(dve.tensor_copy(peak_row[:, side, :], bank[6 + side][0:H, 0:NS]))
            link(dve.memset(linked[:, :], -BIG))
            link(dve.tensor_tensor(linked[:, 1:NS], end_row[:, 0, 1:NS], end_row[:, 1, 0:NS - 1], ALU.not_equal))
            link(dve.tensor_scalar(linked[:, 1:NS], linked[:, 1:NS], -BIG, None, ALU.mult))
            link(dve.tensor_tensor(whole[:, :], end_row[:, 0, :], end_row[:, 1, :], ALU.not_equal))
            link(dve.tensor_scalar(whole[:, :], whole[:, :], -BIG, None, ALU.mult))
            link(dve.tensor_tensor(decay[:, :], whole[:, :], linked[:, 0:NS], ALU.min))
            link(dve.memset(carried[:, 0, 0:1], -BIG))
            link(dve.tensor_tensor_scan(carried[:, 0, 1:NS + 1], decay[:, :], peak_row[:, 1, :], -BIG,
                                        ALU.add, ALU.max))
            link(dve.tensor_tensor(carry_row[:, 0, :], carried[:, 0, 0:NS], linked[:, 0:NS], ALU.add))
            link(dve.tensor_tensor(decay[:, :], whole[:, :], linked[:, 1:NS + 1], ALU.min))
            link(dve.memset(carried[:, 1, NS:NS + 1], -BIG))
            link(dve.tensor_tensor_scan(carried[:, 1, 0:NS][:, ::-1], decay[:, ::-1], peak_row[:, 0, ::-1], -BIG,
                                        ALU.add, ALU.max))
            dve.tensor_tensor(carry_row[:, 1, :], carried[:, 1, 1:NS + 1], linked[:, 1:NS + 1], ALU.add)\
               .then_inc(taken, 1)
            dve.wait_ge(pe_step, SB + 2)
            for side in range(2):
                link(dve.tensor_copy(carry[:, side, :, :].rearrange("p b h -> p (b h)"), bank[side][0:RB, 0:SB * H]))
            for side in range(2):
                link(dve.tensor_tensor(same[:, :, :], dst_rows[:, :, :],
                                       ends[:, side, :, 0:1].broadcast_to([RB, SB, P]), ALU.not_equal))
                link(dve.tensor_scalar(offer[:, :, :, :], same[:, :, :].unsqueeze(2).broadcast_to([RB, SB, H, P]),
                                       -BIG, None, ALU.mult))
                link(dve.tensor_tensor(offer[:, :, :, :], offer[:, :, :, :],
                                       carry[:, side, :, :].unsqueeze(3).broadcast_to([RB, SB, H, P]), ALU.add))
                last = dve.tensor_tensor((value, best)[side][:, :, :, :], value[:, :, :, :], offer[:, :, :, :], ALU.max)
                link(last) if side == 0 else last.then_inc(taken, 1)
            dve.wait_ge(pe_step, SB + 3)
            for h in range(H):
                link(dve.tensor_copy(el_er[:, 1, :, h], bank[4 + h][:, 0:NS]))


def aggregate(nc, A, hold, name, bank, const, acc, step_tile, src_lane, dst_lane, table, weight, edge_weight):
    HALF = W_AGG // 2
    HV = H - 1
    WIDTH = D + H if edge_weight is None else D
    with Stage(nc) as ctx:
        def sb(nm, shape, dt=F32):
            return ctx.enter_context(nc.sbuf_tensor(f"{name}_{nm}", shape, dt))

        def sem(nm):
            return ctx.semaphore(f"{name}_{nm}")

        index = sb("index", [P, 2, HALF], I32)
        rows = sb("rows", [P, W_AGG, WIDTH])
        hot = sb("hot", [P, W_AGG, P])
        msg = sb("msg", [P, W_AGG, WIDTH]) if edge_weight is None else rows
        zeroed, index_ready = sem("zeroed"), sem("index_ready")
        gathered = [sem(f"gathered{s}") for s in range(W_AGG)]
        ready, last_ready, summed, added = sem("ready"), sem("last_ready"), sem("summed"), sem("added")
        block = ctx.enter_context(nc.Block())

        @block.gpsimd
        def _(pool):
            def gather(i, s):
                half, at = divmod(s, HALF)
                if at == 0:
                    hold(pool, index_ready, 2 * i + half + 1)
                if s % 5 == 0:
                    once(pool, summed, i * W_AGG + s - W_AGG + 5, hold)
                pool.indirect_dma_start(rows[:, s, :], None, table,
                                        bass.IndirectOffsetOnAxis(ap=index[:, half, at:at + 1], axis=0))\
                    .then_inc(gathered[s], 16)

            pipeline(pool, [(0, gather)], NS // W_AGG, W_AGG)

        @block.vector
        def _(dve):
            def weigh(i, s):
                n = i * W_AGG + s
                half, at = divmod(s, HALF)
                once(dve, summed, n - W_AGG + 1)
                lane = dst_lane[:, bass.ds(n, 1)]
                if edge_weight is None:
                    dve.tensor_scalar(hot[:, s, :], const[:, C_IOTA:C_IOTA + P], lane, None, ALU.is_equal)
                    dve.wait_ge(gathered[s], i * 16 + 16)
                    w = weight[:, bass.ds(n, 1), 0:HV].rearrange("p a h -> p (a h)")
                    dve.tensor_tensor(msg[:, s, 0:HV * DW].rearrange("p (h d) -> p h d", h=HV),
                                      rows[:, s, 0:HV * DW].rearrange("p (h d) -> p h d", h=HV),
                                      w.unsqueeze(2).broadcast_to([P, HV, DW]), ALU.mult).then_inc(ready, 1)
                else:
                    dve.tensor_scalar(hot[:, s, :], const[:, C_IOTA:C_IOTA + P], lane, edge_weight[:, bass.ds(n, 1)],
                                      ALU.is_equal, ALU.mult).then_inc(ready, 1)
                    dve.wait_ge(gathered[s], i * 16 + 16)
                if at == HALF - 1:
                    dve.tensor_copy(index[:, half, :], src_lane[:, bass.ds(n + 1 + HALF, HALF)]).then_inc(index_ready, 1)

            tiles = []

            def add(i, s):
                n = i * W_AGG + s
                if s % 4 == 0:
                    tiles[:] = tiles_of(nc, dve, step_tile, n, 4)
                tile = tiles[s % 4]
                dve.wait_ge(summed, n + 1)
                once(dve, added, n)
                to = acc[:, bass.ds(tile, 1), 0:WIDTH].rearrange("p a n -> p (a n)")
                dve.tensor_tensor(to, bank[s % 4][:, 0:WIDTH], to, ALU.add).then_inc(added, 1)

            for half in range(2):
                dve.tensor_copy(index[:, half, :], src_lane[:, half * HALF:(half + 1) * HALF]).then_inc(index_ready, 1)
            dve.memset(acc[:, :, :], 0.0).then_inc(zeroed, 1)
            dve.wait_ge(zeroed, 1)
            pipeline(dve, [(0, weigh), (4, add)], NS // W_AGG, W_AGG)

        @block.scalar
        def _(act):
            def weigh(i, s):
                n = i * W_AGG + s
                once(act, summed, n - W_AGG + 1)
                act.wait_ge(gathered[s], i * 16 + 16)
                act.activation(msg[:, s, HV * DW:], rows[:, s, HV * DW:], ACT.Copy,
                               scale=weight[:, bass.ds(n, 1), HV:H].rearrange("p a h -> p (a h)")).then_inc(last_ready, 1)

            if edge_weight is None:
                pipeline(act, [(0, weigh)], NS // W_AGG, W_AGG)

        @block.tensor
        def _(pe):
            def add_up(i, s):
                n = i * W_AGG + s
                if edge_weight is None:
                    pe.wait_ge(last_ready, n + 1)
                pe.wait_ge(gathered[s], i * 16 + 16)
                pe.wait_ge(ready, n + 1)
                once(pe, added, n - 3)
                pe.matmul(bank[s % 4][:, 0:WIDTH], hot[:, s, :], msg[:, s, :], start=True, stop=True)\
                  .then_inc(summed, 1)

            pipeline(pe, [(0, add_up)], NS // W_AGG, W_AGG)


class Scope:

    def __init__(self, nc, ctx, name):
        self.nc, self.ctx, self.name = nc, ctx, name

    def sb(self, name, shape, dt=F32):
        return self.ctx.enter_context(self.nc.sbuf_tensor(f"{self.name}_{name}", shape, dt))

    def sem(self, name):
        return self.ctx.semaphore(f"{self.name}_{name}")

    def sems(self, name, n=R):
        return [self.sem(f"{name}{j}") for j in range(n)]

    def block(self):
        return self.ctx.enter_context(self.nc.Block())


def rows_of(x, g):
    return x[bass.ds(g * P, P), :]


def tile_of(x, g):
    return x[:, bass.ds(g, 1), :].rearrange("p a n -> p (a n)")


def weights(x):
    return x.rearrange("(k p) n -> p k n", p=P)


def first_graph_mlp(nc, A, hold, bank, const, acc, fold, xn1T, x_d, xn_d, xnT_d, x1_d, xn1_d):
    ident = const[:, C_ID:C_ID + P]
    FT = DF // P
    with Stage(nc) as ctx:
        S = Scope(nc, ctx, "g1")
        w1, w2, b1 = S.sb("w1", [P, KT, DF]), S.sb("w2", [P, FT, D]), S.sb("b1", [P, FT])
        bias = S.sb("bias", [P, 3, D])
        x_in, xn_in, xT_in = S.sb("x_in", [P, R, D]), S.sb("xn_in", [P, R, D]), S.sb("xT_in", [P, R, D])
        share, rst, low, high = (S.sb("share", [P, H]), S.sb("rst", [P, R, D]), S.sb("low", [P, R, D]),
                                 S.sb("high", [P, D]))
        h, hT, mid, x1, xn1 = (S.sb("h", [P, R, D]), S.sb("hT", [P, R, D]), S.sb("mid", [P, R, DF]),
                               S.sb("x1", [P, R, D]), S.sb("xn1", [P, R, D]))
        hT_ps, mid_ps, y_ps, xT_ps = ([bank[2 * n], bank[2 * n + 1]] for n in range(4))
        w_in, bias_ready = S.sem("w_in"), S.sem("bias_ready")
        loaded, x1_stored, xn1_stored = S.sems("loaded"), S.sems("x1_stored"), S.sems("xn1_stored")
        a_step, b_step, c_step = S.sem("a_step"), S.sem("b_step"), S.sem("c_step")
        low_ready, low_exp, h_ready, h_turned, hT_ready, mid_done, mid_ready, y_done, x1_ready, xn1_ready, \
            xn1_turned, xn1T_ready = (S.sem(n) for n in (
                "low_ready", "low_exp", "h_ready", "h_turned", "hT_ready", "mid_done", "mid_ready", "y_done",
                "x1_ready", "xn1_ready", "xn1_turned", "xn1T_ready"))
        norm = Norm(nc, ctx, "g1_norm", hold, const[:, C_POW:C_POW + 1])
        block = S.block()

        @block.sync
        def _(sp):
            for dst, src in ((w1, weights(A["L0_gnn_w1"])), (w2, weights(A["L0_gnn_w2"])), (b1, A["L0_gnn_b1"])):
                sp.dma_start(dst[...], src).then_inc(w_in, 16)
            for n, name in enumerate(("L0_gnn_gat_bias", "L0_gnn_b2", "L0_mix_b_out")):
                sp.dma_start(bias[:, n, :], A[name].broadcast_to([P, D])).then_inc(w_in, 16)

            def load(i, j):
                g = i * R + j
                once(sp, y_done, g - R + 1)
                once(sp, x1_ready, g - R + 1, hold)
                sp.dma_start(x_in[:, j, :], rows_of(x_d, g)).then_inc(loaded[j], 16)
                sp.dma_start(xn_in[:, j, :], rows_of(xn_d, g)).then_inc(loaded[j], 16)
                sp.dma_start(xT_in[:, j, :], xnT_d[bass.ds(g, 1), :, :].rearrange("a p n -> p (a n)"))\
                  .then_inc(loaded[j], 16)

            pipeline(sp, [(0, load)])
            for j in range(R):
                sp.wait_ge(x1_stored[j], 16 * NI)
                sp.wait_ge(xn1_stored[j], 16 * NI)

        @block.gpsimd
        def _(pool):
            def store_x(i, j):
                g = i * R + j
                norm.root(pool, g)
                pool.dma_start(rows_of(x1_d, g), x1[:, j, :]).then_inc(x1_stored[j], 16)

            def store_xn(i, j):
                g = i * R + j
                hold(pool, xn1_ready, g + 1)
                pool.dma_start(rows_of(xn1_d, g), xn1[:, j, :]).then_inc(xn1_stored[j], 16)

            pipeline(pool, [(4, store_xn), (3, store_x)])

        @block.vector
        def _(dve):
            dve.wait_ge(w_in, 96)
            dve.tensor_tensor(bias[:, 1, :], bias[:, 1, :], bias[:, 2, :], ALU.add).then_inc(bias_ready, 1)
            dve.wait_ge(bias_ready, 1)

            def mean(i, j):
                g = i * R + j
                link = Steps(dve, a_step, g, 4)
                sums = tile_of(acc, g).rearrange("p (h d) -> p h d", h=H)
                link(dve.tensor_scalar(share[:, :], sums[:, :, DH], 1e-30, None, ALU.max))
                link(dve.reciprocal(share[:, :], share[:, :]))
                link(dve.tensor_tensor(rst[:, j, :].rearrange("p (h d) -> p h d", h=H),
                                       sums[:, :, 0:DH],
                                       share[:, :].unsqueeze(2).broadcast_to([P, H, DH]), ALU.mult))
                link(dve.tensor_tensor(rst[:, j, :], rst[:, j, :], bias[:, 0, :], ALU.add))
                link.end()
                dve.tensor_scalar(low[:, j, :], rst[:, j, :], 0.0, None, ALU.min).then_inc(low_ready, 1)

            def elu(i, j):
                g = i * R + j
                link = Steps(dve, b_step, g, 1)
                dve.wait_ge(low_exp, g + 1)
                dve.wait_ge(loaded[j], 48 * i + 48)
                link(dve.scalar_tensor_tensor(out=high[:, :], in0=rst[:, j, :], scalar=0.0, in1=low[:, j, :],
                                              op0=ALU.max, op1=ALU.add))
                link.end()
                dve.scalar_tensor_tensor(out=h[:, j, :], in0=high[:, :], scalar=-1.0, in1=xn_in[:, j, :],
                                         op0=ALU.add, op1=ALU.add).then_inc(h_ready, 1)

            def residual(i, j):
                g = i * R + j
                link = Steps(dve, c_step, g, 1)
                once(dve, x1_stored[j], i * 16)
                link(dve.tensor_tensor(x1[:, j, :], x_in[:, j, :], bias[:, 1, :], ALU.add))
                link.end()
                dve.wait_ge(y_done, g + 1)
                dve.tensor_tensor(x1[:, j, :], y_ps[j % 2][:, 0:D], x1[:, j, :], ALU.add).then_inc(x1_ready, 1)
                dve.wait_ge(x1_ready, g + 1)
                norm.find(dve, x1[:, j, :], g)

            def norm_x(i, j):
                g = i * R + j
                once(dve, xn1_stored[j], i * 16)
                once(dve, xn1_turned, g - R + 1)
                norm.apply(dve, xn1[:, j, :], x1[:, j, :], g).then_inc(xn1_ready, 1)

            pipeline(dve, [(1, elu), (4, norm_x), (3, residual), (0, mean)])

        @block.scalar
        def _(act):
            act.wait_ge(w_in, 96)

            def exp_low(i, j):
                g = i * R + j
                act.wait_ge(low_ready, g + 1)
                act.activation(low[:, j, :], low[:, j, :], ACT.Exp).then_inc(low_exp, 1)

            def copy_h(i, j):
                g = i * R + j
                act.wait_ge(h_turned, g + 1)
                act.activation(hT[:, j, :], hT_ps[j % 2][:, 0:D], ACT.Copy).then_inc(hT_ready, 1)

            def relu(i, j):
                g = i * R + j
                act.wait_ge(mid_done, g + 1)
                for f in range(FT):
                    last = act.activation(mid[:, j, f * P:(f + 1) * P], mid_ps[j % 2][:, f * P:(f + 1) * P], ACT.Relu,
                                          bias=b1[:, f:f + 1])
                last.then_inc(mid_ready, 1)

            def copy_x(i, j):
                g = i * R + j
                act.wait_ge(xn1_turned, g + 1)
                act.activation(xn1T[:, :, bass.ds(g * P, P)], xT_ps[j % 2][:, 0:D].rearrange("p (k n) -> p k n", k=KT),
                               ACT.Copy).then_inc(xn1T_ready, 1)

            pipeline(act, [(1, copy_h), (2, relu), (4, copy_x), (0, exp_low)])

        @block.tensor
        def _(pe):
            pe.wait_ge(w_in, 96)

            def turn_h(i, j):
                g = i * R + j
                pe.wait_ge(h_ready, g + 1)
                once(pe, hT_ready, g - bank_gap(j) + 1)
                for k in range(KT):
                    last = pe.transpose(hT_ps[j % 2][:, k * P:(k + 1) * P], h[:, j, k * P:(k + 1) * P], ident)
                last.then_inc(h_turned, 1)

            def mlp_in(i, j):
                g = i * R + j
                pe.wait_ge(hT_ready, g + 1)
                once(pe, mid_ready, g - bank_gap(j) + 1)
                for f in range(FT):
                    for k in range(KT):
                        last = pe.matmul(mid_ps[j % 2][:, f * P:(f + 1) * P], w1[:, k, f * P:(f + 1) * P],
                                         hT[:, j, k * P:(k + 1) * P], start=(k == 0), stop=(k == KT - 1))
                last.then_inc(mid_done, 1)

            def mlp_out(i, j):
                g = i * R + j
                pe.wait_ge(mid_ready, g + 1)
                once(pe, x1_ready, g - bank_gap(j) + 1)
                pe.wait_ge(loaded[j], 48 * i + 48)
                for f in range(FT):
                    pe.matmul(y_ps[j % 2][:, 0:D], mid[:, j, f * P:(f + 1) * P], w2[:, f, :], start=(f == 0), stop=False)
                for k in range(KT):
                    last = pe.matmul(y_ps[j % 2][:, 0:D], xT_in[:, j, k * P:(k + 1) * P], fold[:, k, :],
                                     start=False, stop=(k == KT - 1))
                last.then_inc(y_done, 1)

            def turn_x(i, j):
                g = i * R + j
                pe.wait_ge(xn1_ready, g + 1)
                once(pe, xn1T_ready, g - bank_gap(j) + 1)
                for k in range(KT):
                    last = pe.transpose(xT_ps[j % 2][:, k * P:(k + 1) * P], xn1[:, j, k * P:(k + 1) * P], ident)
                last.then_inc(xn1_turned, 1)

            pipeline(pe, [(3, mlp_out), (1, turn_h), (2, mlp_in), (4, turn_x)])


def first_router(nc, A, hold, bank, const, xn1T, w1, w2, b1, bias):
    FT = DF // P
    capacity = float(-(-N_NODES * 5 // (4 * E)))
    with Stage(nc) as ctx:
        S = Scope(nc, ctx, "r1")
        mean, w_r, line, small = S.sb("mean", [P, KT]), S.sb("w_r", [P, KT, E]), S.sb("line", [1, 6, E]), S.sb("small", [1, 4])
        top, index, pair = S.sb("top", [1, E]), S.sb("index", [1, E], U32), S.sb("pair", [1, 2])
        share, b2 = S.sb("share", [P, 2]), S.sb("b2", [P, 2, D])
        w_in, step, mean_ready, logits, peak, exp_done, picked, spread, experts_in, shared = (S.sem(n) for n in (
            "w_in", "step", "mean_ready", "logits", "peak", "exp_done", "picked", "spread", "experts_in", "shared"))
        block = S.block()
        x, e, rw, load, cut, br = (line[:, n, :] for n in range(6))

        @block.sync
        def _(sp):
            sp.dma_start(w_r[:, :, :], weights(A["L0_ffn_Wr"])).then_inc(w_in, 16)
            sp.dma_start(br, A["L0_ffn_br"]).then_inc(w_in, 16)
            sp.wait_ge(picked, 1)
            for n in range(2):
                at = sp.value_load(index[0:1, n:n + 1], min_val=0, max_val=E - 1)
                sp.dma_start(w1[:, n, :, :], A["L0_ffn_W1"][bass.ds(at, 1), :, :]
                             .rearrange("a (k p) n -> p (a k) n", p=P)).then_inc(experts_in, 16)
                sp.dma_start(w2[:, n, :, :], A["L0_ffn_W2"][bass.ds(at, 1), :, :]
                             .rearrange("a (k p) n -> p (a k) n", p=P)).then_inc(experts_in, 16)
                sp.dma_start(b1[:, n, :], A["L0_ffn_b1"][bass.ds(at, 1), :, :].rearrange("a p f -> p (a f)"))\
                  .then_inc(experts_in, 16)
                sp.dma_start(b2[:, n, :], A["L0_ffn_b2"][bass.ds(at, 1), :].broadcast_to([P, D])).then_inc(experts_in, 16)

        @block.tensor
        def _(pe):
            pe.wait_ge(w_in, 32)
            pe.wait_ge(mean_ready, 1)
            for k in range(KT):
                last = pe.matmul(bank[0][0:1, 0:E], mean[:, k:k + 1], w_r[:, k, :], start=(k == 0), stop=(k == KT - 1))
            last.then_inc(logits, 1)
            pe.wait_ge(shared, 1)
            pe.matmul(bank[1][:, 0:2], const[0:1, C_ONE:C_ONE + P], pair[:, :], start=True, stop=True).then_inc(spread, 1)

        @block.scalar
        def _(act):
            for n, (dst, width) in enumerate(((e, E), (e, E), (pair[:, :], 2))):
                act.wait_ge(peak, n + 1)
                src = dst if n == 2 else x
                act.activation(dst, src, ACT.Exp).then_inc(exp_done, 1)

        @block.vector
        def _(dve):
            link = Steps(dve, step)

            def softmax(src, dst, at, n, tmp):
                link(dve.tensor_reduce(small[:, at:at + 1], src, AX, ALU.max))
                dve.tensor_scalar(tmp, src, small[:, at:at + 1], None, ALU.subtract).then_inc(peak, 1)
                dve.wait_ge(exp_done, n + 1)
                out = pair[:, :] if n == 2 else e
                link(dve.tensor_reduce(small[:, at:at + 1], out, AX, ALU.add))
                link(dve.reciprocal(small[:, at:at + 1], small[:, at:at + 1]))
                return dve.tensor_scalar(dst, out, small[:, at:at + 1], None, ALU.mult)

            link(dve.tensor_reduce(mean[:, :], xn1T[:, :, 0:N_NODES], AX, ALU.add))
            dve.tensor_scalar(mean[:, :], mean[:, :], 1.0 / N_NODES, None, ALU.mult).then_inc(mean_ready, 1)
            dve.wait_ge(logits, 1)
            link(dve.tensor_tensor(cut, bank[0][0:1, 0:E], br, ALU.add))
            link(softmax(cut, rw, 0, 0, x))
            link(dve.tensor_scalar(load, rw, float(N_NODES), None, ALU.mult))
            link(dve.reciprocal(cut, load))
            link(dve.tensor_scalar(cut, cut, capacity, None, ALU.mult))
            link(dve.tensor_scalar(load, load, capacity, None, ALU.is_gt))
            link(dve.tensor_tensor(cut, cut, load, ALU.mult))
            link(dve.tensor_scalar(load, load, -1.0, 1.0, ALU.mult, ALU.add))
            link(dve.tensor_tensor(cut, cut, load, ALU.add))
            link(dve.tensor_tensor(rw, rw, cut, ALU.mult))
            link(softmax(rw, cut, 1, 1, x))
            link(dve.max(top[:, :], cut))
            dve.max_index(index[:, :], top[:, :], cut).then_inc(picked, 1)
            link(softmax(top[:, 0:2], pair[:, :], 2, 2, pair[:, :]))
            dve.engine_nop().then_inc(shared, 1)
            dve.wait_ge(spread, 1)
            link(dve.tensor_copy(share[:, :], bank[1][:, 0:2]))
            dve.wait_ge(experts_in, 16 * 8)
            for n in range(2):
                link(dve.tensor_scalar(w2[:, n, :, :], w2[:, n, :, :], share[:, n:n + 1], None, ALU.mult))
            link(dve.tensor_scalar(bias[:, :], b2[:, 0, :], share[:, 0:1], None, ALU.mult))
            link(dve.scalar_tensor_tensor(out=bias[:, :], in0=b2[:, 1, :], scalar=share[:, 1:2], in1=bias[:, :],
                                          op0=ALU.mult, op1=ALU.add))


def first_experts(nc, A, hold, bank, const, xn1T, w1, w2, b1, bias, big_k, big_v, x1_d, xn1_d, x2_d, xn2_d, qT_d):
    ident = const[:, C_ID:C_ID + P]
    FT = 2 * DF // P
    HM, SM = 8, 32
    with Stage(nc) as ctx:
        S = Scope(nc, ctx, "e1")
        vec = S.sb("vec", [P, 2, D])
        col = S.sb("col", [P, 3, KT])
        w_x, w_q, w_k, w_v = S.sb("w_x", [P, KT, D]), S.sb("w_q", [P, P]), S.sb("w_k", [P, P]), S.sb("w_v", [P, P])
        x1_in, xn1_in = S.sb("x1_in", [P, R, D]), S.sb("xn1_in", [P, R, D])
        mid = S.sb("mid", [P, R, FT * P])
        y, out0 = S.sb("y", [P, D]), S.sb("out0", [P, D])
        x2, xn2, ln = S.sb("x2", [P, R, D]), S.sb("xn2", [P, R, D]), S.sb("ln", [P, R, D])
        lnT, xm = S.sb("lnT", [P, D]), S.sb("xm", [P, D])
        q, most, total, qT = S.sb("q", [P, R, D]), S.sb("most", [P, HM]), S.sb("total", [P, HM]), S.sb("qT", [P, R, D])
        w_in = S.sem("w_in")
        loaded, x2_stored, xn2_stored, qT_stored = (S.sems(n) for n in ("loaded", "x2_stored", "xn2_stored", "qT_stored"))
        a_step, b_step, c_step, d_step = (S.sem(n) for n in ("a_step", "b_step", "c_step", "d_step"))
        mid_done0, mid_done1, mid_ready0, mid_ready1, y_done, y_ready, x2_ready, xn2_ready, ln_ready, ln_turned, lnT_ready, \
            xm_done, xm_ready, qv_done, k_done, k_ready, q_cut, v_ready, q_exp, q_ready, q_turned, qT_ready = (
                S.sem(n) for n in ("mid_done0", "mid_done1", "mid_ready0", "mid_ready1", "y_done", "y_ready",
                                   "x2_ready", "xn2_ready", "ln_ready", "ln_turned", "lnT_ready", "xm_done", "xm_ready",
                                   "qv_done", "k_done", "k_ready", "q_cut", "v_ready", "q_exp", "q_ready", "q_turned",
                                   "qT_ready"))
        norms = [Norm(nc, ctx, f"e1_norm{n}", hold, const[:, C_POW:C_POW + 1]) for n in range(3)]
        mid_ps, y_ps, ln_ps, xm_ps, qv_ps, k_ps, q_ps = [bank[0], bank[1]], *bank[2:8]
        mid_done, mid_ready = [mid_done0, mid_done1], [mid_ready0, mid_ready1]
        block = S.block()

        @block.sync
        def _(sp):
            for n, name in enumerate(("L0_ffn_gamma", "L0_ffn_beta")):
                sp.dma_start(vec[:, n, :], A[name].broadcast_to([P, D])).then_inc(w_in, 16)
            for n, name in enumerate(("L1_mix_ln1_w", "L1_mix_ln1_b", "L1_mix_bx")):
                sp.dma_start(col[:, n, :], A[name]).then_inc(w_in, 16)
            sp.dma_start(w_x[:, :, :], weights(A["L1_mix_WxT"])).then_inc(w_in, 16)
            for w, name in ((w_q, "L1_mix_WqT4"), (w_k, "L1_mix_WkT4"), (w_v, "L1_mix_WvT4")):
                sp.dma_start(w[:, :], A[name]).then_inc(w_in, 16)

            def load(i, j):
                g = i * R + j
                once(sp, x2_ready, g - R + 1, hold)
                sp.dma_start(x1_in[:, j, :], rows_of(x1_d, g)).then_inc(loaded[j], 16)
                sp.dma_start(xn1_in[:, j, :], rows_of(xn1_d, g)).then_inc(loaded[j], 16)

            pipeline(sp, [(0, load)])
            for j in range(R):
                for s in (x2_stored, xn2_stored, qT_stored):
                    sp.wait_ge(s[j], 16 * NI)

        @block.gpsimd
        def _(pool):
            def root_y(i, j):
                norms[0].root(pool, i * R + j)

            def store_x(i, j):
                g = i * R + j
                norms[1].root(pool, g)
                pool.dma_start(rows_of(x2_d, g), x2[:, j, :]).then_inc(x2_stored[j], 16)

            def store_xn(i, j):
                g = i * R + j
                norms[2].root(pool, g)
                pool.dma_start(rows_of(xn2_d, g), xn2[:, j, :]).then_inc(xn2_stored[j], 16)

            pipeline(pool, [(3, store_xn), (2, store_x), (1, root_y)])

        @block.vector
        def _(dve):
            dve.wait_ge(w_in, 16 * 9)

            def add_y(i, j):
                g = i * R + j
                dve.wait_ge(loaded[j], 32 * i + 32)
                link = Steps(dve, c_step, g, 1)
                link(dve.tensor_tensor(y[:, :], xn1_in[:, j, :], bias[:, :], ALU.add))
                link.end()
                dve.wait_ge(y_done, g + 1)
                dve.tensor_tensor(y[:, :], y_ps[:, 0:D], y[:, :], ALU.add).then_inc(y_ready, 1)
                dve.wait_ge(y_ready, g + 1)
                norms[0].find(dve, y[:, :], g)

            def residual(i, j):
                g = i * R + j
                link = Steps(dve, d_step, g, 3)
                link(norms[0].apply(dve, out0[:, :], y[:, :], g))
                link(dve.tensor_tensor(out0[:, :], out0[:, :], vec[:, 0, :], ALU.mult))
                link(dve.tensor_tensor(out0[:, :], out0[:, :], vec[:, 1, :], ALU.add))
                link.end()
                once(dve, x2_stored[j], 16 * i)
                dve.tensor_tensor(x2[:, j, :], out0[:, :], x1_in[:, j, :], ALU.add).then_inc(x2_ready, 1)
                dve.wait_ge(x2_ready, g + 1)
                norms[1].find(dve, x2[:, j, :], g)

            def norm_x(i, j):
                g = i * R + j
                once(dve, xn2_stored[j], 16 * i)
                norms[1].apply(dve, xn2[:, j, :], x2[:, j, :], g).then_inc(xn2_ready, 1)
                dve.wait_ge(xn2_ready, g + 1)
                norms[2].find(dve, xn2[:, j, :], g)

            def norm_again(i, j):
                g = i * R + j
                once(dve, ln_turned, g - R + 1)
                norms[2].apply(dve, ln[:, j, :], xn2[:, j, :], g).then_inc(ln_ready, 1)

            def cut(i, j):
                g = i * R + j
                dve.wait_ge(qv_done, g + 1)
                link = Steps(dve, a_step, g, 1)
                q_in = qv_ps[:, 0:D].rearrange("p (h s) -> p h s", h=HM)
                link(dve.tensor_reduce(most[:, :], q_in, AX, ALU.max))
                link.end()
                once(dve, q_turned, g - R + 1)
                dve.tensor_tensor(q[:, j, :].rearrange("p (h s) -> p h s", h=HM), q_in,
                                  most[:, :].unsqueeze(2).broadcast_to([P, HM, SM]), ALU.subtract).then_inc(q_cut, 1)
                dve.tensor_copy(tile_of(big_v, g), qv_ps[:, D:2 * D]).then_inc(v_ready, 1)

            def divide(i, j):
                g = i * R + j
                dve.wait_ge(q_exp, g + 1)
                link = Steps(dve, b_step, g, 2)
                view = q[:, j, :].rearrange("p (h s) -> p h s", h=HM)
                link(dve.tensor_reduce(total[:, :], view, AX, ALU.add))
                link(dve.reciprocal(total[:, :], total[:, :]))
                link.end()
                dve.tensor_tensor(view, view, total[:, :].unsqueeze(2).broadcast_to([P, HM, SM]), ALU.mult)\
                   .then_inc(q_ready, 1)

            pipeline(dve, [(4, norm_again), (5, divide), (3, norm_x), (2, residual), (4, cut), (1, add_y)])

        @block.scalar
        def _(act):
            act.wait_ge(w_in, 16 * 9)

            def copy_ln(i, j):
                g = i * R + j
                act.wait_ge(ln_turned, g + 1)
                once(act, xm_done, g)
                for k in range(KT):
                    last = act.activation(lnT[:, k * P:(k + 1) * P], ln_ps[:, k * P:(k + 1) * P], ACT.Identity,
                                          bias=col[:, 1, k:k + 1], scale=col[:, 0, k:k + 1])
                last.then_inc(lnT_ready, 1)

            def copy_q(i, j):
                g = i * R + j
                act.wait_ge(q_turned, g + 1)
                once(act, qT_stored[j], 16 * i)
                act.activation(qT[:, j, :], q_ps[:, 0:D], ACT.Copy).then_inc(qT_ready, 1)
                act.wait_ge(qT_ready, g + 1)
                act.dma_start(qT_d[bass.ds(g, 1), :, :].rearrange("a p n -> p (a n)"), qT[:, j, :])\
                   .then_inc(qT_stored[j], 16)

            def gelu(half):
                def stage(i, j):
                    g = i * R + j
                    once(act, y_done, g - R + 1)
                    act.wait_ge(mid_done[half], g + 1)
                    for f in range(4):
                        n = half * 4 + f
                        last = act.activation(mid[:, j, n * P:(n + 1) * P], mid_ps[half][:, f * P:(f + 1) * P],
                                              ACT.Gelu, bias=b1[:, half, f:f + 1])
                    last.then_inc(mid_ready[half], 1)
                return stage

            def add_bx(i, j):
                g = i * R + j
                act.wait_ge(xm_done, g + 1)
                once(act, k_done, g)
                for k in range(KT):
                    last = act.activation(xm[:, k * P:(k + 1) * P], xm_ps[:, k * P:(k + 1) * P], ACT.Identity,
                                          bias=col[:, 2, k:k + 1])
                last.then_inc(xm_ready, 1)

            def copy_k(i, j):
                g = i * R + j
                act.wait_ge(k_done, g + 1)
                act.activation(big_k[:, :].rearrange("p (k n) -> p k n", k=KT)[:, :, bass.ds(g * P, P)],
                               k_ps[:, 0:D].rearrange("p (k n) -> p k n", k=KT), ACT.Copy).then_inc(k_ready, 1)
                act.wait_ge(q_cut, g + 1)
                act.activation(q[:, j, :], q[:, j, :], ACT.Exp).then_inc(q_exp, 1)

            pipeline(act, [(0, gelu(0)), (4, copy_ln), (0, gelu(1)), (4, add_bx), (4, copy_k), (5, copy_q)])

        @block.tensor
        def _(pe):
            pe.wait_ge(w_in, 16 * 9)

            def turn_ln(i, j):
                g = i * R + j
                pe.wait_ge(ln_ready, g + 1)
                once(pe, lnT_ready, g)
                for k in range(KT):
                    last = pe.transpose(ln_ps[:, k * P:(k + 1) * P], ln[:, j, k * P:(k + 1) * P], ident)
                last.then_inc(ln_turned, 1)

            def turn_q(i, j):
                g = i * R + j
                pe.wait_ge(q_ready, g + 1)
                once(pe, qT_ready, g)
                for k in range(KT):
                    last = pe.transpose(q_ps[:, k * P:(k + 1) * P], q[:, j, k * P:(k + 1) * P], ident)
                last.then_inc(q_turned, 1)

            def expert_in(half):
                def stage(i, j):
                    g = i * R + j
                    once(pe, mid_ready[half], g)
                    for f in range(4):
                        for k in range(KT):
                            last = pe.matmul(mid_ps[half][:, f * P:(f + 1) * P], w1[:, half, k, f * P:(f + 1) * P],
                                             xn1T[:, k, bass.ds(g * P, P)], start=(k == 0), stop=(k == KT - 1))
                    last.then_inc(mid_done[half], 1)
                return stage

            def expert_out(half):
                def stage(i, j):
                    g = i * R + j
                    once(pe, y_ready, g)
                    pe.wait_ge(mid_ready[half], g + 1)
                    for f in range(4):
                        n = half * 4 + f
                        last = pe.matmul(y_ps[:, 0:D], mid[:, j, n * P:(n + 1) * P], w2[:, half, f, :],
                                         start=(n == 0), stop=(n == FT - 1))
                    if half == 1:
                        last.then_inc(y_done, 1)
                return stage

            def project_x(i, j):
                g = i * R + j
                pe.wait_ge(lnT_ready, g + 1)
                once(pe, xm_ready, g)
                for m in range(KT):
                    for k in range(KT):
                        last = pe.matmul(xm_ps[:, m * P:(m + 1) * P], w_x[:, k, m * P:(m + 1) * P],
                                         lnT[:, k * P:(k + 1) * P], start=(k == 0), stop=(k == KT - 1))
                last.then_inc(xm_done, 1)

            def project_qkv(i, j):
                g = i * R + j
                pe.wait_ge(xm_ready, g + 1)
                once(pe, v_ready, g)
                for n, w in enumerate((w_q, w_v)):
                    for m in range(KT):
                        last = pe.matmul(qv_ps[:, n * D + m * P:n * D + (m + 1) * P], xm[:, m * P:(m + 1) * P], w[:, :],
                                         start=True, stop=True)
                last.then_inc(qv_done, 1)
                once(pe, k_ready, g)
                for m in range(KT):
                    last = pe.matmul(k_ps[:, m * P:(m + 1) * P], w_k[:, :], xm[:, m * P:(m + 1) * P],
                                     start=True, stop=True)
                last.then_inc(k_done, 1)

            pipeline(pe, [(0, expert_in(0)), (4, turn_ln), (0, expert_in(1)), (4, project_x), (1, expert_out(0)),
                          (4, project_qkv), (1, expert_out(1)), (5, turn_q)])


def second_mixer(nc, A, hold, bank, const, big_k, big_v, folded):
    ident = const[:, C_ID:C_ID + P]
    zero = const[:, C_ZERO:C_ZERO + P]
    with Stage(nc) as ctx:
        S = Scope(nc, ctx, "m2")
        w_o, peak, total = S.sb("w_o", [P, KT, D]), S.sb("peak", [P, KT]), S.sb("total", [P, KT])
        ekT, ek = S.sb("ekT", [P, R, D]), S.sb("ek", [P, R, D])
        kv, kvT = S.sb("kv", [P, KT, P]), S.sb("kvT", [P, KT, P])
        w_in, step, peak_ready, exp_ready, cut, turned, ek_ready, summed, pe_step, done = (S.sem(n) for n in (
            "w_in", "step", "peak_ready", "exp_ready", "cut", "turned", "ek_ready", "summed", "pe_step", "done"))
        block = S.block()
        k_view = big_k[:, :].rearrange("p (k n) -> p k n", k=KT)

        @block.sync
        def _(sp):
            sp.dma_start(w_o[:, :, :], weights(A["L1_mix_WoT"])).then_inc(w_in, 16)

        @block.vector
        def _(dve):
            link = Steps(dve, step)
            link(dve.memset(k_view[:, :, N_NODES:NP], 0.0))
            link(dve.tensor_reduce(peak[:, :], k_view[:, :, 0:N_NODES], AX, ALU.max))
            dve.tensor_scalar(peak[:, :], peak[:, :], -1.0, None, ALU.mult).then_inc(peak_ready, 1)
            dve.wait_ge(exp_ready, KT)
            link(dve.reciprocal(total[:, :], total[:, :]))

            def cut_tile(i, j):
                g = i * R + j
                once(dve, turned, g - R + 1)
                dve.tensor_copy(ekT[:, j, :].rearrange("p (k n) -> p k n", k=KT), k_view[:, :, bass.ds(g * P, P)])\
                   .then_inc(cut, 1)

            pipeline(dve, [(0, cut_tile)])
            dve.wait_ge(pe_step, 1)
            for m in range(KT):
                last = dve.tensor_tensor(kv[:, m, :], bank[4 + m][:, 0:P], const[:, C_BD:C_BD + P], ALU.mult)
            last.then_inc(done, 1)
            dve.wait_ge(pe_step, 2)
            dve.tensor_copy(kvT[:, :, :].rearrange("p k n -> p (k n)"), bank[2][:, 0:D]).then_inc(done, 1)
            dve.wait_ge(pe_step, 3)
            for m in range(KT):
                last = dve.tensor_scalar(folded[:, m, :], bank[3][:, m * D:(m + 1) * D], total[:, m:m + 1], None, ALU.mult)
            last.then_inc(done, 1)
            dve.wait_ge(done, 3)

        @block.scalar
        def _(act):
            act.wait_ge(peak_ready, 1)
            for k in range(KT):
                act.activation(k_view[:, k, 0:N_NODES], k_view[:, k, 0:N_NODES], ACT.Exp, bias=peak[:, k:k + 1],
                               accum_out=total[:, k:k + 1]).then_inc(exp_ready, 1)

            def copy_ek(i, j):
                g = i * R + j
                act.wait_ge(turned, g + 1)
                once(act, summed, g - R + 1)
                act.activation(ek[:, j, :], bank[j % 2][:, 0:D], ACT.Copy).then_inc(ek_ready, 1)

            pipeline(act, [(0, copy_ek)])

        @block.tensor
        def _(pe):
            pe.wait_ge(w_in, 16)
            for m in range(KT):
                pe.matmul(bank[4 + m][:, 0:P], zero, ident, start=True, stop=False)

            def turn(i, j):
                g = i * R + j
                pe.wait_ge(cut, g + 1)
                once(pe, ek_ready, g - bank_gap(j) + 1)
                for k in range(KT):
                    last = pe.transpose(bank[j % 2][:, k * P:(k + 1) * P], ekT[:, j, k * P:(k + 1) * P], ident)
                last.then_inc(turned, 1)

            def add(i, j):
                g = i * R + j
                pe.wait_ge(ek_ready, g + 1)
                for m in range(KT):
                    last = pe.matmul(bank[4 + m][:, 0:P], ek[:, j, m * P:(m + 1) * P],
                                     tile_of(big_v, g)[:, m * P:(m + 1) * P], start=False, stop=False)
                last.then_inc(summed, 1)

            pipeline(pe, [(0, turn), (1, add)])
            for m in range(KT):
                last = pe.matmul(bank[4 + m][:, 0:P], zero, ident, start=False, stop=True)
            last.then_inc(pe_step, 1)
            pe.wait_ge(done, 1)
            for m in range(KT):
                last = pe.transpose(bank[2][:, m * P:(m + 1) * P], kv[:, m, :], ident)
            last.then_inc(pe_step, 1)
            pe.wait_ge(done, 2)
            for m in range(KT):
                last = pe.matmul(bank[3][:, m * D:(m + 1) * D], kvT[:, m, :], w_o[:, m, :], start=True, stop=True)
            last.then_inc(pe_step, 1)


def mixer_mlp(nc, A, hold, bank, const, folded, x2_d, xn2_d, qT_d, mixed_d):
    ident = const[:, C_ID:C_ID + P]
    FT = HID // P
    with Stage(nc) as ctx:
        S = Scope(nc, ctx, "x2")
        w1, w2, b1 = S.sb("w1", [P, KT, HID]), S.sb("w2", [P, FT, D]), S.sb("b1", [P, FT])
        vec, col = S.sb("vec", [P, 2, D]), S.sb("col", [P, 2, KT])
        x_in, xn_in, qT_in = S.sb("x_in", [P, R, D]), S.sb("xn_in", [P, R, D]), S.sb("qT_in", [P, R, D])
        h, ln, lnT, mid, mixed = (S.sb("h", [P, R, D]), S.sb("ln", [P, R, D]), S.sb("lnT", [P, R, D]),
                                  S.sb("mid", [P, FT * P]), S.sb("mixed", [P, R, D]))
        w_in = S.sem("w_in")
        loaded, stored = S.sems("loaded"), S.sems("stored")
        a_step, c_step = S.sem("a_step"), S.sem("c_step")
        h_done, h_ready, ln_ready, ln_turned, lnT_ready, y_done, mixed_ready, mid_done0, mid_done1, mid_ready0, \
            mid_ready1 = (S.sem(n) for n in ("h_done", "h_ready", "ln_ready", "ln_turned", "lnT_ready", "y_done",
                                             "mixed_ready", "mid_done0", "mid_done1", "mid_ready0", "mid_ready1"))
        mid_done, mid_ready = [mid_done0, mid_done1], [mid_ready0, mid_ready1]
        norm = Norm(nc, ctx, "x2_norm", hold, const[:, C_POW:C_POW + 1])
        block = S.block()
        mid_ps, h_ps, ln_ps, y_ps = bank[0:2], bank[2], bank[3], bank[4]

        @block.sync
        def _(sp):
            for dst, src in ((w1, weights(A["L1_mix_W1T"])), (w2, weights(A["L1_mix_W2T"])), (b1, A["L1_mix_b1"])):
                sp.dma_start(dst[...], src).then_inc(w_in, 16)
            for n, name in enumerate(("L1_mix_bo", "L1_mix_b2")):
                sp.dma_start(vec[:, n, :], A[name].broadcast_to([P, D])).then_inc(w_in, 16)
            for n, name in enumerate(("L1_mix_ln2_w", "L1_mix_ln2_b")):
                sp.dma_start(col[:, n, :], A[name]).then_inc(w_in, 16)

            def load(i, j):
                g = i * R + j
                once(sp, mixed_ready, g - R + 1, hold)
                sp.dma_start(x_in[:, j, :], rows_of(x2_d, g)).then_inc(loaded[j], 16)
                sp.dma_start(xn_in[:, j, :], rows_of(xn2_d, g)).then_inc(loaded[j], 16)
                sp.dma_start(qT_in[:, j, :], qT_d[bass.ds(g, 1), :, :].rearrange("a p n -> p (a n)"))\
                  .then_inc(loaded[j], 16)

            pipeline(sp, [(0, load)])
            for j in range(R):
                sp.wait_ge(stored[j], 16 * NI)

        @block.gpsimd
        def _(pool):
            def root(i, j):
                norm.root(pool, i * R + j)

            def store(i, j):
                g = i * R + j
                hold(pool, mixed_ready, g + 1)
                pool.dma_start(rows_of(mixed_d, g), mixed[:, j, :]).then_inc(stored[j], 16)

            pipeline(pool, [(0, root), (4, store)])

        @block.vector
        def _(dve):
            dve.wait_ge(w_in, 16 * 7)

            def attend(i, j):
                g = i * R + j
                link = Steps(dve, a_step, g, 2)
                dve.wait_ge(loaded[j], 48 * i + 48)
                link(dve.tensor_tensor(h[:, j, :], xn_in[:, j, :], vec[:, 0, :], ALU.add))
                dve.wait_ge(h_done, g + 1)
                dve.tensor_tensor(h[:, j, :], h_ps[:, 0:D], h[:, j, :], ALU.add).then_inc(h_ready, 1)
                dve.wait_ge(h_ready, g + 1)
                norm.find(dve, h[:, j, :], g)
                norm.apply(dve, ln[:, j, :], h[:, j, :], g).then_inc(ln_ready, 1)
                link(dve.tensor_tensor(x_in[:, j, :], x_in[:, j, :], h[:, j, :], ALU.add))
                link.end()

            def residual(i, j):
                g = i * R + j
                link = Steps(dve, c_step, g, 1)
                once(dve, stored[j], 16 * i)
                link(dve.tensor_tensor(mixed[:, j, :], x_in[:, j, :], vec[:, 1, :], ALU.add))
                link.end()
                dve.wait_ge(y_done, g + 1)
                dve.tensor_tensor(mixed[:, j, :], y_ps[:, 0:D], mixed[:, j, :], ALU.add).then_inc(mixed_ready, 1)

            pipeline(dve, [(0, attend), (3, residual)])

        @block.scalar
        def _(act):
            act.wait_ge(w_in, 16 * 7)

            def copy_ln(i, j):
                g = i * R + j
                act.wait_ge(ln_turned, g + 1)
                for k in range(KT):
                    last = act.activation(lnT[:, j, k * P:(k + 1) * P], ln_ps[:, k * P:(k + 1) * P], ACT.Identity,
                                          bias=col[:, 1, k:k + 1], scale=col[:, 0, k:k + 1])
                last.then_inc(lnT_ready, 1)

            def gelu(i, j):
                g = i * R + j
                once(act, y_done, g)
                for half in range(2):
                    act.wait_ge(mid_done[half], g + 1)
                    for f in range(4):
                        n = half * 4 + f
                        last = act.activation(mid[:, n * P:(n + 1) * P], mid_ps[half][:, f * P:(f + 1) * P],
                                              ACT.Gelu, bias=b1[:, n:n + 1])
                    last.then_inc(mid_ready[half], 1)

            pipeline(act, [(1, copy_ln), (2, gelu)])

        @block.tensor
        def _(pe):
            pe.wait_ge(w_in, 16 * 7)

            def attend(i, j):
                g = i * R + j
                pe.wait_ge(loaded[j], 48 * i + 48)
                once(pe, h_ready, g)
                for k in range(KT):
                    last = pe.matmul(h_ps[:, 0:D], qT_in[:, j, k * P:(k + 1) * P], folded[:, k, :],
                                     start=(k == 0), stop=(k == KT - 1))
                last.then_inc(h_done, 1)

            def turn(i, j):
                g = i * R + j
                pe.wait_ge(ln_ready, g + 1)
                once(pe, lnT_ready, g)
                for k in range(KT):
                    last = pe.transpose(ln_ps[:, k * P:(k + 1) * P], ln[:, j, k * P:(k + 1) * P], ident)
                last.then_inc(ln_turned, 1)

            def mlp_in(i, j):
                g = i * R + j
                pe.wait_ge(lnT_ready, g + 1)
                for half in range(2):
                    once(pe, mid_ready[half], g)
                    for f in range(4):
                        n = half * 4 + f
                        for k in range(KT):
                            last = pe.matmul(mid_ps[half][:, f * P:(f + 1) * P], w1[:, k, n * P:(n + 1) * P],
                                             lnT[:, j, k * P:(k + 1) * P], start=(k == 0), stop=(k == KT - 1))
                    last.then_inc(mid_done[half], 1)

            def mlp_out(i, j):
                g = i * R + j
                once(pe, mixed_ready, g)
                for half in range(2):
                    pe.wait_ge(mid_ready[half], g + 1)
                    for f in range(4):
                        n = half * 4 + f
                        last = pe.matmul(y_ps[:, 0:D], mid[:, n * P:(n + 1) * P], w2[:, n, :],
                                         start=(n == 0), stop=(n == FT - 1))
                last.then_inc(y_done, 1)

            pipeline(pe, [(0, attend), (1, turn), (2, mlp_in), (3, mlp_out)])


def second_graph(nc, A, hold, bank, const, acc, xn3T, combine, mixed_d, big_k, big_v):
    ident = const[:, C_ID:C_ID + P]
    with Stage(nc) as ctx:
        S = Scope(nc, ctx, "g2")
        w, w_r = S.sb("w", [P, KT, D]), S.sb("w_r", [P, KT, E])
        mixed, sums, sumsT, x3, xn3, nT = (S.sb(n, [P, R, D]) for n in ("mixed", "sums", "sumsT", "x3", "xn3", "nT"))
        pr, pick, rank = S.sb("pr", [P, T, E]), S.sb("pick", [P, 2, T, E]), S.sb("rank", [P, T, E])
        most = S.sb("most", [P, 3, T])
        w_in, ew_in, loaded = S.sem("w_in"), S.sem("ew_in"), S.sems("loaded")
        r_step, c_step, shifted, pr_exp = S.sem("r_step"), S.sem("c_step"), S.sem("shifted"), S.sem("pr_exp")
        sums_ready, sums_turned, sumsT_ready, g_done, x3_ready, xn3_ready, xn3_turned, nT_ready, xn3T_ready, logits, \
            pr_ready = (S.sem(n) for n in (
                "sums_ready", "sums_turned", "sumsT_ready", "g_done", "x3_ready", "xn3_ready", "xn3_turned", "nT_ready",
                "xn3T_ready", "logits", "pr_ready"))
        norm = Norm(nc, ctx, "g2_norm", hold, const[:, C_POW:C_POW + 1])
        block = S.block()
        s_ps, g_ps, n_ps, l_ps = bank[0:2], bank[2:4], bank[4:6], bank[6:8]

        @block.sync
        def _(sp):
            sp.dma_start(w[:, :, :], weights(A["L1_gnn_weight"])).then_inc(w_in, 16)
            sp.dma_start(w_r[:, :, :], weights(A["L1_ffn_router_wT"])).then_inc(w_in, 16)

            def load(i, j):
                g = i * R + j
                once(sp, x3_ready, g - R + 1, hold)
                sp.dma_start(mixed[:, j, :], rows_of(mixed_d, g)).then_inc(loaded[j], 16)

            pipeline(sp, [(0, load)])
            ew1, ew2 = expert_weights(big_k, big_v)
            for e in range(E):
                sp.dma_start(ew1[:, e, :, :], weights(A["L1_ffn_w1"][e, :, :])).then_inc(ew_in, 16)
                sp.dma_start(ew2[:, e, :, :], weights(A["L1_ffn_w2"][e, :, :])).then_inc(ew_in, 16)
            sp.wait_ge(ew_in, 32 * E)

        @block.gpsimd
        def _(pool):
            pipeline(pool, [(0, lambda i, j: norm.root(pool, i * R + j))])

        @block.vector
        def _(dve):
            order = const[:, C_ORDER:C_ORDER + E].unsqueeze(1).broadcast_to([P, T, E])

            def cut(i, j):
                g = i * R + j
                once(dve, sums_turned, g - R + 1)
                dve.tensor_copy(sums[:, j, :], tile_of(acc, g)[:, 0:D]).then_inc(sums_ready, 1)

            def residual(i, j):
                g = i * R + j
                dve.wait_ge(loaded[j], 16 * i + 16)
                dve.wait_ge(g_done, g + 1)
                dve.scalar_tensor_tensor(out=x3[:, j, :], in0=g_ps[j % 2][:, 0:D], scalar=0.0, in1=mixed[:, j, :],
                                         op0=ALU.max, op1=ALU.add).then_inc(x3_ready, 1)
                dve.wait_ge(x3_ready, g + 1)
                norm.find(dve, x3[:, j, :], g)

            def norm_x(i, j):
                g = i * R + j
                once(dve, xn3_turned, g - R + 1)
                norm.apply(dve, xn3[:, j, :], x3[:, j, :], g).then_inc(xn3_ready, 1)
                dve.wait_ge(xn3_ready, g + 1)
                dve.tensor_tensor(tile_of(acc, g)[:, 0:D], x3[:, j, :], xn3[:, j, :], ALU.add).then_inc(c_step, 1)

            pipeline(dve, [(2, norm_x), (0, cut), (1, residual)])

            link = Steps(dve, r_step)

            def wide(x):
                return x.unsqueeze(2).broadcast_to([P, T, E])

            dve.wait_ge(pr_ready, T)
            link(dve.tensor_reduce(most[:, 0, :], pr[:, :, :], AX, ALU.max))
            dve.tensor_tensor(pr[:, :, :], pr[:, :, :], wide(most[:, 0, :]), ALU.subtract).then_inc(shifted, 1)
            dve.wait_ge(pr_exp, 1)
            dve.wait_ge(shifted, 1)
            link(dve.tensor_reduce(most[:, 0, :], pr[:, :, :], AX, ALU.add))
            link(dve.reciprocal(most[:, 0, :], most[:, 0, :]))
            link(dve.tensor_tensor(pr[:, :, :], pr[:, :, :], wide(most[:, 0, :]), ALU.mult))
            for n in range(2):
                link(dve.tensor_reduce(most[:, n, :], pr[:, :, :], AX, ALU.max))
                link(dve.tensor_tensor(pick[:, n], pr[:, :, :], wide(most[:, n, :]), ALU.is_equal))
                link(dve.tensor_tensor(rank[:, :, :], pick[:, n], order, ALU.mult))
                link(dve.tensor_reduce(most[:, 2, :], rank[:, :, :], AX, ALU.max))
                link(dve.tensor_tensor(pick[:, n], rank[:, :, :], wide(most[:, 2, :]), ALU.is_equal))
                if n == 0:
                    link(dve.scalar_tensor_tensor(out=pr[:, :, :], in0=pick[:, 0], scalar=-4.0, in1=pr[:, :, :],
                                                  op0=ALU.mult, op1=ALU.add))
            link(dve.tensor_tensor(most[:, 2, :], most[:, 0, :], most[:, 1, :], ALU.add))
            link(dve.tensor_scalar(most[:, 2, :], most[:, 2, :], 1e-12, None, ALU.max))
            link(dve.reciprocal(most[:, 2, :], most[:, 2, :]))
            for n in range(2):
                link(dve.tensor_tensor(most[:, n, :], most[:, n, :], most[:, 2, :], ALU.mult))
                link(dve.tensor_tensor(pick[:, n], pick[:, n], wide(most[:, n, :]), ALU.mult))
            link(dve.tensor_tensor(combine[:, :, :], pick[:, 0], pick[:, 1], ALU.add))

        @block.scalar
        def _(act):
            def copy_sums(i, j):
                g = i * R + j
                act.wait_ge(sums_turned, g + 1)
                once(act, g_done, g - R + 1)
                act.activation(sumsT[:, j, :], s_ps[j % 2][:, 0:D], ACT.Copy).then_inc(sumsT_ready, 1)

            def copy_n(i, j):
                g = i * R + j
                act.wait_ge(xn3_turned, g + 1)
                once(act, logits, g - R + 1)
                act.activation(nT[:, j, :], n_ps[j % 2][:, 0:D], ACT.Copy).then_inc(nT_ready, 1)
                act.activation(xn3T[:, :, bass.ds(g * P, P)], n_ps[j % 2][:, 0:D].rearrange("p (k n) -> p k n", k=KT),
                               ACT.Copy).then_inc(xn3T_ready, 1)

            def copy_logits(i, j):
                g = i * R + j
                act.wait_ge(logits, g + 1)
                act.activation(tile_of(pr, g), l_ps[j % 2][:, 0:E], ACT.Copy).then_inc(pr_ready, 1)

            pipeline(act, [(0, copy_sums), (2, copy_n), (3, copy_logits)])
            act.wait_ge(shifted, 1)
            act.activation(pr[:, :, :], pr[:, :, :], ACT.Exp).then_inc(pr_exp, 1)

        @block.tensor
        def _(pe):
            pe.wait_ge(w_in, 32)

            def turn_sums(i, j):
                g = i * R + j
                pe.wait_ge(sums_ready, g + 1)
                once(pe, sumsT_ready, g - bank_gap(j) + 1)
                for k in range(KT):
                    last = pe.transpose(s_ps[j % 2][:, k * P:(k + 1) * P], sums[:, j, k * P:(k + 1) * P], ident)
                last.then_inc(sums_turned, 1)

            def project(i, j):
                g = i * R + j
                pe.wait_ge(sumsT_ready, g + 1)
                once(pe, x3_ready, g - bank_gap(j) + 1)
                for k in range(KT):
                    last = pe.matmul(g_ps[j % 2][:, 0:D], sumsT[:, j, k * P:(k + 1) * P], w[:, k, :],
                                     start=(k == 0), stop=(k == KT - 1))
                last.then_inc(g_done, 1)

            def turn_n(i, j):
                g = i * R + j
                pe.wait_ge(xn3_ready, g + 1)
                once(pe, xn3T_ready, g - bank_gap(j) + 1)
                for k in range(KT):
                    last = pe.transpose(n_ps[j % 2][:, k * P:(k + 1) * P], xn3[:, j, k * P:(k + 1) * P], ident)
                last.then_inc(xn3_turned, 1)

            def score(i, j):
                g = i * R + j
                pe.wait_ge(nT_ready, g + 1)
                once(pe, pr_ready, g - bank_gap(j) + 1)
                for k in range(KT):
                    last = pe.matmul(l_ps[j % 2][:, 0:E], nT[:, j, k * P:(k + 1) * P], w_r[:, k, :],
                                     start=(k == 0), stop=(k == KT - 1))
                last.then_inc(logits, 1)

            pipeline(pe, [(2, turn_n), (0, turn_sums), (1, project), (3, score)])


def expert_weights(big_k, big_v):
    return (big_k[:, 0:E * KT * D].rearrange("p (e k n) -> p e k n", e=E, k=KT),
            big_v[:, :, :].rearrange("p t n -> p (t n)")[:, 0:E * KT * D].rearrange("p (e k n) -> p e k n", e=E, k=KT))


def second_experts(nc, A, hold, bank, const, acc, xn3T, combine, big_k, big_v, out):
    FT = D // P
    with Stage(nc) as ctx:
        S = Scope(nc, ctx, "e2")
        w1, w2 = expert_weights(big_k, big_v)
        b1 = S.sb("b1", [P, E, FT])
        b2, combT = S.sb("b2", [E, D]), S.sb("combT", [E, NP])
        mid = S.sb("mid", [P, E, D])
        w_in = S.sem("w_in")
        stored = S.sem("stored")
        mid_done, mid_ready, y_done, added, comb_turned, combT_ready, b2_done, b2_added = (S.sem(n) for n in (
            "mid_done", "mid_ready", "y_done", "added", "comb_turned", "combT_ready", "b2_done", "b2_added"))
        block = S.block()

        @block.sync
        def _(sp):
            sp.dma_start(b1[:, :, :], A["L1_ffn_b1"]).then_inc(w_in, 16)
            sp.dma_start(b2[:, :], A["L1_ffn_b2"]).then_inc(w_in, 16)
            with sp.Fori(0, T) as g:
                hold(sp, added, (g + 1) * E)
                sp.dma_start(rows_of(out, g), tile_of(acc, g)[:, 0:D]).then_inc(stored, 16)
            sp.wait_ge(stored, 16 * T)

        @block.tensor
        def _(pe):
            for t in range(T):
                last = pe.transpose(bank[t // 4][0:E, t % 4 * P:(t % 4 + 1) * P], combine[:, t, :], const[:, C_ID:C_ID + P])
            last.then_inc(comb_turned, 1)
            pe.wait_ge(w_in, 32)
            pe.wait_ge(combT_ready, 1)
            for n in range(-(-T // 2)):
                once(pe, b2_added, n - 1)
                for t in range(2 * n, min(2 * n + 2, T)):
                    last = pe.matmul(bank[n % 2][:, (t - 2 * n) * D:(t - 2 * n + 1) * D], combT[:, t * P:(t + 1) * P], b2[:, :],
                                     start=True, stop=True)
                last.then_inc(b2_done, 1)
            pe.wait_ge(b2_added, -(-T // 2))

            def expert_in(g, e):
                n = g * E + e
                once(pe, mid_ready, n - 1)
                for f in range(FT):
                    for k in range(KT):
                        last = pe.matmul(bank[e % 2][:, f * P:(f + 1) * P], w1[:, e, k, f * P:(f + 1) * P],
                                         xn3T[:, k, bass.ds(g * P, P)], start=(k == 0), stop=(k == KT - 1))
                last.then_inc(mid_done, 1)

            def expert_out(g, e):
                n = g * E + e
                pe.wait_ge(mid_ready, n + 1)
                once(pe, added, n - 1)
                for f in range(FT):
                    last = pe.matmul(bank[2 + e % 2][:, 0:D], mid[:, e, f * P:(f + 1) * P], w2[:, e, f, :],
                                     start=(f == 0), stop=(f == FT - 1))
                last.then_inc(y_done, 1)

            pipeline(pe, [(0, expert_in), (1, expert_out)], T, E)

        @block.scalar
        def _(act):
            act.wait_ge(w_in, 32)
            act.wait_ge(comb_turned, 1)
            for b in range(-(-T // 4)):
                width = min(4 * P, (T - 4 * b) * P)
                last = act.activation(combT[:, 4 * b * P:4 * b * P + width], bank[b][0:E, 0:width], ACT.Copy)
            last.then_inc(combT_ready, 1)

            def gelu(g, e):
                n = g * E + e
                act.wait_ge(mid_done, n + 1)
                once(act, y_done, n - E + 1)
                for f in range(FT):
                    last = act.activation(mid[:, e, f * P:(f + 1) * P], bank[e % 2][:, f * P:(f + 1) * P], ACT.Gelu,
                                          bias=b1[:, e, f:f + 1])
                last.then_inc(mid_ready, 1)

            pipeline(act, [(0, gelu)], T, E)

        @block.vector
        def _(dve):
            for n in range(-(-T // 2)):
                to = acc[:, 2 * n:min(2 * n + 2, T), 0:D]
                dve.wait_ge(b2_done, n + 1)
                dve.tensor_tensor(to, bank[n % 2][:, 0:to.shape[1] * D].rearrange("p (t n) -> p t n", n=D), to, ALU.add)\
                   .then_inc(b2_added, 1)
            dve.wait_ge(b2_added, -(-T // 2))

            def add(g, e):
                n = g * E + e
                dve.wait_ge(y_done, n + 1)
                once(dve, added, n)
                to = tile_of(acc, g)[:, 0:D]
                dve.scalar_tensor_tensor(out=to, in0=bank[2 + e % 2][:, 0:D], scalar=tile_of(combine, g)[:, e:e + 1],
                                         in1=to, op0=ALU.mult, op1=ALU.add).then_inc(added, 1)

            pipeline(dve, [(0, add)], T, E)


def laid_out(inputs):

    a = {k: np.asarray(v) for k, v in inputs.items()}

    def rows(x):
        y = np.zeros((NP, x.shape[1]), x.dtype)
        y[:N_NODES] = x[:N_NODES]
        return y

    def edges(x, fill):
        y = np.full((NC * P,), fill, x.dtype)
        y[:N_EDGES] = x
        return y.reshape(NC, P)

    def column(x):
        return np.ascontiguousarray(x.reshape(-1, P).T)

    def four(w):
        y = np.zeros((P, P), w.dtype)
        for n in range(4):
            y[32 * n:32 * n + 32, 32 * n:32 * n + 32] = w
        return y

    const = np.zeros((P, C_N), np.float32)
    const[:, C_ID:C_ID + P] = np.eye(P)
    const[:, C_BD:C_BD + P] = np.kron(np.eye(4), np.ones((32, 32)))
    const[:, C_IOTA:C_IOTA + P] = np.arange(P)
    const[:, C_P] = np.arange(P)
    const[:, C_STEP:C_STEP + SB] = np.arange(P)[:, None] + RB * np.arange(SB)
    const[:, C_TILE:C_TILE + T] = np.arange(T)
    const[:, C_CHUNK:C_CHUNK + NC] = np.arange(NC)
    const[:, C_ONE:C_ONE + P] = 1
    const[:, C_POW] = -0.5
    const[:, C_ORDER:C_ORDER + E] = E - np.arange(E)
    return {
        "const": const,
        "x": rows(a["x"]),
        "sentT": np.ascontiguousarray(rows(a["L0_gnn_sent_repr"]).T),
        "L0_gnn_W_src": a["L0_gnn_W_src"], "L0_gnn_W_dst": a["L0_gnn_W_dst"],
        "L0_gnn_attn_l": a["L0_gnn_attn_l"].reshape(1, D), "L0_gnn_attn_r": a["L0_gnn_attn_r"].reshape(1, D),
        "L0_mix_W_qT": np.ascontiguousarray(a["L0_mix_W_qkv"][:, 0:128].T),
        "L0_mix_W_k": np.ascontiguousarray(a["L0_mix_W_qkv"][:, 128:256]),
        "L0_mix_W_v": np.ascontiguousarray(a["L0_mix_W_qkv"][:, 256:384]),
        "L0_mix_W_out": a["L0_mix_W_out"],
        "L0_gnn_w1": a["L0_gnn_w1"], "L0_gnn_w2": a["L0_gnn_w2"], "L0_gnn_b1": column(a["L0_gnn_b1"]),
        "L0_ffn_Wr": a["L0_ffn_Wr"], "L0_ffn_W1": a["L0_ffn_W1"], "L0_ffn_W2": a["L0_ffn_W2"],
        "L0_ffn_b1": np.ascontiguousarray(a["L0_ffn_b1"].reshape(E, -1, P).transpose(0, 2, 1)),
        "L0_ffn_b2": a["L0_ffn_b2"],
        **{k: a[k].reshape(1, -1) for k in ("L0_gnn_gat_bias", "L0_gnn_b2", "L0_mix_b_out", "L0_ffn_br",
                                            "L0_ffn_gamma", "L0_ffn_beta", "L1_mix_bo", "L1_mix_b2")},
        **{k: column(a[k]) for k in ("L1_mix_ln1_w", "L1_mix_ln1_b", "L1_mix_bx", "L1_mix_b1", "L1_mix_ln2_w",
                                     "L1_mix_ln2_b")},
        **{k + "T": np.ascontiguousarray(a[k].T) for k in ("L1_mix_Wx", "L1_mix_Wo", "L1_mix_W1", "L1_mix_W2",
                                                           "L1_ffn_router_w")},
        **{k + "T4": four(a[k].T) for k in ("L1_mix_Wq", "L1_mix_Wk", "L1_mix_Wv")},
        "L1_gnn_weight": a["L1_gnn_weight"], "L1_ffn_w1": a["L1_ffn_w1"], "L1_ffn_w2": a["L1_ffn_w2"],
        "L1_ffn_b1": np.ascontiguousarray(a["L1_ffn_b1"].reshape(E, -1, P).transpose(2, 0, 1)),
        "L1_ffn_b2": a["L1_ffn_b2"],
        "src": edges(a["src"], 0),
        "dst": edges(a["dst"], PAD_DST),
        "dst_first": np.ascontiguousarray(edges(a["dst"], PAD_DST)[:, 0].reshape(1, NC)),
        "ew": edges(a["edge_weight"], 0),
    }


def kernel(**inputs):
    import concourse.bacc as bacc
    from concourse.bass_utils import run_bass_kernel_spmd

    arrays = laid_out(inputs)
    nc = bacc.Bacc("TRN2", target_bir_lowering=False, num_devices=1)
    A = {k: nc.dram_tensor(f"in_{k}", v.shape, mybir.dt.from_np(v.dtype), kind="ExternalInput").ap()
         for k, v in arrays.items()}
    out = nc.dram_tensor("out", [NP, D], F32, kind="ExternalOutput").ap()
    program(nc, A, out)
    r = run_bass_kernel_spmd(nc, [{f"in_{k}": v for k, v in arrays.items()}], core_ids=[0])
    return r.results[0]["out"][:N_NODES]
```

```python
from contextlib import ExitStack

import numpy as np
import concourse.bass as bass
from concourse import mybir

ALU = mybir.AluOpType
ACT = mybir.ActivationFunctionType
AX = mybir.AxisListType.X
F32 = mybir.dt.float32
BF16 = mybir.dt.bfloat16
I32 = mybir.dt.int32
U32 = mybir.dt.uint32

P = 128
N_NODES = 3125
D = 256
KT = D // P
T = -(-N_NODES // P)
NP = T * P
R = 5
NI = T // R
N_EDGES = 53125
NC = -(-N_EDGES // P)
SB = 4
W_AGG = 16
NS = -(-(NC + T - 1) // (SB * W_AGG)) * SB * W_AGG
RB = NS // SB
H = 4
DH = D // H
DW = DH + 1
DF = 512
HID = 1024
E = 8
PAD_DST = 1 << 20
BIG = 1.0e30
EPS = 1.0e-5
assert T % R == 0 and NS == RB * SB and NS % W_AGG == 0 and RB <= P

C_ID, C_BD, C_IOTA = 0, 128, 256
C_P, C_STEP, C_TILE, C_CHUNK, C_ONE, C_ZERO = 384, 385, 389, 414, 414 + NC, 414 + NC + P
C_POW = C_ZERO + P
C_ORDER = C_POW + 1
C_N = C_ORDER + E


class Stage(ExitStack):

    def __init__(self, nc):
        super().__init__()
        self.nc, self.semaphores = nc, []

    def semaphore(self, name):
        self.semaphores.append(self.nc.alloc_semaphore(name))
        return self.semaphores[-1]

    def __exit__(self, *failure):
        super().__exit__(*failure)
        self.nc.clear_and_free_semaphores(self.semaphores)
        self.nc.all_engine_barrier()


class Steps:

    def __init__(self, eng, sem, i=None, per=0, base=0):
        self.eng, self.sem, self.i, self.per, self.base, self.k = eng, sem, i, per, base, 0

    def at(self):
        k = self.base + self.k
        return k if self.i is None else self.i * self.per + k

    def __call__(self, ins):
        self.k += 1
        ins.then_inc(self.sem, 1)
        self.eng.wait_ge(self.sem, self.at())

    def end(self):
        assert self.i is None or self.per == self.k, self.k


def pipeline(eng, stages, turns=NI, width=R, first=1, last=None):
    longest = max(lag for lag, _ in stages)
    first = max(first, 1 - (-longest // width))
    last = turns if last is None else last
    for n in range(first * width):
        for lag, stage in stages:
            if n >= lag:
                stage((n - lag) // width, (n - lag) % width)
    with eng.Fori(first, last) as i:
        for j in range(width):
            for lag, stage in stages:
                stage(i + (j - lag) // width, (j - lag) % width)
    for n in range(last * width, turns * width + longest):
        for lag, stage in stages:
            if n - lag < turns * width:
                stage((n - lag) // width, (n - lag) % width)


def once(eng, sem, n, hold=None):
    if isinstance(n, int) and n <= 0:
        return
    if hold is None:
        eng.wait_ge(sem, n)
    else:
        hold(eng, sem, n)


def tiles_of(nc, eng, step_tile, n, count):
    return nc.values_load_multi_w_load_instructions(
        step_tile[0:1, bass.ds(n, count)], engines=[eng.engine], min_val=0, max_val=T - 1,
        skip_runtime_bounds_check_because="edge_schedule keeps every tile within 0 and T - 1")[1]


def bank_gap(j, n=2):
    return n if j >= n else R - (R - 1 - j) // n * n


class Norm:

    def __init__(self, nc, ctx, name, hold, power):
        self.power = power
        self.stats = ctx.enter_context(nc.sbuf_tensor(f"{name}_stats", [P, R, 6], F32))
        self.mv = ctx.enter_context(nc.sbuf_tensor(f"{name}_mv", [P, R, 2], F32))
        self.rstd = ctx.enter_context(nc.sbuf_tensor(f"{name}_rstd", [P, R, 1], F32))
        self.found = ctx.semaphore(f"{name}_found")
        self.rooted = ctx.semaphore(f"{name}_rooted")
        self.step = ctx.semaphore(f"{name}_step")
        self.hold = hold

    def find(self, dve, x, n, j=0):
        dve.bn_stats(self.stats[:, j, :], x).then_inc(self.step, 1)
        self.hold(dve, self.step, n * 2 + 1)
        dve.bn_aggr(self.mv[:, j, :], self.stats[:, j, :]).then_inc(self.step, 1)
        dve.wait_ge(self.step, n * 2 + 2)
        dve.tensor_scalar(self.mv[:, j, 1:2], self.mv[:, j, 1:2], EPS, None, ALU.add).then_inc(self.found, 1)

    def root(self, pool, n, j=0):
        self.hold(pool, self.found, n + 1)
        pool.tensor_tensor(self.rstd[:, j, :], self.mv[:, j, 1:2], self.power, ALU.pow).then_inc(self.rooted, 1)

    def apply(self, dve, out, x, n, j=0):
        dve.wait_ge(self.rooted, n + 1)
        dve.wait_ge(self.found, n + 1)
        return dve.tensor_scalar(out, x, self.mv[:, j, 0:1], self.rstd[:, j, 0:1], ALU.subtract, ALU.mult)


def program(nc, A, out):
    with ExitStack() as top:
        def sb(name, shape, dt=F32, ctx=top):
            return ctx.enter_context(nc.sbuf_tensor(name, shape, dt))

        def dram(name, shape, dt=F32):
            return nc.dram_tensor(name, shape, dt, kind="Internal").ap()

        passed = top.enter_context(nc.semaphore("passed"))

        def hold(eng, sem, value):
            eng.wait_ge(sem, value)
            eng.sem_inc(passed, 1)

        bank = [top.enter_context(nc.psum_tensor(f"bank{i}", [P, 512], F32)) for i in range(8)]

        const = sb("const", [P, C_N])

        step_tile = sb("step_tile", [1, NS], I32)
        src_lane = sb("src_lane", [P, NS + W_AGG], I32)
        dst_lane = sb("dst_lane", [P, NS])
        ew_lane = sb("ew_lane", [P, NS])
        hi_lane = sb("hi_lane", [P, NS])
        acc = sb("acc", [P, T, D + H])
        big_k = sb("big_k", [P, KT * NP])
        big_v = sb("big_v", [P, T, D])
        combine = sb("combine", [P, T, 8])

        src_lo_d = dram("src_lo_d", [NS, P], BF16)
        dst_lo_d = dram("dst_lo_d", [NS, P], BF16)
        feat_d = dram("feat_d", [NP, H * DW])
        xn_d = dram("xn_d", [NP, D])
        xnT_d = dram("xnT_d", [T, P, D])
        x1_d = dram("x1_d", [NP, D])
        xn1_d = dram("xn1_d", [NP, D])
        x2_d = dram("x2_d", [NP, D])
        xn2_d = dram("xn2_d", [NP, D])
        qT_d = dram("qT_d", [T, P, D])
        mixed_d = dram("mixed_d", [NP, D])

        dst_rows = sb("dst_rows", [RB, SB, P])
        edge_schedule(nc, A, dst_rows, bank, const, step_tile, src_lane, dst_lane, ew_lane, hi_lane,
                      src_lo_d, dst_lo_d)
        scores = sb("scores", [P, 2, T, H])
        first_projections(nc, A, hold, bank, const, big_k, big_v, scores, feat_d, xn_d, xnT_d)
        fold = sb("fold", [P, KT, D])
        with ExitStack() as held:
            weight = sb("edge_exp", [P, NS, H], ctx=held)
            with ExitStack() as brief:
                el_er = sb("el_er", [P, 2, NS, H], ctx=brief)
                er = sb("er", [P, NS, H], ctx=brief)
                edge_lookup(nc, A, hold, bank, const, scores, el_er, er, hi_lane, step_tile, src_lo_d, dst_lo_d)
                segment_maximum(nc, bank, const, dst_rows, el_er)
                edge_exp(nc, el_er, er, weight)
            aggregate(nc, A, hold, "a0", bank, const, acc, step_tile, src_lane, dst_lane, feat_d, weight, None,
                      first_mixer(nc, A, bank, const, big_k, big_v, fold))
        with ExitStack() as held:
            xnT = sb("xn1T", [P, KT, NP], ctx=held)
            first_graph_mlp(nc, A, hold, bank, const, acc, fold, xnT, A["x"], xn_d, xnT_d, x1_d, xn1_d)
            w1 = sb("top_w1", [P, 2, KT, DF], ctx=held)
            w2 = sb("top_w2", [P, 2, DF // P, D], ctx=held)
            b1 = sb("top_b1", [P, 2, DF // P], ctx=held)
            bias = sb("top_bias", [P, D], ctx=held)
            first_router(nc, A, hold, bank, const, xnT, w1, w2, b1, bias)
            first_experts(nc, A, hold, bank, const, xnT, w1, w2, b1, bias, big_k, big_v,
                          x1_d, xn1_d, x2_d, xn2_d, qT_d)
        folded = sb("folded", [P, KT, D])
        second_mixer(nc, A, hold, bank, const, big_k, big_v, folded)
        aggregate(nc, A, hold, "a1", bank, const, acc, step_tile, src_lane, dst_lane, xn2_d, None, ew_lane,
                  mixer_mlp(nc, A, hold, bank, const, folded, x2_d, xn2_d, qT_d, mixed_d))
        with ExitStack() as held:
            xnT = sb("xn3T", [P, KT, NP], ctx=held)
            second_graph(nc, A, hold, bank, const, acc, xnT, combine, mixed_d, big_k, big_v)
            second_experts(nc, A, hold, bank, const, acc, xnT, combine, big_k, big_v, out)


def edge_schedule(nc, A, rows, bank, const, step_tile, src_lane, dst_lane, ew_lane, hi_lane, src_lo_d, dst_lo_d):
    with Stage(nc) as ctx:
        def sb(name, shape, dt=F32):
            return ctx.enter_context(nc.sbuf_tensor(name, shape, dt))

        def sem(name):
            return ctx.semaphore(name)

        first = sb("es_first", [1, NC], I32)
        first_t = sb("es_first_t", [1, NC], I32)
        key = sb("es_key", [1, NC])
        below = sb("es_below", [RB, NC])
        count = sb("es_count", [RB, SB])
        chunk = sb("es_chunk", [RB, SB], I32)
        tile_f = sb("es_tile_f", [RB, SB])
        base = sb("es_base", [RB, SB])
        src_i = sb("es_src_i", [RB, SB, P], I32)
        dst_i = sb("es_dst_i", [RB, SB, P], I32)
        ew_r = sb("es_ew_r", [RB, SB, P])
        hi_i = sb("es_hi_i", [RB, SB, P], I32)
        lo_i = sb("es_lo_i", [RB, SB, P], I32)
        src_f = sb("es_src_f", [RB, SB, P])
        hi_f = sb("es_hi_f", [RB, SB, P])
        local = sb("es_local", [RB, SB, P])
        lo_b = sb("es_lo_b", [RB, SB, P], BF16)
        loc_b = sb("es_loc_b", [RB, SB, P], BF16)

        const_in, first_in = sem("es_const_in"), sem("es_first_in")
        dve_step, key_ready, key_spread = sem("es_dve_step"), sem("es_key_ready"), sem("es_key_spread")
        chunk_ready, tile_ready, tile_row = sem("es_chunk_ready"), sem("es_tile_ready"), sem("es_tile_row")
        rows_in = [sem(f"es_rows_in{k}") for k in range(3)]
        rows_ready, lanes_ready, stored, lo_ready = (sem("es_rows_ready"), sem("es_lanes_ready"),
                                                     sem("es_stored"), sem("es_lo_ready"))
        block = ctx.enter_context(nc.Block())

        @block.sync
        def _(sp):
            sp.dma_start(const[:, :], A["const"]).then_inc(const_in, 16)
            sp.dma_start(first[:, :], A["dst_first"]).then_inc(first_in, 16)
            sp.wait_ge(lo_ready, 1)
            sp.dma_start(src_lo_d.rearrange("(b p) l -> p b l", b=SB), lo_b[:, :, :]).then_inc(stored, 16)
            sp.dma_start(dst_lo_d.rearrange("(b p) l -> p b l", b=SB), loc_b[:, :, :]).then_inc(stored, 16)
            sp.wait_ge(stored, 32)

        @block.gpsimd
        def _(pool):
            pool.wait_ge(chunk_ready, 1)
            for b in range(SB):
                at = bass.IndirectOffsetOnAxis(ap=chunk[:, b:b + 1], axis=0)
                for k, (dst, src) in enumerate(((dst_i, A["dst"]), (src_i, A["src"]), (ew_r, A["ew"]))):
                    pool.indirect_dma_start(dst[:, b, :], None, src, at).then_inc(rows_in[k], 16)

        @block.vector
        def _(dve):
            link = Steps(dve, dve_step)
            dve.wait_ge(const_in, 16)
            dve.wait_ge(first_in, 16)
            link(dve.tensor_single_scalar(first_t[:, :], first[:, :], 7, ALU.arith_shift_right))
            link(dve.tensor_copy(key[:, :], first_t[:, :]))
            dve.tensor_tensor(key[:, :], key[:, :], const[0:1, C_CHUNK:C_CHUNK + NC], ALU.add).then_inc(key_ready, 1)
            dve.wait_ge(key_spread, 1)
            for b in range(SB):
                link(dve.tensor_scalar(below[:, 1:NC], bank[0][0:RB, 1:NC], const[0:RB, C_STEP + b:C_STEP + b + 1],
                                       None, ALU.is_le))
                link(dve.tensor_reduce(count[:, b:b + 1], below[:, 1:NC], AX, ALU.add))
            dve.tensor_copy(chunk[:, :], count[:, :]).then_inc(chunk_ready, 1)
            dve.tensor_tensor(tile_f[:, :], const[0:RB, C_STEP:C_STEP + SB], count[:, :], ALU.subtract)\
               .then_inc(tile_ready, 1)
            dve.wait_ge(tile_ready, 1)
            link(dve.tensor_scalar(base[:, :], tile_f[:, :], float(P), None, ALU.mult))
            dve.wait_ge(tile_row, 1)
            link(dve.tensor_scalar(step_tile[:, :], bank[1][0:1, 0:NS], 0.0, float(T - 1), ALU.max, ALU.min))
            dve.wait_ge(rows_in[0], 16 * SB)
            link(dve.tensor_copy(rows[:, :, :], dst_i[:, :, :]))
            link(dve.tensor_tensor(local[:, :, :], rows[:, :, :],
                                   base[:, :].unsqueeze(2).broadcast_to([RB, SB, P]), ALU.subtract))
            link(dve.tensor_copy(loc_b[:, :, :], local[:, :, :]))
            dve.wait_ge(rows_in[1], 16 * SB)
            link(dve.tensor_copy(src_f[:, :, :], src_i[:, :, :]))
            link(dve.tensor_single_scalar(hi_i[:, :, :], src_i[:, :, :], 7, ALU.arith_shift_right))
            link(dve.tensor_single_scalar(lo_i[:, :, :], src_i[:, :, :], P - 1, ALU.bitwise_and))
            dve.tensor_copy(lo_b[:, :, :], lo_i[:, :, :]).then_inc(lo_ready, 1)
            dve.tensor_copy(hi_f[:, :, :], hi_i[:, :, :]).then_inc(rows_ready, 1)
            dve.wait_ge(lanes_ready, 4)
            for b, dst in ((2, src_lane), (3, dst_lane), (4, ew_lane), (5, hi_lane)):
                link(dve.tensor_copy(dst[:, 0:NS], bank[b][:, 0:NS]))
            link(dve.memset(src_lane[:, NS:NS + W_AGG], 0))

        @block.tensor
        def _(pe):
            pe.wait_ge(const_in, 16)
            pe.wait_ge(key_ready, 1)
            pe.matmul(bank[0][:, 0:NC], const[0:1, C_ONE:C_ONE + P], key[:, :], start=True, stop=True)\
              .then_inc(key_spread, 1)
            pe.wait_ge(tile_ready, 1)
            for b in range(SB):
                last = pe.matmul(bank[1][0:1, b * RB:(b + 1) * RB], tile_f[:, b:b + 1], const[0:RB, C_ID:C_ID + RB],
                                 start=True, stop=True)
            last.then_inc(tile_row, 1)
            pe.wait_ge(rows_in[2], 16 * SB)
            pe.wait_ge(rows_ready, 1)
            for n, src in ((2, src_f), (3, local), (4, ew_r), (5, hi_f)):
                for b in range(SB):
                    last = pe.transpose(bank[n][:, b * RB:(b + 1) * RB], src[:, b, :], const[0:RB, C_ID:C_ID + RB])
                last.then_inc(lanes_ready, 1)


def first_projections(nc, A, hold, bank, const, big_k, big_v, scores, feat_d, xn_d, xnT_d):
    ident = const[:, C_ID:C_ID + P]
    HD = 128
    with Stage(nc) as ctx:
        def sb(name, shape, dt=F32):
            return ctx.enter_context(nc.sbuf_tensor(name, shape, dt))

        def sem(name):
            return ctx.semaphore(name)

        w_feat = sb("p1_w_feat", [P, KT, D + H])
        w_v = sb("p1_w_v", [P, KT, HD + H])
        w_k = sb("p1_w_k", [P, KT, HD])
        w_dst = sb("p1_w_dst", [P, KT, D])
        attn = sb("p1_attn", [P, 2, D])
        prod = sb("p1_prod", [P, KT, D])
        x_in = sb("p1_x_in", [P, R, D])
        sent_in = sb("p1_sent_in", [P, R, KT, P])
        xn = sb("p1_xn", [P, R, D])
        xnT = sb("p1_xnT", [P, R, D])
        feat = sb("p1_feat", [P, R, H * DW])
        norm = Norm(nc, ctx, "p1_norm", hold, const[:, C_POW:C_POW + 1])
        turned_ps, feat_ps, v_ps, k_ps = ([bank[2 * n], bank[2 * n + 1]] for n in range(4))

        w_in, wd, w_ready = sem("p1_w_in"), sem("p1_wd"), sem("p1_w_ready")
        x_loaded = [sem(f"p1_x_loaded{j}") for j in range(R)]
        sent_loaded = [sem(f"p1_sent_loaded{j}") for j in range(R)]
        xn_stored = [sem(f"p1_xn_stored{j}") for j in range(R)]
        xnT_stored = [sem(f"p1_xnT_stored{j}") for j in range(R)]
        feat_stored = [sem(f"p1_feat_stored{j}") for j in range(R)]
        xn_ready, turned, turned_sb, feat_done, el_sb, feat_sb, v_done, k_done, v_sb, k_sb = (sem(f"p1_{n}") for n in (
            "xn_ready", "turned", "turned_sb", "feat_done", "el_sb", "feat_sb", "v_done", "k_done", "v_sb", "k_sb"))
        block = ctx.enter_context(nc.Block())

        @block.sync
        def _(sp):
            sp.dma_start(w_feat[:, :, 0:D], A["L0_gnn_W_src"].rearrange("(k p) n -> p k n", p=P)).then_inc(w_in, 16)
            sp.dma_start(w_dst[:, :, :], A["L0_gnn_W_dst"].rearrange("(k p) n -> p k n", p=P)).then_inc(w_in, 16)
            sp.dma_start(w_k[:, :, :], A["L0_mix_W_k"].rearrange("(k p) n -> p k n", p=P)).then_inc(w_in, 16)
            sp.dma_start(w_v[:, :, 0:HD], A["L0_mix_W_v"].rearrange("(k p) n -> p k n", p=P)).then_inc(w_in, 16)
            sp.dma_start(attn[:, 0, :], A["L0_gnn_attn_l"].broadcast_to([P, D])).then_inc(w_in, 16)
            sp.dma_start(attn[:, 1, :], A["L0_gnn_attn_r"].broadcast_to([P, D])).then_inc(w_in, 16)

            def load(i, j):
                g = i * R + j
                once(sp, xn_ready, g - R + 1, hold)
                sp.dma_start(x_in[:, j, :], rows_of(A["x"], g)).then_inc(x_loaded[j], 16)
                once(sp, feat_done, g - R + 1, hold)
                sp.dma_start(sent_in[:, j, :, :], A["sentT"][:, bass.ds(g * P, P)].rearrange("(k p) n -> p k n", p=P))\
                  .then_inc(sent_loaded[j], 16)

            pipeline(sp, [(0, load)])
            for j in range(R):
                sp.wait_ge(xn_stored[j], 16 * NI)
                sp.wait_ge(xnT_stored[j], 16 * NI)
                sp.wait_ge(feat_stored[j], 16 * NI)

        @block.gpsimd
        def _(pool):
            def store_xn(i, j):
                g = i * R + j
                hold(pool, xn_ready, g + 1)
                pool.dma_start(rows_of(xn_d, g), xn[:, j, :]).then_inc(xn_stored[j], 16)

            pipeline(pool, [(2, store_xn), (0, lambda i, j: norm.root(pool, i * R + j, j))])

        @block.scalar
        def _(act):
            def copy_feat(i, j):
                g = i * R + j
                act.wait_ge(feat_done, g + 1)
                once(act, feat_stored[j], i * 16)
                act.activation(feat[:, j, :].rearrange("p (h d) -> p h d", h=H)[:, :, 0:DH],
                               feat_ps[j % 2][:, 0:D].rearrange("p (h d) -> p h d", h=H), ACT.Copy).then_inc(el_sb, 1)
                act.activation(scores[:, 0, bass.ds(g, 1), :].rearrange("p a h -> p (a h)"),
                               feat_ps[j % 2][:, D:D + H], ACT.Copy).then_inc(feat_sb, 1)

            def send_feat(i, j):
                act.wait_ge(el_sb, i * R + j + 1)
                act.dma_start(rows_of(feat_d, i * R + j), feat[:, j, :]).then_inc(feat_stored[j], 16)

            def copy_xn(i, j):
                g = i * R + j
                act.wait_ge(turned, g + 1)
                once(act, k_done, g - R + 1)
                once(act, xnT_stored[j], i * 16)
                act.activation(xnT[:, j, :], turned_ps[j % 2][:, 0:D], ACT.Copy).then_inc(turned_sb, 1)

            def send_xn(i, j):
                g = i * R + j
                act.wait_ge(turned_sb, g + 1)
                act.dma_start(xnT_d[bass.ds(g, 1), :, :].rearrange("a p n -> p (a n)"), xnT[:, j, :])\
                   .then_inc(xnT_stored[j], 16)

            def copy_k(i, j):
                g = i * R + j
                act.wait_ge(k_done, g + 1)
                act.activation(big_k[:, bass.ds(g * P, P)], k_ps[j % 2][:, 0:P], ACT.Copy).then_inc(k_sb, 1)

            pipeline(act, [(0, copy_feat), (1, copy_xn), (1, send_feat), (2, send_xn), (2, copy_k)])

        @block.vector
        def _(dve):
            link = Steps(dve, wd)
            dve.wait_ge(w_in, 96)
            for w, side in ((w_feat[:, :, 0:D], 0), (w_dst[:, :, :], 1)):
                link(dve.tensor_tensor(prod[:, :, :], w, attn[:, side:side + 1, :].broadcast_to([P, KT, D]), ALU.mult))
                to = (w_feat[:, :, D:D + H], w_v[:, :, HD:HD + H])[side]
                link(dve.tensor_reduce(to, prod[:, :, :].rearrange("p k (h d) -> p k h d", h=H), AX, ALU.add))
            link(dve.memset(feat[:, :, :], 1.0))
            dve.engine_nop().then_inc(w_ready, 1)

            def find(i, j):
                dve.wait_ge(x_loaded[j], i * 16 + 16)
                norm.find(dve, x_in[:, j, :], i * R + j, j)

            def apply(i, j):
                g = i * R + j
                once(dve, turned, g - R + 1)
                once(dve, xn_stored[j], i * 16)
                norm.apply(dve, xn[:, j, :], x_in[:, j, :], g, j).then_inc(xn_ready, 1)

            def copy_v(i, j):
                g = i * R + j
                dve.wait_ge(v_done, g + 1)
                dve.tensor_copy(tile_of(big_v, g)[:, 0:HD + H], v_ps[j % 2][:, 0:HD + H]).then_inc(v_sb, 1)

            pipeline(dve, [(1, apply), (0, find), (2, copy_v)])
            dve.wait_ge(v_sb, T)
            dve.tensor_copy(scores[:, 1, :, :], big_v[:, :, HD:HD + H]).then_inc(wd, 1)
            dve.wait_ge(wd, 6)

        @block.tensor
        def _(pe):
            pe.wait_ge(w_ready, 1)

            def project_feat(i, j):
                g = i * R + j
                pe.wait_ge(sent_loaded[j], i * 16 + 16)
                once(pe, feat_sb, g - bank_gap(j) + 1)
                for k in range(KT):
                    last = pe.matmul(feat_ps[j % 2][:, 0:D + H], sent_in[:, j, k, :], w_feat[:, k, :],
                                     start=(k == 0), stop=(k == KT - 1))
                last.then_inc(feat_done, 1)

            def turn(i, j):
                g = i * R + j
                pe.wait_ge(xn_ready, g + 1)
                once(pe, turned_sb, g - bank_gap(j) + 1)
                for k in range(KT):
                    last = pe.transpose(turned_ps[j % 2][:, k * P:(k + 1) * P], xn[:, j, k * P:(k + 1) * P], ident)
                last.then_inc(turned, 1)

            def project(i, j):
                g = i * R + j
                pe.wait_ge(turned_sb, g + 1)
                once(pe, v_sb, g - bank_gap(j) + 1)
                for k in range(KT):
                    last = pe.matmul(v_ps[j % 2][:, 0:HD + H], xnT[:, j, k * P:(k + 1) * P], w_v[:, k, :],
                                     start=(k == 0), stop=(k == KT - 1))
                last.then_inc(v_done, 1)
                once(pe, k_sb, g - bank_gap(j) + 1)
                for k in range(KT):
                    last = pe.matmul(k_ps[j % 2][:, 0:P], w_k[:, k, :], xnT[:, j, k * P:(k + 1) * P],
                                     start=(k == 0), stop=(k == KT - 1))
                last.then_inc(k_done, 1)

            pipeline(pe, [(2, project), (0, project_feat), (1, turn)])


FRONT, BACK = 2, 3
TURNS = NS // W_AGG
assert FRONT + T <= TURNS - 1 and BACK + T <= TURNS


def at(place, turn, work):
    def stage(i, s):
        if s == place and not (isinstance(i, int) and not 0 <= i - turn < T):
            work(i - turn)
    return (0, stage)


def at_end(place, work):
    def stage(i, s):
        if s == place and isinstance(i, int) and i == TURNS - 1:
            work()
    return (0, stage)


def first_mixer(nc, A, bank, const, big_k, big_v, fold):
    ident = const[:, C_ID:C_ID + P]
    zero = const[:, C_ZERO:C_ZERO + P]

    def beside(ctx):
        S = Scope(nc, ctx, "m1")
        w_qT, w_out, through = S.sb("w_qT", [P, D]), S.sb("w_out", [P, D]), S.sb("through", [P, D])
        peak, total = S.sb("peak", [P, 1]), S.sb("total", [P, 1])
        ekT, ek, ctx_sb, ctxT = (S.sb(n, [P, P]) for n in ("ekT", "ek", "ctx", "ctxT"))
        w_in, dve_step, peak_ready, exp_ready, pe_step, done = (S.sem(n) for n in (
            "w_in", "dve_step", "peak_ready", "exp_ready", "pe_step", "done"))
        cut, turned, ek_ready, summed = (S.sem(n) for n in ("cut", "turned", "ek_ready", "summed"))
        turn_ps, last_ps, sum_ps = bank[4], bank[5:7], bank[7]

        def before_sp(sp):
            sp.dma_start(w_qT[:, :], A["L0_mix_W_qT"]).then_inc(w_in, 16)
            sp.dma_start(w_out[:, :], A["L0_mix_W_out"]).then_inc(w_in, 16)

        def before_dve(dve):
            link = Steps(dve, dve_step)
            link(dve.tensor_reduce(peak[:, :], big_k[:, 0:N_NODES], AX, ALU.max))
            dve.tensor_scalar(peak[:, :], peak[:, :], -1.0, None, ALU.mult).then_inc(peak_ready, 1)

        def before_act(act):
            act.wait_ge(peak_ready, 1)
            act.activation(big_k[:, 0:N_NODES], big_k[:, 0:N_NODES], ACT.Exp, bias=peak[:, :],
                           accum_out=total[:, :]).then_inc(exp_ready, 1)

        def before_pe(pe):
            pe.matmul(sum_ps[:, 0:P], zero, ident, start=True, stop=False)

        def vector(dve):
            def scale():
                link = Steps(dve, dve_step, base=1)
                link(dve.reciprocal(total[:, :], total[:, :]))
                link(dve.tensor_scalar(total[:, :], total[:, :], 32.0 ** -0.5, None, ALU.mult))

            def cut_tile(g):
                if isinstance(g, int) and g == 0:
                    dve.wait_ge(exp_ready, 1)
                    scale()
                once(dve, turned, g)
                dve.tensor_copy(ekT[:, :], big_k[:, bass.ds(g * P, P)]).then_inc(cut, 1)

            def mask():
                dve.wait_ge(pe_step, 1)
                dve.tensor_tensor(ctx_sb[:, :], sum_ps[:, 0:P], const[:, C_BD:C_BD + P], ALU.mult).then_inc(done, 1)

            def copy():
                dve.wait_ge(pe_step, 2)
                dve.tensor_copy(ctxT[:, :], turn_ps[:, 0:P]).then_inc(done, 1)

            def divide():
                dve.wait_ge(pe_step, 3)
                dve.tensor_scalar(through[:, :], last_ps[0][:, 0:D], total[:, 0:1], None, ALU.mult).then_inc(done, 1)

            def keep():
                dve.wait_ge(pe_step, 4)
                dve.tensor_copy(fold[:, :, :].rearrange("p k n -> p (k n)"), last_ps[1][:, :]).then_inc(done, 1)
                dve.wait_ge(done, 4)

            return [at(2, FRONT, cut_tile), at_end(2, mask), at_end(5, copy), at_end(8, divide), at_end(12, keep)]

        def scalar(act):
            def copy(g):
                act.wait_ge(turned, g + 1)
                once(act, summed, g)
                act.activation(ek[:, :], turn_ps[:, 0:P], ACT.Copy).then_inc(ek_ready, 1)

            return [at(5, FRONT, copy)]

        def tensor(pe):
            def turn(g):
                pe.wait_ge(cut, g + 1)
                once(pe, ek_ready, g)
                pe.transpose(turn_ps[:, 0:P], ekT[:, :], ident).then_inc(turned, 1)

            def add(g):
                pe.wait_ge(ek_ready, g + 1)
                pe.matmul(sum_ps[:, 0:P], ek[:, :], tile_of(big_v, g)[:, 0:P], start=False, stop=False).then_inc(summed, 1)

            def finish():
                pe.matmul(sum_ps[:, 0:P], zero, ident, start=False, stop=True).then_inc(pe_step, 1)

            def turn_ctx():
                pe.wait_ge(done, 1)
                pe.transpose(turn_ps[:, 0:P], ctx_sb[:, :], ident).then_inc(pe_step, 1)

            def project():
                pe.wait_ge(w_in, 32)
                pe.wait_ge(done, 2)
                pe.matmul(last_ps[0][:, 0:D], ctxT[:, :], w_out[:, :], start=True, stop=True).then_inc(pe_step, 1)

            def unproject():
                pe.wait_ge(done, 3)
                for k in range(KT):
                    last = pe.matmul(last_ps[1][:, k * D:(k + 1) * D], w_qT[:, k * P:(k + 1) * P], through[:, :],
                                     start=True, stop=True)
                last.then_inc(pe_step, 1)

            return [at(4, FRONT, turn), at(7, FRONT, add), at_end(1, finish), at_end(4, turn_ctx), at_end(7, project),
                    at_end(11, unproject)]

        return dict(before=dict(sync=before_sp, vector=before_dve, scalar=before_act, tensor=before_pe), after={},
                    vector=vector, scalar=scalar, tensor=tensor)

    return beside


def edge_lookup(nc, A, hold, bank, const, scores, el_er, er, hi_lane, step_tile, src_lo_d, dst_lo_d):
    U = 4
    L = 4
    TURNS = NS // U // L
    EL = U * H * T
    with Stage(nc) as ctx:
        S = Scope(nc, ctx, "ew")
        part_el, part_er, rest = (S.sb("part_el", [P, 3, H, T], BF16), S.sb("part_er", [P, 3, T, H], BF16),
                                  S.sb("rest", [P, T, H]))
        src_bc, dst_bc, src_hot, dst_hot = (S.sb(n, [P, L, U * P], BF16) for n in ("src_bc", "dst_bc", "src_hot", "dst_hot"))
        hi_hot, picked = S.sb("hi_hot", [P, L, U, T]), S.sb("picked", [P, L, U, H, T])
        split, parts_ready, loaded = S.sem("split"), S.sem("parts_ready"), S.sems("loaded", L)
        hot_ready, looked_up, was_picked, el_taken, er_taken = (S.sem(n) for n in (
            "hot_ready", "looked_up", "was_picked", "el_taken", "er_taken"))
        block = S.block()

        @block.sync
        def _(sp):
            def load(i, j):
                q = i * L + j
                once(sp, hot_ready, q - L + 1, hold)
                for bc, lo in ((src_bc, src_lo_d), (dst_bc, dst_lo_d)):
                    row = lo[bass.ds(q * U, U), :].rearrange("s l -> (s l)").partition_broadcast(P)
                    sp.dma_start(bc[:, j, :], row).then_inc(loaded[j], 16)

            pipeline(sp, [(0, load)], TURNS, L)

        @block.vector
        def _(dve):
            link = Steps(dve, split)
            for side, part in ((0, part_el[:, :, :, :].rearrange("p n h t -> p n t h")), (1, part_er[:, :, :, :])):
                link(dve.tensor_copy(rest[:, :, :], scores[:, side, :, :]))
                for n in range(3):
                    link(dve.tensor_copy(part[:, n], rest[:, :, :]))
                    if n < 2:
                        link(dve.tensor_tensor(rest[:, :, :], rest[:, :, :], part[:, n], ALU.subtract))
            dve.engine_nop().then_inc(parts_ready, 1)

            def compare(i, j):
                q = i * L + j
                dve.wait_ge(loaded[j], 32 * i + 32)
                once(dve, looked_up, q - L + 1)
                once(dve, was_picked, q - L + 1)
                dve.tensor_scalar(src_hot[:, j, :], src_bc[:, j, :], const[:, C_P:C_P + 1], None, ALU.is_equal)
                dve.tensor_scalar(dst_hot[:, j, :], dst_bc[:, j, :], const[:, C_P:C_P + 1], None, ALU.is_equal)
                dve.tensor_tensor(hi_hot[:, j, :, :], const[:, C_TILE:C_TILE + T].unsqueeze(1).broadcast_to([P, U, T]),
                                  hi_lane[:, bass.ds(q * U, U)].unsqueeze(2).broadcast_to([P, U, T]),
                                  ALU.is_equal).then_inc(hot_ready, 1)

            def pick(i, j):
                q = i * L + j
                dve.wait_ge(looked_up, q + 1)
                dve.wait_ge(hot_ready, q + 1)
                once(dve, el_taken, q - L + 1)
                dve.tensor_tensor(picked[:, j, :, :, :], bank[j][:, 0:EL].rearrange("p (s h t) -> p s h t", s=U, h=H),
                                  hi_hot[:, j, :, :].unsqueeze(2).broadcast_to([P, U, H, T]), ALU.mult).then_inc(was_picked, 1)

            def add(i, j):
                q = i * L + j
                dve.wait_ge(was_picked, q + 1)
                dve.tensor_reduce(el_er[:, 0, bass.ds(q * U, U), :], picked[:, j, :, :, :], AX, ALU.add).then_inc(el_taken, 1)

            pipeline(dve, [(0, compare), (3, add), (2, pick)], TURNS, L)

        @block.scalar
        def _(act):
            def take(i, j):
                q = i * L + j
                act.wait_ge(looked_up, q + 1)
                act.wait_ge(was_picked, q + 1)
                act.activation(er[:, bass.ds(q * U, U), :], bank[j][:, EL:EL + U * H].rearrange("p (s h) -> p s h", s=U),
                               ACT.Copy).then_inc(er_taken, 1)

            pipeline(act, [(0, take)], TURNS, L)

        @block.tensor
        def _(pe):
            pe.wait_ge(parts_ready, 1)

            tiles = []

            def look_up(i, j):
                q = i * L + j
                if j == 0:
                    tiles[:] = tiles_of(nc, pe, step_tile, q * U, L * U)
                pe.wait_ge(hot_ready, q + 1)
                once(pe, er_taken, q - L + 1)
                for s in range(U):
                    for n in range(3):
                        pe.matmul(bank[j][:, s * H * T:(s + 1) * H * T], src_hot[:, j, s * P:(s + 1) * P],
                                  part_el[:, n, :, :].rearrange("p h t -> p (h t)"), start=(n == 0), stop=(n == 2))
                for s in range(U):
                    for n in range(3):
                        last = pe.matmul(bank[j][:, EL + s * H:EL + (s + 1) * H], dst_hot[:, j, s * P:(s + 1) * P],
                                         part_er[:, n, bass.ds(tiles[j * U + s], 1), :].rearrange("p a h -> p (a h)"),
                                         start=(n == 0), stop=(n == 2))
                last.then_inc(looked_up, 1)

            pipeline(pe, [(0, look_up)], TURNS, L)


def edge_exp(nc, el_er, er, weight):
    with Stage(nc) as last_ctx:
        def sem2(name):
            return last_ctx.semaphore(name)

        step, diff_ready, exp_ready = sem2("ee_step"), sem2("ee_diff_ready"), sem2("ee_exp_ready")
        leaky = last_ctx.enter_context(nc.sbuf_tensor("ee_leaky", [P, 2, NS, H], F32))
        block = last_ctx.enter_context(nc.Block())

        @block.vector
        def _(dve):
            link = Steps(dve, step)
            link(dve.tensor_tensor(el_er[:, :, :, :], el_er[:, :, :, :],
                                   er[:, :, :].unsqueeze(1).broadcast_to([P, 2, NS, H]), ALU.add))
            link(dve.scalar_tensor_tensor(out=leaky[:, :, :, :], in0=el_er[:, :, :, :], scalar=0.2,
                                          in1=el_er[:, :, :, :], op0=ALU.mult, op1=ALU.max))
            dve.tensor_tensor(weight[:, :, :], leaky[:, 0], leaky[:, 1], ALU.subtract).then_inc(diff_ready, 1)

        @block.scalar
        def _(act):
            act.wait_ge(diff_ready, 1)
            flat = weight[:, :, :].rearrange("p s h -> p (s h)")
            act.activation(flat, flat, ACT.Exp).then_inc(exp_ready, 1)
            act.wait_ge(exp_ready, 1)


def segment_maximum(nc, bank, const, dst_rows, el_er):
    with Stage(nc) as inner:
        def sb(name, shape, dt=F32):
            return inner.enter_context(nc.sbuf_tensor(name, shape, dt))

        def sem(name):
            return inner.semaphore(name)

        value = sb("sm_value", [RB, SB, H, P])
        change = sb("sm_change", [RB, SB, H, P])
        best = sb("sm_best", [RB, SB, H, P])
        ends = sb("sm_ends", [RB, 2, SB, H])
        peaks = sb("sm_peaks", [RB, 2, SB, H])
        end_row = sb("sm_end_row", [H, 2, NS])
        peak_row = sb("sm_peak_row", [H, 2, NS])
        linked = sb("sm_linked", [H, NS + 1])
        whole = sb("sm_whole", [H, NS])
        decay = sb("sm_decay", [H, NS])
        carried = sb("sm_carried", [H, 2, NS + 1])
        carry_row = sb("sm_carry_row", [H, 2, NS])
        carry = sb("sm_carry", [RB, 2, SB, H])
        same = sb("sm_same", [RB, SB, P])
        offer = sb("sm_offer", [RB, SB, H, P])
        step, pe_step, taken = sem("sm_step"), sem("sm_pe_step"), sem("sm_taken")
        block = inner.enter_context(nc.Block())
        ID = const[0:RB, C_ID:C_ID + RB]

        @block.tensor
        def _(pe):
            for b in range(SB):
                for h in range(H):
                    last = pe.transpose(bank[b][0:RB, h * P:(h + 1) * P],
                                        el_er[:, 0, b * RB:(b + 1) * RB, h], const[:, C_ID:C_ID + P])
                last.then_inc(pe_step, 1)
            pe.wait_ge(taken, 1)
            for n, src in enumerate((ends, peaks)):
                for side in range(2):
                    for b in range(SB):
                        last = pe.transpose(bank[4 + 2 * n + side][0:H, b * RB:(b + 1) * RB], src[:, side, b, :], ID)
            last.then_inc(pe_step, 1)
            pe.wait_ge(taken, 2)
            for side in range(2):
                for b in range(SB):
                    last = pe.transpose(bank[side][0:RB, b * H:(b + 1) * H],
                                        carry_row[:, side, b * RB:(b + 1) * RB], const[0:H, C_ID:C_ID + H])
            last.then_inc(pe_step, 1)
            pe.wait_ge(taken, 3)
            for h in range(H):
                for b in range(SB):
                    last = pe.transpose(bank[4 + h][:, b * RB:(b + 1) * RB], best[:, b, h, :], ID)
            last.then_inc(pe_step, 1)

        @block.vector
        def _(dve):
            link = Steps(dve, step)
            link(dve.memset(change[:, :, :, 0:1], -BIG))
            differ = dve.tensor_tensor(same[:, :, 1:P], dst_rows[:, :, 1:P], dst_rows[:, :, 0:P - 1], ALU.not_equal)
            link(differ)
            link(dve.tensor_scalar(change[:, :, :, 1:P], same[:, :, 1:P].unsqueeze(2).broadcast_to([RB, SB, H, P - 1]),
                                   -BIG, None, ALU.mult))
            for b in range(SB):
                dve.wait_ge(pe_step, b + 1)
                link(dve.tensor_copy(value[:, b, :, :].rearrange("p h l -> p (h l)"), bank[b][0:RB, :]))
            flat = "p b h l -> p (b h l)"
            n = SB * H * P
            v, c, m = (x[:, :, :, :].rearrange(flat) for x in (value, change, best))
            link(dve.tensor_tensor_scan(m, c, v, -BIG, ALU.add, ALU.max))
            link(dve.tensor_copy(v[:, n - 1:n], m[:, n - 1:n]))
            link(dve.tensor_tensor_scan(v[:, 0:n - 1][:, ::-1], c[:, 1:n][:, ::-1], m[:, 0:n - 1][:, ::-1],
                                        v[:, n - 1:n], ALU.add, ALU.max))
            for side, at in ((0, 0), (1, P - 1)):
                link(dve.tensor_copy(ends[:, side, :, :], dst_rows[:, :, at:at + 1].broadcast_to([RB, SB, H])))
                last = dve.tensor_copy(peaks[:, side, :, :], value[:, :, :, at])
                link(last) if side == 0 else last.then_inc(taken, 1)
            dve.wait_ge(pe_step, SB + 1)
            for side in range(2):
                link(dve.tensor_copy(end_row[:, side, :], bank[4 + side][0:H, 0:NS]))
                link(dve.tensor_copy(peak_row[:, side, :], bank[6 + side][0:H, 0:NS]))
            link(dve.memset(linked[:, :], -BIG))
            link(dve.tensor_tensor(linked[:, 1:NS], end_row[:, 0, 1:NS], end_row[:, 1, 0:NS - 1], ALU.not_equal))
            link(dve.tensor_scalar(linked[:, 1:NS], linked[:, 1:NS], -BIG, None, ALU.mult))
            link(dve.tensor_tensor(whole[:, :], end_row[:, 0, :], end_row[:, 1, :], ALU.not_equal))
            link(dve.tensor_scalar(whole[:, :], whole[:, :], -BIG, None, ALU.mult))
            link(dve.tensor_tensor(decay[:, :], whole[:, :], linked[:, 0:NS], ALU.min))
            link(dve.memset(carried[:, 0, 0:1], -BIG))
            link(dve.tensor_tensor_scan(carried[:, 0, 1:NS + 1], decay[:, :], peak_row[:, 1, :], -BIG,
                                        ALU.add, ALU.max))
            link(dve.tensor_tensor(carry_row[:, 0, :], carried[:, 0, 0:NS], linked[:, 0:NS], ALU.add))
            link(dve.tensor_tensor(decay[:, :], whole[:, :], linked[:, 1:NS + 1], ALU.min))
            link(dve.memset(carried[:, 1, NS:NS + 1], -BIG))
            link(dve.tensor_tensor_scan(carried[:, 1, 0:NS][:, ::-1], decay[:, ::-1], peak_row[:, 0, ::-1], -BIG,
                                        ALU.add, ALU.max))
            dve.tensor_tensor(carry_row[:, 1, :], carried[:, 1, 1:NS + 1], linked[:, 1:NS + 1], ALU.add)\
               .then_inc(taken, 1)
            dve.wait_ge(pe_step, SB + 2)
            for side in range(2):
                link(dve.tensor_copy(carry[:, side, :, :].rearrange("p b h -> p (b h)"), bank[side][0:RB, 0:SB * H]))
            for side in range(2):
                link(dve.tensor_tensor(same[:, :, :], dst_rows[:, :, :],
                                       ends[:, side, :, 0:1].broadcast_to([RB, SB, P]), ALU.not_equal))
                link(dve.tensor_scalar(offer[:, :, :, :], same[:, :, :].unsqueeze(2).broadcast_to([RB, SB, H, P]),
                                       -BIG, None, ALU.mult))
                link(dve.tensor_tensor(offer[:, :, :, :], offer[:, :, :, :],
                                       carry[:, side, :, :].unsqueeze(3).broadcast_to([RB, SB, H, P]), ALU.add))
                last = dve.tensor_tensor((value, best)[side][:, :, :, :], value[:, :, :, :], offer[:, :, :, :], ALU.max)
                link(last) if side == 0 else last.then_inc(taken, 1)
            dve.wait_ge(pe_step, SB + 3)
            for h in range(H):
                link(dve.tensor_copy(el_er[:, 1, :, h], bank[4 + h][:, 0:NS]))


def aggregate(nc, A, hold, name, bank, const, acc, step_tile, src_lane, dst_lane, table, weight, edge_weight, beside=None):
    HALF = W_AGG // 2
    HV = H - 1
    WIDTH = D + H if edge_weight is None else D
    with Stage(nc) as ctx:
        def sb(nm, shape, dt=F32):
            return ctx.enter_context(nc.sbuf_tensor(f"{name}_{nm}", shape, dt))

        def sem(nm):
            return ctx.semaphore(f"{name}_{nm}")

        index = sb("index", [P, 2, HALF], I32)
        rows = sb("rows", [P, W_AGG, WIDTH])
        hot = sb("hot", [P, W_AGG, P])
        msg = sb("msg", [P, W_AGG, WIDTH]) if edge_weight is None else rows
        zeroed, index_ready = sem("zeroed"), sem("index_ready")
        gathered = [sem(f"gathered{s}") for s in range(W_AGG)]
        ready, last_ready, summed, added = sem("ready"), sem("last_ready"), sem("summed"), sem("added")
        extra = beside(ctx) if beside else {}
        loop = dict(turns=NS // W_AGG, width=W_AGG)
        if beside:
            loop.update(first=BACK, last=FRONT + T)
        block = ctx.enter_context(nc.Block())

        def before(name, eng):
            if beside and name in extra["before"]:
                extra["before"][name](eng)

        def beside_on(name, eng):
            return extra[name](eng) if beside and name in extra else []

        @block.sync
        def _(sp):
            before("sync", sp)
            if beside_on("sync", sp):
                pipeline(sp, beside_on("sync", sp), **loop)
                extra["after"]["sync"](sp)

        @block.gpsimd
        def _(pool):
            def gather(i, s):
                half, at = divmod(s, HALF)
                if at == 0:
                    hold(pool, index_ready, 2 * i + half + 1)
                if s % 4 == 0:
                    once(pool, summed, i * W_AGG + s - W_AGG + 4, hold)
                pool.indirect_dma_start(rows[:, s, :], None, table,
                                        bass.IndirectOffsetOnAxis(ap=index[:, half, at:at + 1], axis=0))\
                    .then_inc(gathered[s], 16)

            pipeline(pool, [(0, gather)] + beside_on("gpsimd", pool), **loop)

        @block.vector
        def _(dve):
            def weigh(i, s):
                n = i * W_AGG + s
                half, at = divmod(s, HALF)
                once(dve, summed, n - W_AGG + 1)
                lane = dst_lane[:, bass.ds(n, 1)]
                if edge_weight is None:
                    dve.tensor_scalar(hot[:, s, :], const[:, C_IOTA:C_IOTA + P], lane, None, ALU.is_equal)
                    dve.wait_ge(gathered[s], i * 16 + 16)
                    w = weight[:, bass.ds(n, 1), 0:HV].rearrange("p a h -> p (a h)")
                    dve.tensor_tensor(msg[:, s, 0:HV * DW].rearrange("p (h d) -> p h d", h=HV),
                                      rows[:, s, 0:HV * DW].rearrange("p (h d) -> p h d", h=HV),
                                      w.unsqueeze(2).broadcast_to([P, HV, DW]), ALU.mult).then_inc(ready, 1)
                else:
                    dve.tensor_scalar(hot[:, s, :], const[:, C_IOTA:C_IOTA + P], lane, edge_weight[:, bass.ds(n, 1)],
                                      ALU.is_equal, ALU.mult).then_inc(ready, 1)
                    dve.wait_ge(gathered[s], i * 16 + 16)
                if at == HALF - 1:
                    dve.tensor_copy(index[:, half, :], src_lane[:, bass.ds(n + 1 + HALF, HALF)]).then_inc(index_ready, 1)

            tiles = []

            def add(i, s):
                n = i * W_AGG + s
                if s % 4 == 0:
                    tiles[:] = tiles_of(nc, dve, step_tile, n, 4)
                tile = tiles[s % 4]
                dve.wait_ge(summed, n + 1)
                once(dve, added, n)
                to = acc[:, bass.ds(tile, 1), 0:WIDTH].rearrange("p a n -> p (a n)")
                dve.tensor_tensor(to, bank[s % 4][:, 0:WIDTH], to, ALU.add).then_inc(added, 1)

            for half in range(2):
                dve.tensor_copy(index[:, half, :], src_lane[:, half * HALF:(half + 1) * HALF]).then_inc(index_ready, 1)
            dve.memset(acc[:, :, :], 0.0).then_inc(zeroed, 1)
            dve.wait_ge(zeroed, 1)
            before("vector", dve)
            pipeline(dve, [(0, weigh), (4, add)] + beside_on("vector", dve), **loop)

        @block.scalar
        def _(act):
            def weigh(i, s):
                n = i * W_AGG + s
                once(act, summed, n - W_AGG + 1)
                act.wait_ge(gathered[s], i * 16 + 16)
                act.activation(msg[:, s, HV * DW:], rows[:, s, HV * DW:], ACT.Copy,
                               scale=weight[:, bass.ds(n, 1), HV:H].rearrange("p a h -> p (a h)")).then_inc(last_ready, 1)

            before("scalar", act)
            stages = ([(0, weigh)] if edge_weight is None else []) + beside_on("scalar", act)
            pipeline(act, stages, **loop)

        @block.tensor
        def _(pe):
            def add_up(i, s):
                n = i * W_AGG + s
                if edge_weight is None:
                    pe.wait_ge(last_ready, n + 1)
                pe.wait_ge(gathered[s], i * 16 + 16)
                pe.wait_ge(ready, n + 1)
                once(pe, added, n - 3)
                pe.matmul(bank[s % 4][:, 0:WIDTH], hot[:, s, :], msg[:, s, :], start=True, stop=True)\
                  .then_inc(summed, 1)

            before("tensor", pe)
            pipeline(pe, [(0, add_up)] + beside_on("tensor", pe), **loop)


class Scope:

    def __init__(self, nc, ctx, name):
        self.nc, self.ctx, self.name = nc, ctx, name

    def sb(self, name, shape, dt=F32):
        return self.ctx.enter_context(self.nc.sbuf_tensor(f"{self.name}_{name}", shape, dt))

    def sem(self, name):
        return self.ctx.semaphore(f"{self.name}_{name}")

    def sems(self, name, n=R):
        return [self.sem(f"{name}{j}") for j in range(n)]

    def block(self):
        return self.ctx.enter_context(self.nc.Block())


def rows_of(x, g):
    return x[bass.ds(g * P, P), :]


def tile_of(x, g):
    return x[:, bass.ds(g, 1), :].rearrange("p a n -> p (a n)")


def weights(x):
    return x.rearrange("(k p) n -> p k n", p=P)


def first_graph_mlp(nc, A, hold, bank, const, acc, fold, xn1T, x_d, xn_d, xnT_d, x1_d, xn1_d):
    ident = const[:, C_ID:C_ID + P]
    FT = DF // P
    with Stage(nc) as ctx:
        S = Scope(nc, ctx, "g1")
        w1, w2, b1 = S.sb("w1", [P, KT, DF]), S.sb("w2", [P, FT, D]), S.sb("b1", [P, FT])
        bias = S.sb("bias", [P, 3, D])
        x_in, xn_in, xT_in = S.sb("x_in", [P, R, D]), S.sb("xn_in", [P, R, D]), S.sb("xT_in", [P, R, D])
        share, rst, low, high = (S.sb("share", [P, H]), S.sb("rst", [P, R, D]), S.sb("low", [P, R, D]),
                                 S.sb("high", [P, D]))
        h, hT, mid, x1, xn1 = (S.sb("h", [P, R, D]), S.sb("hT", [P, R, D]), S.sb("mid", [P, R, DF]),
                               S.sb("x1", [P, R, D]), S.sb("xn1", [P, R, D]))
        hT_ps, mid_ps, y_ps, xT_ps = ([bank[2 * n], bank[2 * n + 1]] for n in range(4))
        w_in, bias_ready = S.sem("w_in"), S.sem("bias_ready")
        loaded, x1_stored, xn1_stored = S.sems("loaded"), S.sems("x1_stored"), S.sems("xn1_stored")
        a_step, b_step, c_step = S.sem("a_step"), S.sem("b_step"), S.sem("c_step")
        low_ready, low_exp, h_ready, h_turned, hT_ready, mid_done, mid_ready, y_done, x1_ready, xn1_ready, \
            xn1_turned, xn1T_ready = (S.sem(n) for n in (
                "low_ready", "low_exp", "h_ready", "h_turned", "hT_ready", "mid_done", "mid_ready", "y_done",
                "x1_ready", "xn1_ready", "xn1_turned", "xn1T_ready"))
        norm = Norm(nc, ctx, "g1_norm", hold, const[:, C_POW:C_POW + 1])
        block = S.block()

        @block.sync
        def _(sp):
            for dst, src in ((w1, weights(A["L0_gnn_w1"])), (w2, weights(A["L0_gnn_w2"])), (b1, A["L0_gnn_b1"])):
                sp.dma_start(dst[...], src).then_inc(w_in, 16)
            for n, name in enumerate(("L0_gnn_gat_bias", "L0_gnn_b2", "L0_mix_b_out")):
                sp.dma_start(bias[:, n, :], A[name].broadcast_to([P, D])).then_inc(w_in, 16)

            def load(i, j):
                g = i * R + j
                once(sp, y_done, g - R + 1)
                once(sp, x1_ready, g - R + 1, hold)
                sp.dma_start(x_in[:, j, :], rows_of(x_d, g)).then_inc(loaded[j], 16)
                sp.dma_start(xn_in[:, j, :], rows_of(xn_d, g)).then_inc(loaded[j], 16)
                sp.dma_start(xT_in[:, j, :], xnT_d[bass.ds(g, 1), :, :].rearrange("a p n -> p (a n)"))\
                  .then_inc(loaded[j], 16)

            pipeline(sp, [(0, load)])
            for j in range(R):
                sp.wait_ge(x1_stored[j], 16 * NI)
                sp.wait_ge(xn1_stored[j], 16 * NI)

        @block.gpsimd
        def _(pool):
            def store_x(i, j):
                g = i * R + j
                norm.root(pool, g, j)
                pool.dma_start(rows_of(x1_d, g), x1[:, j, :]).then_inc(x1_stored[j], 16)

            def store_xn(i, j):
                g = i * R + j
                hold(pool, xn1_ready, g + 1)
                pool.dma_start(rows_of(xn1_d, g), xn1[:, j, :]).then_inc(xn1_stored[j], 16)

            pipeline(pool, [(4, store_xn), (3, store_x)])

        @block.vector
        def _(dve):
            dve.wait_ge(w_in, 96)
            dve.tensor_tensor(bias[:, 1, :], bias[:, 1, :], bias[:, 2, :], ALU.add).then_inc(bias_ready, 1)
            dve.wait_ge(bias_ready, 1)

            def mean(i, j):
                g = i * R + j
                link = Steps(dve, a_step, g, 4)
                sums = tile_of(acc, g).rearrange("p (h d) -> p h d", h=H)
                link(dve.tensor_scalar(share[:, :], sums[:, :, DH], 1e-30, None, ALU.max))
                link(dve.reciprocal(share[:, :], share[:, :]))
                link(dve.tensor_tensor(rst[:, j, :].rearrange("p (h d) -> p h d", h=H),
                                       sums[:, :, 0:DH],
                                       share[:, :].unsqueeze(2).broadcast_to([P, H, DH]), ALU.mult))
                link(dve.tensor_tensor(rst[:, j, :], rst[:, j, :], bias[:, 0, :], ALU.add))
                link.end()
                dve.tensor_scalar(low[:, j, :], rst[:, j, :], 0.0, None, ALU.min).then_inc(low_ready, 1)

            def elu(i, j):
                g = i * R + j
                link = Steps(dve, b_step, g, 1)
                dve.wait_ge(low_exp, g + 1)
                dve.wait_ge(loaded[j], 48 * i + 48)
                link(dve.scalar_tensor_tensor(out=high[:, :], in0=rst[:, j, :], scalar=0.0, in1=low[:, j, :],
                                              op0=ALU.max, op1=ALU.add))
                link.end()
                dve.scalar_tensor_tensor(out=h[:, j, :], in0=high[:, :], scalar=-1.0, in1=xn_in[:, j, :],
                                         op0=ALU.add, op1=ALU.add).then_inc(h_ready, 1)

            def residual(i, j):
                g = i * R + j
                link = Steps(dve, c_step, g, 1)
                once(dve, x1_stored[j], i * 16)
                link(dve.tensor_tensor(x1[:, j, :], x_in[:, j, :], bias[:, 1, :], ALU.add))
                link.end()
                dve.wait_ge(y_done, g + 1)
                dve.tensor_tensor(x1[:, j, :], y_ps[j % 2][:, 0:D], x1[:, j, :], ALU.add).then_inc(x1_ready, 1)
                dve.wait_ge(x1_ready, g + 1)
                norm.find(dve, x1[:, j, :], g, j)

            def norm_x(i, j):
                g = i * R + j
                once(dve, xn1_stored[j], i * 16)
                once(dve, xn1_turned, g - R + 1)
                norm.apply(dve, xn1[:, j, :], x1[:, j, :], g, j).then_inc(xn1_ready, 1)

            pipeline(dve, [(1, elu), (4, norm_x), (3, residual), (0, mean)])

        @block.scalar
        def _(act):
            act.wait_ge(w_in, 96)

            def exp_low(i, j):
                g = i * R + j
                act.wait_ge(low_ready, g + 1)
                act.activation(low[:, j, :], low[:, j, :], ACT.Exp).then_inc(low_exp, 1)

            def copy_h(i, j):
                g = i * R + j
                act.wait_ge(h_turned, g + 1)
                act.activation(hT[:, j, :], hT_ps[j % 2][:, 0:D], ACT.Copy).then_inc(hT_ready, 1)

            def relu(i, j):
                g = i * R + j
                act.wait_ge(mid_done, g + 1)
                for f in range(FT):
                    last = act.activation(mid[:, j, f * P:(f + 1) * P], mid_ps[j % 2][:, f * P:(f + 1) * P], ACT.Relu,
                                          bias=b1[:, f:f + 1])
                last.then_inc(mid_ready, 1)

            def copy_x(i, j):
                g = i * R + j
                act.wait_ge(xn1_turned, g + 1)
                act.activation(xn1T[:, :, bass.ds(g * P, P)], xT_ps[j % 2][:, 0:D].rearrange("p (k n) -> p k n", k=KT),
                               ACT.Copy).then_inc(xn1T_ready, 1)

            pipeline(act, [(1, copy_h), (2, relu), (4, copy_x), (0, exp_low)])

        @block.tensor
        def _(pe):
            pe.wait_ge(w_in, 96)

            def turn_h(i, j):
                g = i * R + j
                pe.wait_ge(h_ready, g + 1)
                once(pe, hT_ready, g - bank_gap(j) + 1)
                for k in range(KT):
                    last = pe.transpose(hT_ps[j % 2][:, k * P:(k + 1) * P], h[:, j, k * P:(k + 1) * P], ident)
                last.then_inc(h_turned, 1)

            def mlp_in(i, j):
                g = i * R + j
                pe.wait_ge(hT_ready, g + 1)
                once(pe, mid_ready, g - bank_gap(j) + 1)
                for f in range(FT):
                    for k in range(KT):
                        last = pe.matmul(mid_ps[j % 2][:, f * P:(f + 1) * P], w1[:, k, f * P:(f + 1) * P],
                                         hT[:, j, k * P:(k + 1) * P], start=(k == 0), stop=(k == KT - 1))
                last.then_inc(mid_done, 1)

            def mlp_out(i, j):
                g = i * R + j
                pe.wait_ge(mid_ready, g + 1)
                once(pe, x1_ready, g - bank_gap(j) + 1)
                pe.wait_ge(loaded[j], 48 * i + 48)
                for f in range(FT):
                    pe.matmul(y_ps[j % 2][:, 0:D], mid[:, j, f * P:(f + 1) * P], w2[:, f, :], start=(f == 0), stop=False)
                for k in range(KT):
                    last = pe.matmul(y_ps[j % 2][:, 0:D], xT_in[:, j, k * P:(k + 1) * P], fold[:, k, :],
                                     start=False, stop=(k == KT - 1))
                last.then_inc(y_done, 1)

            def turn_x(i, j):
                g = i * R + j
                pe.wait_ge(xn1_ready, g + 1)
                once(pe, xn1T_ready, g - bank_gap(j) + 1)
                for k in range(KT):
                    last = pe.transpose(xT_ps[j % 2][:, k * P:(k + 1) * P], xn1[:, j, k * P:(k + 1) * P], ident)
                last.then_inc(xn1_turned, 1)

            pipeline(pe, [(3, mlp_out), (1, turn_h), (2, mlp_in), (4, turn_x)])


def first_router(nc, A, hold, bank, const, xn1T, w1, w2, b1, bias):
    capacity = float(-(-N_NODES * 5 // (4 * E)))
    with Stage(nc) as ctx:
        S = Scope(nc, ctx, "r1")
        mean, w_r, line, small = S.sb("mean", [P, KT]), S.sb("w_r", [P, KT, E]), S.sb("line", [1, 6, E]), S.sb("small", [1, 4])
        top, index, pair = S.sb("top", [1, E]), S.sb("index", [1, E], U32), S.sb("pair", [1, 2])
        share, b2 = S.sb("share", [P, 2]), S.sb("b2", [P, 2, D])
        w_in, step, mean_ready, logits, peak, exp_done, picked, spread, experts_in, shared = (S.sem(n) for n in (
            "w_in", "step", "mean_ready", "logits", "peak", "exp_done", "picked", "spread", "experts_in", "shared"))
        block = S.block()
        x, e, rw, load, cut, br = (line[:, n, :] for n in range(6))

        @block.sync
        def _(sp):
            sp.dma_start(w_r[:, :, :], weights(A["L0_ffn_Wr"])).then_inc(w_in, 16)
            sp.dma_start(br, A["L0_ffn_br"]).then_inc(w_in, 16)
            sp.wait_ge(picked, 1)
            for n in range(2):
                at = sp.value_load(index[0:1, n:n + 1], min_val=0, max_val=E - 1)
                sp.dma_start(w1[:, n, :, :], A["L0_ffn_W1"][bass.ds(at, 1), :, :]
                             .rearrange("a (k p) n -> p (a k) n", p=P)).then_inc(experts_in, 16)
                sp.dma_start(w2[:, n, :, :], A["L0_ffn_W2"][bass.ds(at, 1), :, :]
                             .rearrange("a (k p) n -> p (a k) n", p=P)).then_inc(experts_in, 16)
                sp.dma_start(b1[:, n, :], A["L0_ffn_b1"][bass.ds(at, 1), :, :].rearrange("a p f -> p (a f)"))\
                  .then_inc(experts_in, 16)
                sp.dma_start(b2[:, n, :], A["L0_ffn_b2"][bass.ds(at, 1), :].broadcast_to([P, D])).then_inc(experts_in, 16)

        @block.tensor
        def _(pe):
            pe.wait_ge(w_in, 32)
            pe.wait_ge(mean_ready, 1)
            for k in range(KT):
                last = pe.matmul(bank[0][0:1, 0:E], mean[:, k:k + 1], w_r[:, k, :], start=(k == 0), stop=(k == KT - 1))
            last.then_inc(logits, 1)
            pe.wait_ge(shared, 1)
            pe.matmul(bank[1][:, 0:2], const[0:1, C_ONE:C_ONE + P], pair[:, :], start=True, stop=True).then_inc(spread, 1)

        @block.scalar
        def _(act):
            for n, dst in enumerate((e, e, pair[:, :])):
                act.wait_ge(peak, n + 1)
                src = dst if n == 2 else x
                act.activation(dst, src, ACT.Exp).then_inc(exp_done, 1)

        @block.vector
        def _(dve):
            link = Steps(dve, step)

            def softmax(src, dst, at, n, tmp):
                link(dve.tensor_reduce(small[:, at:at + 1], src, AX, ALU.max))
                dve.tensor_scalar(tmp, src, small[:, at:at + 1], None, ALU.subtract).then_inc(peak, 1)
                dve.wait_ge(exp_done, n + 1)
                out = pair[:, :] if n == 2 else e
                link(dve.tensor_reduce(small[:, at:at + 1], out, AX, ALU.add))
                link(dve.reciprocal(small[:, at:at + 1], small[:, at:at + 1]))
                return dve.tensor_scalar(dst, out, small[:, at:at + 1], None, ALU.mult)

            link(dve.tensor_reduce(mean[:, :], xn1T[:, :, 0:N_NODES], AX, ALU.add))
            dve.tensor_scalar(mean[:, :], mean[:, :], 1.0 / N_NODES, None, ALU.mult).then_inc(mean_ready, 1)
            dve.wait_ge(logits, 1)
            link(dve.tensor_tensor(cut, bank[0][0:1, 0:E], br, ALU.add))
            link(softmax(cut, rw, 0, 0, x))
            link(dve.tensor_scalar(load, rw, float(N_NODES), None, ALU.mult))
            link(dve.reciprocal(cut, load))
            link(dve.tensor_scalar(cut, cut, capacity, None, ALU.mult))
            link(dve.tensor_scalar(load, load, capacity, None, ALU.is_gt))
            link(dve.tensor_tensor(cut, cut, load, ALU.mult))
            link(dve.tensor_scalar(load, load, -1.0, 1.0, ALU.mult, ALU.add))
            link(dve.tensor_tensor(cut, cut, load, ALU.add))
            link(dve.tensor_tensor(rw, rw, cut, ALU.mult))
            link(softmax(rw, cut, 1, 1, x))
            link(dve.max(top[:, :], cut))
            dve.max_index(index[:, :], top[:, :], cut).then_inc(picked, 1)
            link(softmax(top[:, 0:2], pair[:, :], 2, 2, pair[:, :]))
            dve.engine_nop().then_inc(shared, 1)
            dve.wait_ge(spread, 1)
            link(dve.tensor_copy(share[:, :], bank[1][:, 0:2]))
            dve.wait_ge(experts_in, 16 * 8)
            for n in range(2):
                link(dve.tensor_scalar(w2[:, n, :, :], w2[:, n, :, :], share[:, n:n + 1], None, ALU.mult))
            link(dve.tensor_scalar(bias[:, :], b2[:, 0, :], share[:, 0:1], None, ALU.mult))
            link(dve.scalar_tensor_tensor(out=bias[:, :], in0=b2[:, 1, :], scalar=share[:, 1:2], in1=bias[:, :],
                                          op0=ALU.mult, op1=ALU.add))


def first_experts(nc, A, hold, bank, const, xn1T, w1, w2, b1, bias, big_k, big_v, x1_d, xn1_d, x2_d, xn2_d, qT_d):
    ident = const[:, C_ID:C_ID + P]
    FT = 2 * DF // P
    HM, SM = 8, 32
    with Stage(nc) as ctx:
        S = Scope(nc, ctx, "e1")
        vec = S.sb("vec", [P, 2, D])
        col = S.sb("col", [P, 3, KT])
        w_x, w_q, w_k, w_v = S.sb("w_x", [P, KT, D]), S.sb("w_q", [P, P]), S.sb("w_k", [P, P]), S.sb("w_v", [P, P])
        x1_in, xn1_in = S.sb("x1_in", [P, R, D]), S.sb("xn1_in", [P, R, D])
        mid = S.sb("mid", [P, R, FT * P])
        y, out0 = S.sb("y", [P, D]), S.sb("out0", [P, D])
        x2, xn2, ln = S.sb("x2", [P, R, D]), S.sb("xn2", [P, R, D]), S.sb("ln", [P, R, D])
        lnT, xm = S.sb("lnT", [P, D]), S.sb("xm", [P, D])
        q, most, total, qT = S.sb("q", [P, R, D]), S.sb("most", [P, HM]), S.sb("total", [P, HM]), S.sb("qT", [P, R, D])
        w_in = S.sem("w_in")
        loaded, x2_stored, xn2_stored, qT_stored = (S.sems(n) for n in ("loaded", "x2_stored", "xn2_stored", "qT_stored"))
        a_step, b_step, c_step, d_step = (S.sem(n) for n in ("a_step", "b_step", "c_step", "d_step"))
        mid_done0, mid_done1, mid_ready0, mid_ready1, y_done, y_ready, x2_ready, xn2_ready, ln_ready, ln_turned, lnT_ready, \
            xm_done, xm_ready, qv_done, k_done, k_ready, q_cut, v_ready, q_exp, q_ready, q_turned, qT_ready = (
                S.sem(n) for n in ("mid_done0", "mid_done1", "mid_ready0", "mid_ready1", "y_done", "y_ready",
                                   "x2_ready", "xn2_ready", "ln_ready", "ln_turned", "lnT_ready", "xm_done", "xm_ready",
                                   "qv_done", "k_done", "k_ready", "q_cut", "v_ready", "q_exp", "q_ready", "q_turned",
                                   "qT_ready"))
        norms = [Norm(nc, ctx, f"e1_norm{n}", hold, const[:, C_POW:C_POW + 1]) for n in range(3)]
        mid_ps, y_ps, ln_ps, xm_ps, qv_ps, k_ps, q_ps = [bank[0], bank[1]], *bank[2:8]
        mid_done, mid_ready = [mid_done0, mid_done1], [mid_ready0, mid_ready1]
        block = S.block()

        @block.sync
        def _(sp):
            for n, name in enumerate(("L0_ffn_gamma", "L0_ffn_beta")):
                sp.dma_start(vec[:, n, :], A[name].broadcast_to([P, D])).then_inc(w_in, 16)
            for n, name in enumerate(("L1_mix_ln1_w", "L1_mix_ln1_b", "L1_mix_bx")):
                sp.dma_start(col[:, n, :], A[name]).then_inc(w_in, 16)
            sp.dma_start(w_x[:, :, :], weights(A["L1_mix_WxT"])).then_inc(w_in, 16)
            for w, name in ((w_q, "L1_mix_WqT4"), (w_k, "L1_mix_WkT4"), (w_v, "L1_mix_WvT4")):
                sp.dma_start(w[:, :], A[name]).then_inc(w_in, 16)

            def load(i, j):
                g = i * R + j
                once(sp, x2_ready, g - R + 1, hold)
                sp.dma_start(x1_in[:, j, :], rows_of(x1_d, g)).then_inc(loaded[j], 16)
                sp.dma_start(xn1_in[:, j, :], rows_of(xn1_d, g)).then_inc(loaded[j], 16)

            pipeline(sp, [(0, load)])
            for j in range(R):
                for s in (x2_stored, xn2_stored, qT_stored):
                    sp.wait_ge(s[j], 16 * NI)

        @block.gpsimd
        def _(pool):
            def root_y(i, j):
                norms[0].root(pool, i * R + j, j)

            def store_x(i, j):
                g = i * R + j
                norms[1].root(pool, g, j)
                pool.dma_start(rows_of(x2_d, g), x2[:, j, :]).then_inc(x2_stored[j], 16)

            def store_xn(i, j):
                g = i * R + j
                norms[2].root(pool, g, j)
                pool.dma_start(rows_of(xn2_d, g), xn2[:, j, :]).then_inc(xn2_stored[j], 16)

            pipeline(pool, [(3, store_xn), (2, store_x), (1, root_y)])

        @block.vector
        def _(dve):
            dve.wait_ge(w_in, 16 * 9)

            def add_y(i, j):
                g = i * R + j
                dve.wait_ge(loaded[j], 32 * i + 32)
                link = Steps(dve, c_step, g, 1)
                link(dve.tensor_tensor(y[:, :], xn1_in[:, j, :], bias[:, :], ALU.add))
                link.end()
                dve.wait_ge(y_done, g + 1)
                dve.tensor_tensor(y[:, :], y_ps[:, 0:D], y[:, :], ALU.add).then_inc(y_ready, 1)
                dve.wait_ge(y_ready, g + 1)
                norms[0].find(dve, y[:, :], g, j)

            def residual(i, j):
                g = i * R + j
                link = Steps(dve, d_step, g, 3)
                link(norms[0].apply(dve, out0[:, :], y[:, :], g, j))
                link(dve.tensor_tensor(out0[:, :], out0[:, :], vec[:, 0, :], ALU.mult))
                link(dve.tensor_tensor(out0[:, :], out0[:, :], vec[:, 1, :], ALU.add))
                link.end()
                once(dve, x2_stored[j], 16 * i)
                dve.tensor_tensor(x2[:, j, :], out0[:, :], x1_in[:, j, :], ALU.add).then_inc(x2_ready, 1)
                dve.wait_ge(x2_ready, g + 1)
                norms[1].find(dve, x2[:, j, :], g, j)

            def norm_x(i, j):
                g = i * R + j
                once(dve, xn2_stored[j], 16 * i)
                norms[1].apply(dve, xn2[:, j, :], x2[:, j, :], g, j).then_inc(xn2_ready, 1)
                dve.wait_ge(xn2_ready, g + 1)
                norms[2].find(dve, xn2[:, j, :], g, j)

            def norm_again(i, j):
                g = i * R + j
                once(dve, ln_turned, g - R + 1)
                norms[2].apply(dve, ln[:, j, :], xn2[:, j, :], g, j).then_inc(ln_ready, 1)

            def cut(i, j):
                g = i * R + j
                dve.wait_ge(qv_done, g + 1)
                link = Steps(dve, a_step, g, 1)
                q_in = qv_ps[:, 0:D].rearrange("p (h s) -> p h s", h=HM)
                link(dve.tensor_reduce(most[:, :], q_in, AX, ALU.max))
                link.end()
                once(dve, q_turned, g - R + 1)
                dve.tensor_tensor(q[:, j, :].rearrange("p (h s) -> p h s", h=HM), q_in,
                                  most[:, :].unsqueeze(2).broadcast_to([P, HM, SM]), ALU.subtract).then_inc(q_cut, 1)
                dve.tensor_copy(tile_of(big_v, g), qv_ps[:, D:2 * D]).then_inc(v_ready, 1)

            def divide(i, j):
                g = i * R + j
                dve.wait_ge(q_exp, g + 1)
                link = Steps(dve, b_step, g, 2)
                view = q[:, j, :].rearrange("p (h s) -> p h s", h=HM)
                link(dve.tensor_reduce(total[:, :], view, AX, ALU.add))
                link(dve.reciprocal(total[:, :], total[:, :]))
                link.end()
                dve.tensor_tensor(view, view, total[:, :].unsqueeze(2).broadcast_to([P, HM, SM]), ALU.mult)\
                   .then_inc(q_ready, 1)

            pipeline(dve, [(4, norm_again), (5, divide), (3, norm_x), (2, residual), (4, cut), (1, add_y)])

        @block.scalar
        def _(act):
            act.wait_ge(w_in, 16 * 9)

            def copy_ln(i, j):
                g = i * R + j
                act.wait_ge(ln_turned, g + 1)
                once(act, xm_done, g)
                for k in range(KT):
                    last = act.activation(lnT[:, k * P:(k + 1) * P], ln_ps[:, k * P:(k + 1) * P], ACT.Identity,
                                          bias=col[:, 1, k:k + 1], scale=col[:, 0, k:k + 1])
                last.then_inc(lnT_ready, 1)

            def copy_q(i, j):
                g = i * R + j
                act.wait_ge(q_turned, g + 1)
                once(act, qT_stored[j], 16 * i)
                act.activation(qT[:, j, :], q_ps[:, 0:D], ACT.Copy).then_inc(qT_ready, 1)
                act.wait_ge(qT_ready, g + 1)
                act.dma_start(qT_d[bass.ds(g, 1), :, :].rearrange("a p n -> p (a n)"), qT[:, j, :])\
                   .then_inc(qT_stored[j], 16)

            def gelu(half):
                def stage(i, j):
                    g = i * R + j
                    once(act, y_done, g - R + 1)
                    act.wait_ge(mid_done[half], g + 1)
                    for f in range(4):
                        n = half * 4 + f
                        last = act.activation(mid[:, j, n * P:(n + 1) * P], mid_ps[half][:, f * P:(f + 1) * P],
                                              ACT.Gelu, bias=b1[:, half, f:f + 1])
                    last.then_inc(mid_ready[half], 1)
                return stage

            def add_bx(i, j):
                g = i * R + j
                act.wait_ge(xm_done, g + 1)
                once(act, k_done, g)
                for k in range(KT):
                    last = act.activation(xm[:, k * P:(k + 1) * P], xm_ps[:, k * P:(k + 1) * P], ACT.Identity,
                                          bias=col[:, 2, k:k + 1])
                last.then_inc(xm_ready, 1)

            def copy_k(i, j):
                g = i * R + j
                act.wait_ge(k_done, g + 1)
                act.activation(big_k[:, :].rearrange("p (k n) -> p k n", k=KT)[:, :, bass.ds(g * P, P)],
                               k_ps[:, 0:D].rearrange("p (k n) -> p k n", k=KT), ACT.Copy).then_inc(k_ready, 1)
                act.wait_ge(q_cut, g + 1)
                act.activation(q[:, j, :], q[:, j, :], ACT.Exp).then_inc(q_exp, 1)

            pipeline(act, [(0, gelu(0)), (4, copy_ln), (0, gelu(1)), (4, add_bx), (4, copy_k), (5, copy_q)])

        @block.tensor
        def _(pe):
            pe.wait_ge(w_in, 16 * 9)

            def turn_ln(i, j):
                g = i * R + j
                pe.wait_ge(ln_ready, g + 1)
                once(pe, lnT_ready, g)
                for k in range(KT):
                    last = pe.transpose(ln_ps[:, k * P:(k + 1) * P], ln[:, j, k * P:(k + 1) * P], ident)
                last.then_inc(ln_turned, 1)

            def turn_q(i, j):
                g = i * R + j
                pe.wait_ge(q_ready, g + 1)
                once(pe, qT_ready, g)
                for k in range(KT):
                    last = pe.transpose(q_ps[:, k * P:(k + 1) * P], q[:, j, k * P:(k + 1) * P], ident)
                last.then_inc(q_turned, 1)

            def expert_in(half):
                def stage(i, j):
                    g = i * R + j
                    once(pe, mid_ready[half], g)
                    for f in range(4):
                        for k in range(KT):
                            last = pe.matmul(mid_ps[half][:, f * P:(f + 1) * P], w1[:, half, k, f * P:(f + 1) * P],
                                             xn1T[:, k, bass.ds(g * P, P)], start=(k == 0), stop=(k == KT - 1))
                    last.then_inc(mid_done[half], 1)
                return stage

            def expert_out(half):
                def stage(i, j):
                    g = i * R + j
                    once(pe, y_ready, g)
                    pe.wait_ge(mid_ready[half], g + 1)
                    for f in range(4):
                        n = half * 4 + f
                        last = pe.matmul(y_ps[:, 0:D], mid[:, j, n * P:(n + 1) * P], w2[:, half, f, :],
                                         start=(n == 0), stop=(n == FT - 1))
                    if half == 1:
                        last.then_inc(y_done, 1)
                return stage

            def project_x(i, j):
                g = i * R + j
                pe.wait_ge(lnT_ready, g + 1)
                once(pe, xm_ready, g)
                for m in range(KT):
                    for k in range(KT):
                        last = pe.matmul(xm_ps[:, m * P:(m + 1) * P], w_x[:, k, m * P:(m + 1) * P],
                                         lnT[:, k * P:(k + 1) * P], start=(k == 0), stop=(k == KT - 1))
                last.then_inc(xm_done, 1)

            def project_qkv(i, j):
                g = i * R + j
                pe.wait_ge(xm_ready, g + 1)
                once(pe, v_ready, g)
                for n, w in enumerate((w_q, w_v)):
                    for m in range(KT):
                        last = pe.matmul(qv_ps[:, n * D + m * P:n * D + (m + 1) * P], xm[:, m * P:(m + 1) * P], w[:, :],
                                         start=True, stop=True)
                last.then_inc(qv_done, 1)
                once(pe, k_ready, g)
                for m in range(KT):
                    last = pe.matmul(k_ps[:, m * P:(m + 1) * P], w_k[:, :], xm[:, m * P:(m + 1) * P],
                                     start=True, stop=True)
                last.then_inc(k_done, 1)

            pipeline(pe, [(0, expert_in(0)), (4, turn_ln), (0, expert_in(1)), (4, project_x), (1, expert_out(0)),
                          (4, project_qkv), (1, expert_out(1)), (5, turn_q)])


def second_mixer(nc, A, hold, bank, const, big_k, big_v, folded):
    ident = const[:, C_ID:C_ID + P]
    zero = const[:, C_ZERO:C_ZERO + P]
    with Stage(nc) as ctx:
        S = Scope(nc, ctx, "m2")
        w_o, peak, total = S.sb("w_o", [P, KT, D]), S.sb("peak", [P, KT]), S.sb("total", [P, KT])
        ekT, ek = S.sb("ekT", [P, R, D]), S.sb("ek", [P, R, D])
        kv, kvT = S.sb("kv", [P, KT, P]), S.sb("kvT", [P, KT, P])
        w_in, step, peak_ready, exp_ready, cut, turned, ek_ready, summed, pe_step, done = (S.sem(n) for n in (
            "w_in", "step", "peak_ready", "exp_ready", "cut", "turned", "ek_ready", "summed", "pe_step", "done"))
        block = S.block()
        k_view = big_k[:, :].rearrange("p (k n) -> p k n", k=KT)

        @block.sync
        def _(sp):
            sp.dma_start(w_o[:, :, :], weights(A["L1_mix_WoT"])).then_inc(w_in, 16)

        @block.vector
        def _(dve):
            link = Steps(dve, step)
            link(dve.memset(k_view[:, :, N_NODES:NP], 0.0))
            link(dve.tensor_reduce(peak[:, :], k_view[:, :, 0:N_NODES], AX, ALU.max))
            dve.tensor_scalar(peak[:, :], peak[:, :], -1.0, None, ALU.mult).then_inc(peak_ready, 1)
            dve.wait_ge(exp_ready, KT)
            link(dve.reciprocal(total[:, :], total[:, :]))

            def cut_tile(i, j):
                g = i * R + j
                once(dve, turned, g - R + 1)
                dve.tensor_copy(ekT[:, j, :].rearrange("p (k n) -> p k n", k=KT), k_view[:, :, bass.ds(g * P, P)])\
                   .then_inc(cut, 1)

            pipeline(dve, [(0, cut_tile)])
            dve.wait_ge(pe_step, 1)
            for m in range(KT):
                last = dve.tensor_tensor(kv[:, m, :], bank[4 + m][:, 0:P], const[:, C_BD:C_BD + P], ALU.mult)
            last.then_inc(done, 1)
            dve.wait_ge(pe_step, 2)
            dve.tensor_copy(kvT[:, :, :].rearrange("p k n -> p (k n)"), bank[2][:, 0:D]).then_inc(done, 1)
            dve.wait_ge(pe_step, 3)
            for m in range(KT):
                last = dve.tensor_scalar(folded[:, m, :], bank[3][:, m * D:(m + 1) * D], total[:, m:m + 1], None, ALU.mult)
            last.then_inc(done, 1)
            dve.wait_ge(done, 3)

        @block.scalar
        def _(act):
            act.wait_ge(peak_ready, 1)
            for k in range(KT):
                act.activation(k_view[:, k, 0:N_NODES], k_view[:, k, 0:N_NODES], ACT.Exp, bias=peak[:, k:k + 1],
                               accum_out=total[:, k:k + 1]).then_inc(exp_ready, 1)

            def copy_ek(i, j):
                g = i * R + j
                act.wait_ge(turned, g + 1)
                once(act, summed, g - R + 1)
                act.activation(ek[:, j, :], bank[j % 2][:, 0:D], ACT.Copy).then_inc(ek_ready, 1)

            pipeline(act, [(0, copy_ek)])

        @block.tensor
        def _(pe):
            pe.wait_ge(w_in, 16)
            for m in range(KT):
                pe.matmul(bank[4 + m][:, 0:P], zero, ident, start=True, stop=False)

            def turn(i, j):
                g = i * R + j
                pe.wait_ge(cut, g + 1)
                once(pe, ek_ready, g - bank_gap(j) + 1)
                for k in range(KT):
                    last = pe.transpose(bank[j % 2][:, k * P:(k + 1) * P], ekT[:, j, k * P:(k + 1) * P], ident)
                last.then_inc(turned, 1)

            def add(i, j):
                g = i * R + j
                pe.wait_ge(ek_ready, g + 1)
                for m in range(KT):
                    last = pe.matmul(bank[4 + m][:, 0:P], ek[:, j, m * P:(m + 1) * P],
                                     tile_of(big_v, g)[:, m * P:(m + 1) * P], start=False, stop=False)
                last.then_inc(summed, 1)

            pipeline(pe, [(0, turn), (1, add)])
            for m in range(KT):
                last = pe.matmul(bank[4 + m][:, 0:P], zero, ident, start=False, stop=True)
            last.then_inc(pe_step, 1)
            pe.wait_ge(done, 1)
            for m in range(KT):
                last = pe.transpose(bank[2][:, m * P:(m + 1) * P], kv[:, m, :], ident)
            last.then_inc(pe_step, 1)
            pe.wait_ge(done, 2)
            for m in range(KT):
                last = pe.matmul(bank[3][:, m * D:(m + 1) * D], kvT[:, m, :], w_o[:, m, :], start=True, stop=True)
            last.then_inc(pe_step, 1)


def mixer_mlp(nc, A, hold, bank, const, folded, x2_d, xn2_d, qT_d, mixed_d):
    ident = const[:, C_ID:C_ID + P]
    ones = const[0:1, C_ONE:C_ONE + P]
    FT = HID // P

    def beside(ctx):
        S = Scope(nc, ctx, "x2")
        w1, w2, b1 = S.sb("w1", [P, KT, HID]), S.sb("w2", [P, FT, D]), S.sb("b1", [P, FT])
        vec, col = S.sb("vec", [1, 2, D]), S.sb("col", [P, 2, KT])
        x_in, xn_in, qT_in, h, xh, ln, lnT, mixed = (S.sb(n, [P, D]) for n in (
            "x_in", "xn_in", "qT_in", "h", "xh", "ln", "lnT", "mixed"))
        mid = S.sb("mid", [P, FT * P])
        w_in, loaded, stored = (S.sem(n) for n in ("w_in", "loaded", "stored"))
        h_done, h_ready, xh_ready, ln_ready, ln_turned, lnT_ready, y_done, mixed_ready, mid_done0, mid_done1, \
            mid_ready0, mid_ready1 = (S.sem(n) for n in (
                "h_done", "h_ready", "xh_ready", "ln_ready", "ln_turned", "lnT_ready", "y_done", "mixed_ready",
                "mid_done0", "mid_done1", "mid_ready0", "mid_ready1"))
        mid_done, mid_ready = [mid_done0, mid_done1], [mid_ready0, mid_ready1]
        norm = Norm(nc, ctx, "x2_norm", hold, const[:, C_POW:C_POW + 1])
        mid_ps, h_ps, ln_ps, y_ps = bank[4:6], bank[6][:, 0:D], bank[6][:, D:2 * D], bank[7]

        def before(sp):
            for dst, src in ((w1, weights(A["L1_mix_W1T"])), (w2, weights(A["L1_mix_W2T"])), (b1, A["L1_mix_b1"])):
                sp.dma_start(dst[...], src).then_inc(w_in, 16)
            for n, name in enumerate(("L1_mix_bo", "L1_mix_b2")):
                sp.dma_start(vec[:, n, :], A[name]).then_inc(w_in, 16)
            for n, name in enumerate(("L1_mix_ln2_w", "L1_mix_ln2_b")):
                sp.dma_start(col[:, n, :], A[name]).then_inc(w_in, 16)

        def weights_in(eng, g):
            if isinstance(g, int) and g == 0:
                eng.wait_ge(w_in, 16 * 7)

        def load(sp):
            def work(g):
                once(sp, xh_ready, g, hold)
                sp.dma_start(x_in[:, :], rows_of(x2_d, g)).then_inc(loaded, 16)
                sp.dma_start(xn_in[:, :], rows_of(xn2_d, g)).then_inc(loaded, 16)
                sp.dma_start(qT_in[:, :], qT_d[bass.ds(g, 1), :, :].rearrange("a p n -> p (a n)")).then_inc(loaded, 16)
            return work

        def store(sp):
            def work(g):
                hold(sp, mixed_ready, g + 1)
                sp.dma_start(rows_of(mixed_d, g), mixed[:, :]).then_inc(stored, 16)
            return work

        def after(sp):
            sp.wait_ge(stored, 16 * T)

        def attend_dve(dve):
            def work(g):
                dve.wait_ge(loaded, 48 * g + 48)
                dve.wait_ge(h_done, g + 1)
                dve.tensor_tensor(h[:, :], h_ps, xn_in[:, :], ALU.add).then_inc(h_ready, 1)
                dve.wait_ge(h_ready, g + 1)
                norm.find(dve, h[:, :], g)
            return work

        def normalise(dve):
            def work(g):
                norm.apply(dve, ln[:, :], h[:, :], g).then_inc(ln_ready, 1)
            return work

        def residual(dve):
            def work(g):
                once(dve, stored, 16 * g)
                dve.wait_ge(y_done, g + 1)
                dve.tensor_tensor(mixed[:, :], y_ps[:, 0:D], xh[:, :], ALU.add).then_inc(mixed_ready, 1)
            return work

        def keep(dve):
            def work(g):
                once(dve, mixed_ready, g)
                dve.tensor_tensor(xh[:, :], x_in[:, :], h[:, :], ALU.add).then_inc(xh_ready, 1)
                dve.wait_ge(xh_ready, g + 1)
            return work

        def copy_ln(act):
            def work(g):
                weights_in(act, g)
                act.wait_ge(ln_turned, g + 1)
                for k in range(KT):
                    last = act.activation(lnT[:, k * P:(k + 1) * P], ln_ps[:, k * P:(k + 1) * P], ACT.Identity,
                                          bias=col[:, 1, k:k + 1], scale=col[:, 0, k:k + 1])
                last.then_inc(lnT_ready, 1)
            return work

        def gelu(act, half):
            def work(g):
                once(act, y_done, g)
                act.wait_ge(mid_done[half], g + 1)
                for f in range(4):
                    n = half * 4 + f
                    last = act.activation(mid[:, n * P:(n + 1) * P], mid_ps[half][:, f * P:(f + 1) * P],
                                          ACT.Gelu, bias=b1[:, n:n + 1])
                last.then_inc(mid_ready[half], 1)
            return work

        def attend_pe(pe):
            def work(g):
                weights_in(pe, g)
                pe.wait_ge(loaded, 48 * g + 48)
                once(pe, lnT_ready, g)
                pe.matmul(h_ps, ones, vec[:, 0, :], start=True, stop=False)
                for k in range(KT):
                    last = pe.matmul(h_ps, qT_in[:, k * P:(k + 1) * P], folded[:, k, :],
                                     start=False, stop=(k == KT - 1))
                last.then_inc(h_done, 1)
            return work

        def turn(pe):
            def work(g):
                pe.wait_ge(ln_ready, g + 1)
                for k in range(KT):
                    last = pe.transpose(ln_ps[:, k * P:(k + 1) * P], ln[:, k * P:(k + 1) * P], ident)
                last.then_inc(ln_turned, 1)
            return work

        def mlp_in(pe, half):
            def work(g):
                pe.wait_ge(lnT_ready, g + 1)
                once(pe, mid_ready[half], g)
                for f in range(4):
                    n = half * 4 + f
                    for k in range(KT):
                        last = pe.matmul(mid_ps[half][:, f * P:(f + 1) * P], w1[:, k, n * P:(n + 1) * P],
                                         lnT[:, k * P:(k + 1) * P], start=(k == 0), stop=(k == KT - 1))
                last.then_inc(mid_done[half], 1)
            return work

        def mlp_out(pe, half):
            def work(g):
                once(pe, mixed_ready, g)
                if half == 0:
                    pe.matmul(y_ps[:, 0:D], ones, vec[:, 1, :], start=True, stop=False)
                pe.wait_ge(mid_ready[half], g + 1)
                for f in range(4):
                    n = half * 4 + f
                    last = pe.matmul(y_ps[:, 0:D], mid[:, n * P:(n + 1) * P], w2[:, n, :],
                                     start=False, stop=(n == FT - 1))
                if half == 1:
                    last.then_inc(y_done, 1)
            return work

        return dict(
            before=dict(sync=before), after=dict(sync=after),
            sync=lambda sp: [at(0, FRONT, load(sp)), at(1, BACK, store(sp))],
            gpsimd=lambda pool: [at(2, BACK, lambda g: norm.root(pool, g))],
            vector=lambda dve: [at(1, BACK, normalise(dve)), at(10, FRONT, attend_dve(dve)),
                                at(15, BACK, residual(dve)), at(15, FRONT, keep(dve))],
            scalar=lambda act: [at(2, BACK, copy_ln(act)), at(4, BACK, gelu(act, 0)), at(6, BACK, gelu(act, 1))],
            tensor=lambda pe: [at(1, BACK, turn(pe)), at(3, BACK, mlp_in(pe, 0)), at(5, BACK, mlp_in(pe, 1)),
                               at(8, FRONT, attend_pe(pe)), at(9, BACK, mlp_out(pe, 0)), at(11, BACK, mlp_out(pe, 1))])

    return beside


def second_graph(nc, A, hold, bank, const, acc, xn3T, combine, mixed_d, big_k, big_v):
    ident = const[:, C_ID:C_ID + P]
    with Stage(nc) as ctx:
        S = Scope(nc, ctx, "g2")
        w, w_r = S.sb("w", [P, KT, D]), S.sb("w_r", [P, KT, E])
        mixed, sums, sumsT, x3, xn3, nT = (S.sb(n, [P, R, D]) for n in ("mixed", "sums", "sumsT", "x3", "xn3", "nT"))
        pr, pick, rank = S.sb("pr", [P, T, E]), S.sb("pick", [P, 2, T, E]), S.sb("rank", [P, T, E])
        most = S.sb("most", [P, 3, T])
        w_in, ew_in, loaded = S.sem("w_in"), S.sem("ew_in"), S.sems("loaded")
        r_step, c_step, shifted, pr_exp = S.sem("r_step"), S.sem("c_step"), S.sem("shifted"), S.sem("pr_exp")
        sums_ready, sums_turned, sumsT_ready, g_done, x3_ready, xn3_ready, xn3_turned, nT_ready, xn3T_ready, logits, \
            pr_ready = (S.sem(n) for n in (
                "sums_ready", "sums_turned", "sumsT_ready", "g_done", "x3_ready", "xn3_ready", "xn3_turned", "nT_ready",
                "xn3T_ready", "logits", "pr_ready"))
        norm = Norm(nc, ctx, "g2_norm", hold, const[:, C_POW:C_POW + 1])
        block = S.block()
        s_ps, g_ps, n_ps, l_ps = bank[0:2], bank[2:4], bank[4:6], bank[6:8]

        @block.sync
        def _(sp):
            sp.dma_start(w[:, :, :], weights(A["L1_gnn_weight"])).then_inc(w_in, 16)
            sp.dma_start(w_r[:, :, :], weights(A["L1_ffn_router_wT"])).then_inc(w_in, 16)

            def load(i, j):
                g = i * R + j
                once(sp, x3_ready, g - R + 1, hold)
                sp.dma_start(mixed[:, j, :], rows_of(mixed_d, g)).then_inc(loaded[j], 16)

            pipeline(sp, [(0, load)])
            ew1, ew2 = expert_weights(big_k, big_v)
            for e in range(E):
                sp.dma_start(ew1[:, e, :, :], weights(A["L1_ffn_w1"][e, :, :])).then_inc(ew_in, 16)
                sp.dma_start(ew2[:, e, :, :], weights(A["L1_ffn_w2"][e, :, :])).then_inc(ew_in, 16)
            sp.wait_ge(ew_in, 32 * E)

        @block.gpsimd
        def _(pool):
            pipeline(pool, [(0, lambda i, j: norm.root(pool, i * R + j, j))])

        @block.vector
        def _(dve):
            order = const[:, C_ORDER:C_ORDER + E].unsqueeze(1).broadcast_to([P, T, E])

            def cut(i, j):
                g = i * R + j
                once(dve, sums_turned, g - R + 1)
                dve.tensor_copy(sums[:, j, :], tile_of(acc, g)[:, 0:D]).then_inc(sums_ready, 1)

            def residual(i, j):
                g = i * R + j
                dve.wait_ge(loaded[j], 16 * i + 16)
                dve.wait_ge(g_done, g + 1)
                dve.scalar_tensor_tensor(out=x3[:, j, :], in0=g_ps[j % 2][:, 0:D], scalar=0.0, in1=mixed[:, j, :],
                                         op0=ALU.max, op1=ALU.add).then_inc(x3_ready, 1)
                dve.wait_ge(x3_ready, g + 1)
                norm.find(dve, x3[:, j, :], g, j)

            def norm_x(i, j):
                g = i * R + j
                once(dve, xn3_turned, g - R + 1)
                norm.apply(dve, xn3[:, j, :], x3[:, j, :], g, j).then_inc(xn3_ready, 1)
                dve.wait_ge(xn3_ready, g + 1)
                dve.tensor_tensor(tile_of(acc, g)[:, 0:D], x3[:, j, :], xn3[:, j, :], ALU.add).then_inc(c_step, 1)

            pipeline(dve, [(3, norm_x), (0, cut), (1, residual)])

            link = Steps(dve, r_step)

            def wide(x):
                return x.unsqueeze(2).broadcast_to([P, T, E])

            dve.wait_ge(pr_ready, T)
            link(dve.tensor_reduce(most[:, 0, :], pr[:, :, :], AX, ALU.max))
            dve.tensor_tensor(pr[:, :, :], pr[:, :, :], wide(most[:, 0, :]), ALU.subtract).then_inc(shifted, 1)
            dve.wait_ge(pr_exp, 1)
            dve.wait_ge(shifted, 1)
            link(dve.tensor_reduce(most[:, 0, :], pr[:, :, :], AX, ALU.add))
            link(dve.reciprocal(most[:, 0, :], most[:, 0, :]))
            link(dve.tensor_tensor(pr[:, :, :], pr[:, :, :], wide(most[:, 0, :]), ALU.mult))
            for n in range(2):
                link(dve.tensor_reduce(most[:, n, :], pr[:, :, :], AX, ALU.max))
                link(dve.tensor_tensor(pick[:, n], pr[:, :, :], wide(most[:, n, :]), ALU.is_equal))
                link(dve.tensor_tensor(rank[:, :, :], pick[:, n], order, ALU.mult))
                link(dve.tensor_reduce(most[:, 2, :], rank[:, :, :], AX, ALU.max))
                link(dve.tensor_tensor(pick[:, n], rank[:, :, :], wide(most[:, 2, :]), ALU.is_equal))
                if n == 0:
                    link(dve.scalar_tensor_tensor(out=pr[:, :, :], in0=pick[:, 0], scalar=-4.0, in1=pr[:, :, :],
                                                  op0=ALU.mult, op1=ALU.add))
            link(dve.tensor_tensor(most[:, 2, :], most[:, 0, :], most[:, 1, :], ALU.add))
            link(dve.tensor_scalar(most[:, 2, :], most[:, 2, :], 1e-12, None, ALU.max))
            link(dve.reciprocal(most[:, 2, :], most[:, 2, :]))
            for n in range(2):
                link(dve.tensor_tensor(most[:, n, :], most[:, n, :], most[:, 2, :], ALU.mult))
                link(dve.tensor_tensor(pick[:, n], pick[:, n], wide(most[:, n, :]), ALU.mult))
            link(dve.tensor_tensor(combine[:, :, :], pick[:, 0], pick[:, 1], ALU.add))

        @block.scalar
        def _(act):
            def copy_sums(i, j):
                g = i * R + j
                act.wait_ge(sums_turned, g + 1)
                once(act, g_done, g - R + 1)
                act.activation(sumsT[:, j, :], s_ps[j % 2][:, 0:D], ACT.Copy).then_inc(sumsT_ready, 1)

            def copy_n(i, j):
                g = i * R + j
                act.wait_ge(xn3_turned, g + 1)
                once(act, logits, g - R + 1)
                act.activation(nT[:, j, :], n_ps[j % 2][:, 0:D], ACT.Copy).then_inc(nT_ready, 1)
                act.activation(xn3T[:, :, bass.ds(g * P, P)], n_ps[j % 2][:, 0:D].rearrange("p (k n) -> p k n", k=KT),
                               ACT.Copy).then_inc(xn3T_ready, 1)

            def copy_logits(i, j):
                g = i * R + j
                act.wait_ge(logits, g + 1)
                act.activation(tile_of(pr, g), l_ps[j % 2][:, 0:E], ACT.Copy).then_inc(pr_ready, 1)

            pipeline(act, [(0, copy_sums), (3, copy_n), (4, copy_logits)])
            act.wait_ge(shifted, 1)
            act.activation(pr[:, :, :], pr[:, :, :], ACT.Exp).then_inc(pr_exp, 1)

        @block.tensor
        def _(pe):
            pe.wait_ge(w_in, 32)

            def turn_sums(i, j):
                g = i * R + j
                pe.wait_ge(sums_ready, g + 1)
                once(pe, sumsT_ready, g - bank_gap(j) + 1)
                for k in range(KT):
                    last = pe.transpose(s_ps[j % 2][:, k * P:(k + 1) * P], sums[:, j, k * P:(k + 1) * P], ident)
                last.then_inc(sums_turned, 1)

            def project(i, j):
                g = i * R + j
                pe.wait_ge(sumsT_ready, g + 1)
                once(pe, x3_ready, g - bank_gap(j) + 1)
                for k in range(KT):
                    last = pe.matmul(g_ps[j % 2][:, 0:D], sumsT[:, j, k * P:(k + 1) * P], w[:, k, :],
                                     start=(k == 0), stop=(k == KT - 1))
                last.then_inc(g_done, 1)

            def turn_n(i, j):
                g = i * R + j
                pe.wait_ge(xn3_ready, g + 1)
                once(pe, xn3T_ready, g - bank_gap(j) + 1)
                for k in range(KT):
                    last = pe.transpose(n_ps[j % 2][:, k * P:(k + 1) * P], xn3[:, j, k * P:(k + 1) * P], ident)
                last.then_inc(xn3_turned, 1)

            def score(i, j):
                g = i * R + j
                pe.wait_ge(nT_ready, g + 1)
                once(pe, pr_ready, g - bank_gap(j) + 1)
                for k in range(KT):
                    last = pe.matmul(l_ps[j % 2][:, 0:E], nT[:, j, k * P:(k + 1) * P], w_r[:, k, :],
                                     start=(k == 0), stop=(k == KT - 1))
                last.then_inc(logits, 1)

            pipeline(pe, [(3, turn_n), (0, turn_sums), (1, project), (4, score)])


def expert_weights(big_k, big_v):
    return (big_k[:, 0:E * KT * D].rearrange("p (e k n) -> p e k n", e=E, k=KT),
            big_v[:, :, :].rearrange("p t n -> p (t n)")[:, 0:E * KT * D].rearrange("p (e k n) -> p e k n", e=E, k=KT))


def second_experts(nc, A, hold, bank, const, acc, xn3T, combine, big_k, big_v, out):
    FT = D // P
    with Stage(nc) as ctx:
        S = Scope(nc, ctx, "e2")
        w1, w2 = expert_weights(big_k, big_v)
        b1 = S.sb("b1", [P, E, FT])
        b2, combT = S.sb("b2", [E, D]), S.sb("combT", [E, NP])
        mid = S.sb("mid", [P, E, D])
        w_in = S.sem("w_in")
        stored = S.sem("stored")
        mid_done, mid_ready, y_done, added, comb_turned, combT_ready, b2_done, b2_added = (S.sem(n) for n in (
            "mid_done", "mid_ready", "y_done", "added", "comb_turned", "combT_ready", "b2_done", "b2_added"))
        block = S.block()

        @block.sync
        def _(sp):
            sp.dma_start(b1[:, :, :], A["L1_ffn_b1"]).then_inc(w_in, 16)
            sp.dma_start(b2[:, :], A["L1_ffn_b2"]).then_inc(w_in, 16)
            with sp.Fori(0, T) as g:
                hold(sp, added, (g + 1) * E)
                sp.dma_start(rows_of(out, g), tile_of(acc, g)[:, 0:D]).then_inc(stored, 16)
            sp.wait_ge(stored, 16 * T)

        @block.tensor
        def _(pe):
            for t in range(T):
                last = pe.transpose(bank[t // 4][0:E, t % 4 * P:(t % 4 + 1) * P], combine[:, t, :], const[:, C_ID:C_ID + P])
            last.then_inc(comb_turned, 1)
            pe.wait_ge(w_in, 32)
            pe.wait_ge(combT_ready, 1)
            for n in range(-(-T // 2)):
                once(pe, b2_added, n - 1)
                for t in range(2 * n, min(2 * n + 2, T)):
                    last = pe.matmul(bank[n % 2][:, (t - 2 * n) * D:(t - 2 * n + 1) * D], combT[:, t * P:(t + 1) * P], b2[:, :],
                                     start=True, stop=True)
                last.then_inc(b2_done, 1)
            pe.wait_ge(b2_added, -(-T // 2))

            def expert_in(g, e):
                n = g * E + e
                once(pe, mid_ready, n - 1)
                for f in range(FT):
                    for k in range(KT):
                        last = pe.matmul(bank[e % 2][:, f * P:(f + 1) * P], w1[:, e, k, f * P:(f + 1) * P],
                                         xn3T[:, k, bass.ds(g * P, P)], start=(k == 0), stop=(k == KT - 1))
                last.then_inc(mid_done, 1)

            def expert_out(g, e):
                n = g * E + e
                pe.wait_ge(mid_ready, n + 1)
                once(pe, added, n - 1)
                for f in range(FT):
                    last = pe.matmul(bank[2 + e % 2][:, 0:D], mid[:, e, f * P:(f + 1) * P], w2[:, e, f, :],
                                     start=(f == 0), stop=(f == FT - 1))
                last.then_inc(y_done, 1)

            pipeline(pe, [(0, expert_in), (1, expert_out)], T, E)

        @block.scalar
        def _(act):
            act.wait_ge(w_in, 32)
            act.wait_ge(comb_turned, 1)
            for b in range(-(-T // 4)):
                width = min(4 * P, (T - 4 * b) * P)
                last = act.activation(combT[:, 4 * b * P:4 * b * P + width], bank[b][0:E, 0:width], ACT.Copy)
            last.then_inc(combT_ready, 1)

            def gelu(g, e):
                n = g * E + e
                act.wait_ge(mid_done, n + 1)
                once(act, y_done, n - E + 1)
                for f in range(FT):
                    last = act.activation(mid[:, e, f * P:(f + 1) * P], bank[e % 2][:, f * P:(f + 1) * P], ACT.Gelu,
                                          bias=b1[:, e, f:f + 1])
                last.then_inc(mid_ready, 1)

            pipeline(act, [(0, gelu)], T, E)

        @block.vector
        def _(dve):
            for n in range(-(-T // 2)):
                to = acc[:, 2 * n:min(2 * n + 2, T), 0:D]
                dve.wait_ge(b2_done, n + 1)
                dve.tensor_tensor(to, bank[n % 2][:, 0:to.shape[1] * D].rearrange("p (t n) -> p t n", n=D), to, ALU.add)\
                   .then_inc(b2_added, 1)
            dve.wait_ge(b2_added, -(-T // 2))

            def add(g, e):
                n = g * E + e
                dve.wait_ge(y_done, n + 1)
                once(dve, added, n)
                to = tile_of(acc, g)[:, 0:D]
                dve.scalar_tensor_tensor(out=to, in0=bank[2 + e % 2][:, 0:D], scalar=tile_of(combine, g)[:, e:e + 1],
                                         in1=to, op0=ALU.mult, op1=ALU.add).then_inc(added, 1)

            pipeline(dve, [(0, add)], T, E)


def laid_out(inputs):

    a = {k: np.asarray(v) for k, v in inputs.items()}

    def rows(x):
        y = np.zeros((NP, x.shape[1]), x.dtype)
        y[:N_NODES] = x[:N_NODES]
        return y

    def edges(x, fill):
        y = np.full((NC * P,), fill, x.dtype)
        y[:N_EDGES] = x
        return y.reshape(NC, P)

    def column(x):
        return np.ascontiguousarray(x.reshape(-1, P).T)

    def four(w):
        y = np.zeros((P, P), w.dtype)
        for n in range(4):
            y[32 * n:32 * n + 32, 32 * n:32 * n + 32] = w
        return y

    const = np.zeros((P, C_N), np.float32)
    const[:, C_ID:C_ID + P] = np.eye(P)
    const[:, C_BD:C_BD + P] = np.kron(np.eye(4), np.ones((32, 32)))
    const[:, C_IOTA:C_IOTA + P] = np.arange(P)
    const[:, C_P] = np.arange(P)
    const[:, C_STEP:C_STEP + SB] = np.arange(P)[:, None] + RB * np.arange(SB)
    const[:, C_TILE:C_TILE + T] = np.arange(T)
    const[:, C_CHUNK:C_CHUNK + NC] = np.arange(NC)
    const[:, C_ONE:C_ONE + P] = 1
    const[:, C_POW] = -0.5
    const[:, C_ORDER:C_ORDER + E] = E - np.arange(E)
    return {
        "const": const,
        "x": rows(a["x"]),
        "sentT": np.ascontiguousarray(rows(a["L0_gnn_sent_repr"]).T),
        "L0_gnn_W_src": a["L0_gnn_W_src"], "L0_gnn_W_dst": a["L0_gnn_W_dst"],
        "L0_gnn_attn_l": a["L0_gnn_attn_l"].reshape(1, D), "L0_gnn_attn_r": a["L0_gnn_attn_r"].reshape(1, D),
        "L0_mix_W_qT": np.ascontiguousarray(a["L0_mix_W_qkv"][:, 0:128].T),
        "L0_mix_W_k": np.ascontiguousarray(a["L0_mix_W_qkv"][:, 128:256]),
        "L0_mix_W_v": np.ascontiguousarray(a["L0_mix_W_qkv"][:, 256:384]),
        "L0_mix_W_out": a["L0_mix_W_out"],
        "L0_gnn_w1": a["L0_gnn_w1"], "L0_gnn_w2": a["L0_gnn_w2"], "L0_gnn_b1": column(a["L0_gnn_b1"]),
        "L0_ffn_Wr": a["L0_ffn_Wr"], "L0_ffn_W1": a["L0_ffn_W1"], "L0_ffn_W2": a["L0_ffn_W2"],
        "L0_ffn_b1": np.ascontiguousarray(a["L0_ffn_b1"].reshape(E, -1, P).transpose(0, 2, 1)),
        "L0_ffn_b2": a["L0_ffn_b2"],
        **{k: a[k].reshape(1, -1) for k in ("L0_gnn_gat_bias", "L0_gnn_b2", "L0_mix_b_out", "L0_ffn_br",
                                            "L0_ffn_gamma", "L0_ffn_beta", "L1_mix_bo", "L1_mix_b2")},
        **{k: column(a[k]) for k in ("L1_mix_ln1_w", "L1_mix_ln1_b", "L1_mix_bx", "L1_mix_b1", "L1_mix_ln2_w",
                                     "L1_mix_ln2_b")},
        **{k + "T": np.ascontiguousarray(a[k].T) for k in ("L1_mix_Wx", "L1_mix_Wo", "L1_mix_W1", "L1_mix_W2",
                                                           "L1_ffn_router_w")},
        **{k + "T4": four(a[k].T) for k in ("L1_mix_Wq", "L1_mix_Wk", "L1_mix_Wv")},
        "L1_gnn_weight": a["L1_gnn_weight"], "L1_ffn_w1": a["L1_ffn_w1"], "L1_ffn_w2": a["L1_ffn_w2"],
        "L1_ffn_b1": np.ascontiguousarray(a["L1_ffn_b1"].reshape(E, -1, P).transpose(2, 0, 1)),
        "L1_ffn_b2": a["L1_ffn_b2"],
        "src": edges(a["src"], 0),
        "dst": edges(a["dst"], PAD_DST),
        "dst_first": np.ascontiguousarray(edges(a["dst"], PAD_DST)[:, 0].reshape(1, NC)),
        "ew": edges(a["edge_weight"], 0),
    }


def kernel(**inputs):
    import concourse.bacc as bacc
    from concourse.bass_utils import run_bass_kernel_spmd

    arrays = laid_out(inputs)
    nc = bacc.Bacc("TRN2", target_bir_lowering=False, num_devices=1)
    A = {k: nc.dram_tensor(f"in_{k}", v.shape, mybir.dt.from_np(v.dtype), kind="ExternalInput").ap()
         for k, v in arrays.items()}
    out = nc.dram_tensor("out", [NP, D], F32, kind="ExternalOutput").ap()
    program(nc, A, out)
    r = run_bass_kernel_spmd(nc, [{f"in_{k}": v for k, v in arrays.items()}], core_ids=[0])
    return r.results[0]["out"][:N_NODES]
```
